# Optimizing a Trainium2 kernel written in Bass

```python
import numpy as np
import jax
import jax.numpy as jnp

def _softmax(x, axis=-1):
    return jax.nn.softmax(x, axis=axis)

def _gelu(x):
    return jax.nn.gelu(x, approximate=True)

def _silu(x):
    return jax.nn.silu(x)

def _sigmoid(x):
    return jax.nn.sigmoid(x)

def _layernorm(x, axis=-1, eps=1e-05):
    m = jnp.mean(x, axis=axis, keepdims=True)
    v = jnp.var(x, axis=axis, keepdims=True)
    return (x - m) / jnp.sqrt(v + eps)

def _scatter_add(tgt, idx, src, axis=0):
    return tgt.at[idx].add(src)

def _segment_sum(src, seg, n):
    return jax.ops.segment_sum(src, seg, n)
kernel_name = 'mk_prb_d1_jaxref_r8_eb7d6d'

def setup_inputs(seed: int=0):
    np.random.seed(seed)
    _w = jnp.asarray

    def _L0_attn_setup():
        import jax, jax.numpy as jnp
        import numpy as np
        import math
        D_MODEL = 128
        N_HEADS = 16
        EPS_GN = 1e-05

        def channel_group_norm(x, gamma, beta, num_groups, eps=EPS_GN):
            B, T, D = x.shape
            g = num_groups
            xt = x.transpose(0, 2, 1).reshape(B, g, D // g, T)
            mu = xt.mean(axis=(2, 3), keepdims=True)
            var = xt.var(axis=(2, 3), keepdims=True)
            xn = ((xt - mu) / jnp.sqrt(var + eps)).reshape(B, D, T)
            xn = xn * gamma[None, :, None] + beta[None, :, None]
            return xn.transpose(0, 2, 1)

        def l2_normalize(x, eps=1e-12):
            n = jnp.linalg.norm(x, axis=-1, keepdims=True)
            return x / jnp.maximum(n, eps)

        def decay_gammas(num_heads, dtype=jnp.float32):
            return 1.0 - jnp.exp(jnp.linspace(math.log(1.0 / 32.0), math.log(1.0 / 512.0), num_heads)).astype(dtype)
        key = jax.random.key(seed)
        ks = jax.random.split(key, 16)
        B, T, D = (4, 128, D_MODEL)
        s = 1.0 / math.sqrt(D)
        inp = {'x': jax.random.normal(ks[0], (B, T, D), jnp.float32), 'norm_g': jnp.ones((D,), jnp.float32), 'norm_b': jnp.zeros((D,), jnp.float32), 'qw': jax.random.normal(ks[1], (D, D), jnp.float32) * s, 'kw': jax.random.normal(ks[2], (D, D), jnp.float32) * s, 'vw': jax.random.normal(ks[3], (D, D), jnp.float32) * s, 'ow': jax.random.normal(ks[4], (D, D), jnp.float32) * s, 'ob': jnp.zeros((D,), jnp.float32), 'ffn_norm_g': jnp.ones((D,), jnp.float32), 'ffn_norm_b': jnp.zeros((D,), jnp.float32), 'w1': jax.random.normal(ks[5], (2 * D, D), jnp.float32) * s, 'b1': jnp.zeros((2 * D,), jnp.float32), 'w2': jax.random.normal(ks[6], (D, 2 * D), jnp.float32) * (1.0 / math.sqrt(2 * D)), 'b2': jnp.zeros((D,), jnp.float32)}
        return inp
    _L0_attn_in = _L0_attn_setup()

    def _L0_ffn_setup():
        import jax, jax.numpy as jnp
        import numpy as np
        DIM = 128
        DEPTH = 2
        HEADS = 8
        DIM_HEAD = 64
        WINDOW = 64
        INNER = HEADS * DIM_HEAD
        HID = int(DIM * 4 * 2 / 3)
        B, N = (2, 1024)
        QK_SCALE = 8.0

        def shift_token(t):
            t1, t2 = jnp.split(t, 2, axis=-1)
            t2 = jnp.pad(t2, ((0, 0), (1, 0), (0, 0)))[:, :-1]
            return jnp.concatenate([t1, t2], axis=-1)

        def l2norm(t):
            return t / jnp.clip(jnp.linalg.norm(t, axis=-1, keepdims=True), 1e-12)

        def rotate_half(x):
            x1, x2 = jnp.split(x, 2, axis=-1)
            return jnp.concatenate([-x2, x1], axis=-1)

        def rotary_xpos(q, k):
            n = q.shape[-2]
            half_idx = jnp.arange(0, DIM_HEAD, 2, dtype=jnp.float32)
            inv_freq = 1.0 / 10000.0 ** (half_idx / DIM_HEAD)
            t = jnp.arange(n, dtype=jnp.float32)
            freqs = t[:, None] * inv_freq[None, :]
            freqs = jnp.concatenate([freqs, freqs], axis=-1)
            base = (half_idx + 0.4 * DIM_HEAD) / (1.4 * DIM_HEAD)
            power = (t - n // 2) / float(WINDOW // 2)
            scale = base[None, :] ** power[:, None]
            scale = jnp.concatenate([scale, scale], axis=-1)
            cos, sin = (jnp.cos(freqs), jnp.sin(freqs))
            q = q * cos * scale + rotate_half(q) * sin * scale
            k = k * cos / scale + rotate_half(k) * sin / scale
            return (q, k)

        def local_attention(q, k, v):
            b, h, n, d = q.shape
            w = n // WINDOW
            bq = q.reshape(b, h, w, WINDOW, d) * QK_SCALE
            bk = k.reshape(b, h, w, WINDOW, d)
            bv = v.reshape(b, h, w, WINDOW, d)

            def look_around(t):
                p = jnp.pad(t, ((0, 0), (0, 0), (1, 0), (0, 0), (0, 0)))
                return jnp.concatenate([p[:, :, :w], p[:, :, 1:]], axis=3)
            bk, bv = (look_around(bk), look_around(bv))
            bt = jnp.arange(n).reshape(w, WINDOW)
            btp = jnp.pad(bt, ((1, 0), (0, 0)), constant_values=-1)
            btk = jnp.concatenate([btp[:w], btp[1:]], axis=1)
            sim = jnp.einsum('bhwid,bhwjd->bhwij', bq, bk)
            i = bt[:, :, None]
            j = btk[:, None, :]
            mask = (i < j) | (i > j + WINDOW) | (j == -1)
            sim = jnp.where(mask, -jnp.finfo(sim.dtype).max, sim)
            attn = jax.nn.softmax(sim, axis=-1)
            out = jnp.einsum('bhwij,bhwjd->bhwid', attn, bv)
            return out.reshape(b, h, n, d)

        def _layer(x, wqkv, qs, ksc, wo, lg, lb, w1, b1, w2, b2):
            b, n, _ = x.shape
            h = shift_token(x)
            qkv = h @ wqkv
            q, k, v = jnp.split(qkv, 3, axis=-1)
            to_heads = lambda t: t.reshape(b, n, HEADS, DIM_HEAD).transpose(0, 2, 1, 3)
            q, k, v = (to_heads(q), to_heads(k), to_heads(v))
            q = l2norm(q) * qs
            k = l2norm(k) * ksc
            q, k = rotary_xpos(q, k)
            o = local_attention(q, k, v)
            o = o.transpose(0, 2, 1, 3).reshape(b, n, INNER)
            x = x + o @ wo
            h = shift_token(x)
            mu = h.mean(-1, keepdims=True)
            var = h.var(-1, keepdims=True)
            h = (h - mu) / jnp.sqrt(var + 1e-05) * lg + lb
            h = h @ w1 + b1
            a, g = jnp.split(h, 2, axis=-1)
            h = a * jax.nn.gelu(g, approximate=False)
            x = x + h @ w2 + b2
            return x
        key = jax.random.key(seed)
        ks = jax.random.split(key, 6)
        return {'x': jax.random.normal(ks[0], (B, N, DIM), jnp.float32), 'wqkv': jax.random.normal(ks[1], (DEPTH, DIM, 3 * INNER), jnp.float32) * 0.02, 'q_scale': jnp.ones((DEPTH, DIM_HEAD), jnp.float32), 'k_scale': jnp.ones((DEPTH, DIM_HEAD), jnp.float32), 'wo': jax.random.normal(ks[2], (DEPTH, INNER, DIM), jnp.float32) * 0.02, 'ln_g': jnp.ones((DEPTH, DIM), jnp.float32), 'ln_b': jnp.zeros((DEPTH, DIM), jnp.float32), 'w1': jax.random.normal(ks[3], (DEPTH, DIM, 2 * HID), jnp.float32) * 0.02, 'b1': jnp.zeros((DEPTH, 2 * HID), jnp.float32), 'w2': jax.random.normal(ks[4], (DEPTH, HID, DIM), jnp.float32) * 0.02, 'b2': jnp.zeros((DEPTH, DIM), jnp.float32)}
    _L0_ffn_in = _L0_ffn_setup()
    _d = {'L0_attn_x': _L0_attn_in['x'], 'L0_attn_norm_g': _L0_attn_in['norm_g'], 'L0_attn_norm_b': _L0_attn_in['norm_b'], 'L0_attn_qw': _L0_attn_in['qw'], 'L0_attn_kw': _L0_attn_in['kw'], 'L0_attn_vw': _L0_attn_in['vw'], 'L0_attn_ow': _L0_attn_in['ow'], 'L0_attn_ob': _L0_attn_in['ob'], 'L0_attn_ffn_norm_g': _L0_attn_in['ffn_norm_g'], 'L0_attn_ffn_norm_b': _L0_attn_in['ffn_norm_b'], 'L0_attn_w1': _L0_attn_in['w1'], 'L0_attn_b1': _L0_attn_in['b1'], 'L0_attn_w2': _L0_attn_in['w2'], 'L0_attn_b2': _L0_attn_in['b2'], 'L0_ffn_wqkv': _L0_ffn_in['wqkv'], 'L0_ffn_q_scale': _L0_ffn_in['q_scale'], 'L0_ffn_k_scale': _L0_ffn_in['k_scale'], 'L0_ffn_wo': _L0_ffn_in['wo'], 'L0_ffn_ln_g': _L0_ffn_in['ln_g'], 'L0_ffn_ln_b': _L0_ffn_in['ln_b'], 'L0_ffn_w1': _L0_ffn_in['w1'], 'L0_ffn_b1': _L0_ffn_in['b1'], 'L0_ffn_w2': _L0_ffn_in['w2'], 'L0_ffn_b2': _L0_ffn_in['b2']}
    _x0 = _d['L0_attn_x']
    _d['L0_attn_x'] = jax.random.normal(jax.random.fold_in(jax.random.key(seed), 1), (4, 1024, 128), dtype=_x0.dtype)
    del _x0
    return _d

def reference(L0_attn_x, L0_attn_norm_g, L0_attn_norm_b, L0_attn_qw, L0_attn_kw, L0_attn_vw, L0_attn_ow, L0_attn_ob, L0_attn_ffn_norm_g, L0_attn_ffn_norm_b, L0_attn_w1, L0_attn_b1, L0_attn_w2, L0_attn_b2, L0_ffn_wqkv, L0_ffn_q_scale, L0_ffn_k_scale, L0_ffn_wo, L0_ffn_ln_g, L0_ffn_ln_b, L0_ffn_w1, L0_ffn_b1, L0_ffn_w2, L0_ffn_b2):

    def _L0_attn_ref(x, norm_g, norm_b, qw, kw, vw, ow, ob, ffn_norm_g, ffn_norm_b, w1, b1, w2, b2):
        import jax, jax.numpy as jnp
        import numpy as np
        import math
        D_MODEL = 128
        N_HEADS = 16
        EPS_GN = 1e-05

        def channel_group_norm(x, gamma, beta, num_groups, eps=EPS_GN):
            B, T, D = x.shape
            g = num_groups
            xt = x.transpose(0, 2, 1).reshape(B, g, D // g, T)
            mu = xt.mean(axis=(2, 3), keepdims=True)
            var = xt.var(axis=(2, 3), keepdims=True)
            xn = ((xt - mu) / jnp.sqrt(var + eps)).reshape(B, D, T)
            xn = xn * gamma[None, :, None] + beta[None, :, None]
            return xn.transpose(0, 2, 1)

        def l2_normalize(x, eps=1e-12):
            n = jnp.linalg.norm(x, axis=-1, keepdims=True)
            return x / jnp.maximum(n, eps)

        def decay_gammas(num_heads, dtype=jnp.float32):
            return 1.0 - jnp.exp(jnp.linspace(math.log(1.0 / 32.0), math.log(1.0 / 512.0), num_heads)).astype(dtype)
        B, T, D = x.shape
        H = N_HEADS
        dh = D // H
        residual = x
        xn = channel_group_norm(x, norm_g, norm_b, H)
        q = l2_normalize(xn @ qw.T)
        k = l2_normalize(xn @ kw.T)
        v = xn @ vw.T

        def heads(t):
            return t.reshape(B, T, H, dh).transpose(0, 2, 1, 3)
        qh, kh, vh = (heads(q), heads(k), heads(v))
        gammas = decay_gammas(H)
        n = jnp.arange(T)[:, None]
        m = jnp.arange(T)[None, :]
        diff = n - m
        causal = diff >= 0
        exponent = jnp.where(causal, diff, 0).astype(jnp.float32)
        dmask = jnp.where(causal[None], gammas[:, None, None] ** exponent[None], 0.0)
        scale = 1.0 / math.sqrt(dh)
        sim = jnp.einsum('bhnd,bhmd->bhnm', qh, kh) * scale
        sim = sim * dmask[None]
        yh = jnp.einsum('bhnm,bhmd->bhnd', sim, vh)
        y = yh.transpose(0, 2, 1, 3).reshape(B, T, D)
        y = y @ ow.T + ob
        x = residual + y
        residual = x
        xn = channel_group_norm(x, ffn_norm_g, ffn_norm_b, H)
        h = jax.nn.silu(xn @ w1.T + b1)
        x = residual + (h @ w2.T + b2)
        return x

    def _L0_ffn_ref(x, wqkv, q_scale, k_scale, wo, ln_g, ln_b, w1, b1, w2, b2):
        import jax, jax.numpy as jnp
        import numpy as np
        DIM = 128
        DEPTH = 2
        HEADS = 8
        DIM_HEAD = 64
        WINDOW = 64
        INNER = HEADS * DIM_HEAD
        HID = int(DIM * 4 * 2 / 3)
        B, N = (2, 1024)
        QK_SCALE = 8.0

        def shift_token(t):
            t1, t2 = jnp.split(t, 2, axis=-1)
            t2 = jnp.pad(t2, ((0, 0), (1, 0), (0, 0)))[:, :-1]
            return jnp.concatenate([t1, t2], axis=-1)

        def l2norm(t):
            return t / jnp.clip(jnp.linalg.norm(t, axis=-1, keepdims=True), 1e-12)

        def rotate_half(x):
            x1, x2 = jnp.split(x, 2, axis=-1)
            return jnp.concatenate([-x2, x1], axis=-1)

        def rotary_xpos(q, k):
            n = q.shape[-2]
            half_idx = jnp.arange(0, DIM_HEAD, 2, dtype=jnp.float32)
            inv_freq = 1.0 / 10000.0 ** (half_idx / DIM_HEAD)
            t = jnp.arange(n, dtype=jnp.float32)
            freqs = t[:, None] * inv_freq[None, :]
            freqs = jnp.concatenate([freqs, freqs], axis=-1)
            base = (half_idx + 0.4 * DIM_HEAD) / (1.4 * DIM_HEAD)
            power = (t - n // 2) / float(WINDOW // 2)
            scale = base[None, :] ** power[:, None]
            scale = jnp.concatenate([scale, scale], axis=-1)
            cos, sin = (jnp.cos(freqs), jnp.sin(freqs))
            q = q * cos * scale + rotate_half(q) * sin * scale
            k = k * cos / scale + rotate_half(k) * sin / scale
            return (q, k)

        def local_attention(q, k, v):
            b, h, n, d = q.shape
            w = n // WINDOW
            bq = q.reshape(b, h, w, WINDOW, d) * QK_SCALE
            bk = k.reshape(b, h, w, WINDOW, d)
            bv = v.reshape(b, h, w, WINDOW, d)

            def look_around(t):
                p = jnp.pad(t, ((0, 0), (0, 0), (1, 0), (0, 0), (0, 0)))
                return jnp.concatenate([p[:, :, :w], p[:, :, 1:]], axis=3)
            bk, bv = (look_around(bk), look_around(bv))
            bt = jnp.arange(n).reshape(w, WINDOW)
            btp = jnp.pad(bt, ((1, 0), (0, 0)), constant_values=-1)
            btk = jnp.concatenate([btp[:w], btp[1:]], axis=1)
            sim = jnp.einsum('bhwid,bhwjd->bhwij', bq, bk)
            i = bt[:, :, None]
            j = btk[:, None, :]
            mask = (i < j) | (i > j + WINDOW) | (j == -1)
            sim = jnp.where(mask, -jnp.finfo(sim.dtype).max, sim)
            attn = jax.nn.softmax(sim, axis=-1)
            out = jnp.einsum('bhwij,bhwjd->bhwid', attn, bv)
            return out.reshape(b, h, n, d)

        def _layer(x, wqkv, qs, ksc, wo, lg, lb, w1, b1, w2, b2):
            b, n, _ = x.shape
            h = shift_token(x)
            qkv = h @ wqkv
            q, k, v = jnp.split(qkv, 3, axis=-1)
            to_heads = lambda t: t.reshape(b, n, HEADS, DIM_HEAD).transpose(0, 2, 1, 3)
            q, k, v = (to_heads(q), to_heads(k), to_heads(v))
            q = l2norm(q) * qs
            k = l2norm(k) * ksc
            q, k = rotary_xpos(q, k)
            o = local_attention(q, k, v)
            o = o.transpose(0, 2, 1, 3).reshape(b, n, INNER)
            x = x + o @ wo
            h = shift_token(x)
            mu = h.mean(-1, keepdims=True)
            var = h.var(-1, keepdims=True)
            h = (h - mu) / jnp.sqrt(var + 1e-05) * lg + lb
            h = h @ w1 + b1
            a, g = jnp.split(h, 2, axis=-1)
            h = a * jax.nn.gelu(g, approximate=False)
            x = x + h @ w2 + b2
            return x
        for l in range(DEPTH):
            x = _layer(x, wqkv[l], q_scale[l], k_scale[l], wo[l], ln_g[l], ln_b[l], w1[l], b1[l], w2[l], b2[l])
        return x
    x = L0_attn_x
    xn = _layernorm(x, axis=-1)
    x = x + _L0_attn_ref(xn, L0_attn_norm_g, L0_attn_norm_b, L0_attn_qw, L0_attn_kw, L0_attn_vw, L0_attn_ow, L0_attn_ob, L0_attn_ffn_norm_g, L0_attn_ffn_norm_b, L0_attn_w1, L0_attn_b1, L0_attn_w2, L0_attn_b2) + _L0_ffn_ref(xn, L0_ffn_wqkv, L0_ffn_q_scale, L0_ffn_k_scale, L0_ffn_wo, L0_ffn_ln_g, L0_ffn_ln_b, L0_ffn_w1, L0_ffn_b1, L0_ffn_w2, L0_ffn_b2)
    return x

_drawn_inputs = setup_inputs


def setup_inputs(seed=0):
    import zlib

    import numpy as np

    out = dict(_drawn_inputs(seed))
    spreads = {'L0_attn_norm_g': (1.0, 0.6),
     'L0_attn_norm_b': (0.0, 2.0),
     'L0_attn_ob': (0.0, 2.0),
     'L0_attn_ffn_norm_g': (1.0, 0.6),
     'L0_attn_ffn_norm_b': (0.0, 2.0),
     'L0_attn_b1': (0.0, 2.0),
     'L0_attn_b2': (0.0, 2.0),
     'L0_ffn_q_scale': (1.0, 0.6),
     'L0_ffn_k_scale': (1.0, 0.6),
     'L0_ffn_ln_g': (1.0, 0.6),
     'L0_ffn_ln_b': (0.0, 0.8),
     'L0_ffn_b1': (0.0, 0.8),
     'L0_ffn_b2': (0.0, 0.741)}
    factors = {'L0_ffn_wqkv': 6.095,
     'L0_ffn_wo': 6.051,
     'L0_ffn_w1': 8.0,
     'L0_ffn_w2': 8.0,
     'L0_attn_qw': 3.544,
     'L0_attn_kw': 3.339,
     'L0_attn_vw': 3.508,
     'L0_attn_ow': 3.538,
     'L0_attn_w1': 4.376,
     'L0_attn_w2': 3.748}
    for name, (base, spread) in spreads.items():
        noise = np.random.default_rng([zlib.crc32(name.encode()), seed]).standard_normal(out[name].shape)
        drawn = base * np.exp(spread * noise) if base else spread * noise
        out[name] = jnp.asarray(drawn.astype(out[name].dtype))
    for name, factor in factors.items():
        out[name] = (out[name] * factor).astype(out[name].dtype)
    return out
```

```python
from contextlib import ExitStack

import concourse.bass as bass
import numpy as np
from concourse import mybir

F32 = mybir.dt.float32
BF16 = mybir.dt.bfloat16
ALU = mybir.AluOpType
ACT = mybir.ActivationFunctionType
AX = mybir.AxisListType

P = 128
NB = 4
T = 1024
NT = T // P
D = 128
RH, RD = 16, 8
BL = 32
NBL = P // BL
NG = 4
DEPTH = 2
H, DH = 8, 64
INNER = H * DH
WIN = 64
HID = int(D * 4 * 2 / 3)
CHUNKS = [(0, 128), (128, 128), (256, HID - 256)]
NC = len(CHUNKS)
EPS = 1e-5
MASKED = -1e30

C_ID, C_GRP, C_GQ, C_GK, C_BD, C_VM, C_CAUSAL = 0, 128, 256, 384, 512, 640, 768
C_HM = C_CAUSAL + BL
C_GM, C_SD = C_HM + NG, C_HM + 2 * NG
C_END = C_SD + 1


def constants():
    f = np.float32
    cst = np.zeros((P, C_END), f)
    i = np.arange(P)
    cst[:, C_ID:C_ID + P] = np.eye(P)
    cst[:, C_GRP:C_GRP + P] = (i[:, None] // RD == i[None, :] // RD) / RD
    cst[:, C_CAUSAL:C_CAUSAL + BL] = i[:, None] % BL <= i[None, :BL]
    lin = np.linspace(np.log(1.0 / 32.0), np.log(1.0 / 512.0), RH).astype(f)
    gam = (f(1.0) - np.exp(lin)).astype(np.float64)
    head = i // RD
    cst[:, C_GQ:C_GQ + P] = gam[head][None, :] ** i[:, None] / np.sqrt(RD)
    cst[:, C_GK:C_GK + P] = gam[head][None, :] ** (-i[:, None].astype(np.float64))
    cst[:, C_BD:C_BD + P] = head[:, None] == head[None, :]
    cst[:, C_VM:C_VM + P] = i[:, None] // BL == head[None, :] % NG
    cst[:, C_HM:C_HM + NG] = head[:, None] % NG == np.arange(NG)[None, :]
    cst[:, C_GM:C_GM + NG] = head[:, None] // NG == np.arange(NG)[None, :]
    cst[:, C_SD] = gam[head] ** P
    half = np.arange(0, DH, 2, dtype=f)
    inv = (f(1.0) / np.power(f(10000.0), half / f(DH))).astype(f)
    t = np.arange(T, dtype=f)
    fr = t[:, None] * inv[None, :]
    fr = np.concatenate([fr, fr], -1)
    base = ((half + f(0.4 * DH)) / f(1.4 * DH)).astype(f)
    power = (t - f(T // 2)) / f(WIN // 2)
    sc = np.power(base[None, :], power[:, None]).astype(f)
    sc = np.concatenate([sc, sc], -1)
    sign = np.where(np.arange(DH) < DH // 2, -1.0, 1.0).astype(f)
    cos, sin = np.cos(fr), np.sin(fr) * sign
    tab = np.stack([cos * sc * f(8), cos / sc, sin * sc * f(8), sin / sc], 1).astype(f)
    tab = tab.reshape(NT, P, 4, DH).transpose(1, 0, 2, 3)
    own = (i[:WIN, None] >= i[None, :WIN])
    before = (i[:WIN, None] <= i[None, :WIN])
    even = np.concatenate([own, before], 1)
    odd = np.concatenate([before, own], 1)
    m = np.concatenate([even, odd], 0)
    first = m.copy()
    first[:WIN, WIN:] = False
    mask = np.where(np.stack([first, m], 1), 0.0, MASKED).astype(f)
    mask = np.concatenate([mask, np.eye(P, dtype=f)[:, None, :]], 1)
    return cst, np.ascontiguousarray(tab), np.ascontiguousarray(mask)


def need(eng, sem, value):
    if isinstance(value, int) and value <= 0:
        return
    eng.wait_ge(sem, value)


def program(nc, a, out):
    with ExitStack() as ctx:
        def sb(name, shape, dt=F32):
            return ctx.enter_context(nc.sbuf_tensor(name, shape, dt))

        def sem(name):
            return ctx.enter_context(nc.semaphore(name))

        cst = sb("cst", [P, C_END])
        ident = cst[:, C_ID:C_ID + P]
        group_avg = cst[:, C_GRP:C_GRP + P]
        causal = cst[:, C_CAUSAL:C_CAUSAL + BL]
        decay_q = cst[:, C_GQ:C_GQ + P]
        decay_k = cst[:, C_GK:C_GK + P]
        same_head = cst[:, C_BD:C_BD + P]
        value_mask = cst[:, C_VM:C_VM + P]
        place_mask = cst[:, C_HM:C_HM + NG]
        group_mask = cst[:, C_GM:C_GM + NG]
        state_decay = cst[:, C_SD:C_SD + 1]
        mask32 = sb("mask32", [P, 3, P])
        mask16 = sb("mask16", [P, 3, P], BF16)
        tab = sb("tab", [P, NT, 4, DH])
        gain = sb("gain", [P, DEPTH, 2, DH])
        rope = [sb("rope0", [P, NT, 4, DH]), tab]
        half_neg = sb("half_neg", [P, NB * NT])
        wqkv = sb("wqkv", [P, DEPTH, 3 * INNER])
        wo = sb("wo", [P, DEPTH, 4, D])
        w1 = sb("w1", [P, DEPTH, 2 * HID])
        w2 = sb("w2", [P, DEPTH, NC, D])
        b1c = sb("b1c", [P, DEPTH, 2, NC])
        b1e = sb("b1e", [P, DEPTH, 2, NC])
        col = sb("col", [P, 16])
        COLS = {"ng": 0, "nb": 1, "ob": 2, "fg": 3, "fb": 4, "b1a": 5, "b2a": 7,
                "lg": 8, "lb": 10, "b2": 12}

        def c(name, k=0):
            return col[:, COLS[name] + k:COLS[name] + k + 1]

        aT = sb("aT", [P, 8, P])

        x = sb("x", [P, NB, NT, D])
        x1T = x[:, :, :, :].rearrange("p b t d -> p b (t d)")
        xnT = sb("xnT", [P, NB, 1 + T])
        x2T = sb("x2T", [P, NB, 1 + T])

        bst = sb("bst", [P, NB, 6])
        mv = sb("mv", [P, NT, NB, 2])
        vpe = sb("vpe", [P, NT, NB])
        rstd = sb("rstd", [P, NT, NB])
        cbst = [sb(f"cbst{k}", [P, NB, NT, 6]) for k in range(2)]
        cmv = sb("cmv", [P, NB, 2])
        cst2 = sb("cst2", [P, 2, NB])
        gst = sb("gst", [P, 2, NB])
        gtmp = sb("gtmp", [P, 2, NB])
        grs = sb("grs", [P, NB])
        gsc = [sb(f"gsc{k}", [P, NB]) for k in range(2)]
        gsh = [sb(f"gsh{k}", [P, NB]) for k in range(2)]

        hT = sb("hT", [P, NB, P])
        sq = sb("sq", [P, 2 * INNER])
        ss = sb("ss", [P, 2, 2 * H])
        rn = sb("rn", [P, 2, 2 * H])
        m1 = sb("m1", [P, 2, 2 * INNER])
        m2 = sb("m2", [P, 2, 2 * INNER])
        qkn = sb("qkn", [P, 2, 2 * INNER])
        xn = m1[:, :, 0:NB * D].rearrange("p u (b d) -> p u b d", b=NB)
        qT = sb("qT", [P, 4, P])
        kT = [sb(f"kT{b}", [P, 4, P + WIN]) for b in range(NB)]
        vown = [sb(f"vown{b}", [P, H, DH + 1]) for b in range(NB)]
        vmix = [sb(f"vmix{b}", [P, H, DH + 1]) for b in range(NB)]
        mx = sb("mx", [P, H])
        pr = sb("pr", [P, 2, H, P])
        prT = sb("prT", [P, H, P])
        rec = sb("rec", [P, 2, 4])
        o = sb("o", [P, INNER])
        oT = sb("oT", [P, 4, NB, P])
        xr = sb("xr", [P, NB, 1 + P])
        lmv = sb("lmv", [P, NB, 2])
        lbst = sb("lbst", [P, NB, 6])
        lvar = sb("lvar", [P, NB])
        lrs = sb("lrs", [P, NB])
        hn = sb("hn", [P, NB, D])
        hnT = sb("hnT", [P, NB * P])
        gg = m2[:, 0, :].rearrange("p (s n) -> p s n", s=2)
        hf = m1[:, :, :].rearrange("p u n -> p (u n)")[:, 0:NC * NB * P].rearrange("p (k n) -> p k n", k=NC)
        xa = sb("xa", [P, NB, P])
        xa4 = sb("xa4", [P, 2, NBL, NG, BL])
        asq = sb("asq", [P, P])
        ass = sb("ass", [P, 2, 2])
        ars = sb("ars", [P, 2, 2])
        aqk = qkn[:, 0, :].rearrange("p (b g n) -> p b g n", b=NB, g=2)
        av = sb("av", [P, NB, P])
        aqkT = qkn[:, 1, :].rearrange("p (b g n) -> p b g n", b=NB, g=2)
        araw = pr[:, :, :, :].rearrange("p u h n -> p (u h) n")[:, 0:8, :]
        state = sb("state", [P, NB, P])
        vx = pr[:, :, :, :].rearrange("p u h n -> p (u h n)").rearrange("p (b c n) -> p b c n", b=NB, c=NBL)
        kx = sq[:, :].rearrange("p (u c j n) -> p u c j n", u=2, c=NBL, j=NG)
        qx = prT[:, :, :].rearrange("p h n -> p (h n)").rearrange("p (u c g n) -> p u c g n", u=2, c=NBL, g=NG)
        sm = m1[:, 0, :].rearrange("p (u c g n) -> p u c g n", u=2, c=NBL, g=NG)
        before = m1[:, 1, :].rearrange("p (u c n) -> p u c n", u=2, c=NBL)
        ayT = m2[:, 1, 0:NB * P]
        afh = gg
        att = state
        fin = sb("fin", [P, NB, P])
        xs = sb("xs", [P, NB, D])
        osb = sb("osb", [P, NB, D])

        pQK = ctx.enter_context(nc.psum_tensor("pQK", [P, 1024], F32))
        pV = ctx.enter_context(nc.psum_tensor("pV", [P, 512], F32))
        pT = ctx.enter_context(nc.psum_tensor("pT", [P, 1024], F32))
        pS = ctx.enter_context(nc.psum_tensor("pS", [P, 1024], F32))
        pM = ctx.enter_context(nc.psum_tensor("pM", [P, 512], F32))

        def ln_in(b):
            return pS[:, :].rearrange("p (s z) -> p s z", s=2)[:, :, b * 64:b * 64 + 64]

        x_ld = [sem(f"x_ld{b}") for b in range(NB)]
        cst_ld, tab_ld, aw_ld, w_ld, gain_ld, col_ld = (
            sem(n) for n in ("cst_ld", "tab_ld", "aw_ld", "w_ld", "gain_ld", "col_ld"))
        memset_done, one_done, mask_done = sem("memset_done"), sem("one_done"), sem("mask_done")
        xst_done, agg_done, st_done, var_done, rstd_done, xn_done, xnt_mm, xnt_ev, cs_done = (
            sem(n) for n in ("xst_done", "agg_done", "st_done", "var_done", "rstd_done", "xn_done", "xnt_mm", "xnt_ev", "cs_done"))
        awt_mm, awt_ev, be_mm, be_done, w1g_done, rope_done = (
            sem(n) for n in ("awt_mm", "awt_ev", "be_mm", "be_done", "w1g_done", "rope_done"))
        gn = [{n: sem(f"gn{k}_{n}") for n in ("agg", "dve", "mm", "var", "rs", "done")} for k in range(2)]
        LS = {n: sem(n) for n in (
            "carried", "v_kept", "h_ready", "qk_mm", "v_mm", "sq_done", "ss_done", "mul_done", "max_ss", "rn_done", "add_done",
            "qkn_done", "t_mm", "t_ev", "v_ev", "vmix_done", "s_mm", "mx_done", "sub_done", "exp_done",
            "pt_mm", "pt_ev", "o_mm", "rec_done", "o_done", "ot_mm", "ot_ev", "wo_mm", "xr_carried", "xr_done",
            "ln_mm", "ln_bst", "ln_st", "ln_eps", "ln_rs", "hn_done", "hnt_mm", "hnt_ev", "ag_mm", "gelu_done",
            "hf_done", "w2_mm", "x2_done")}
        A = {n: sem(f"a_{n}") for n in (
            "xa", "xa4", "qkv_mm", "sqq", "v", "floor", "rs", "qk", "t_mm", "t_ev", "vx_mm", "vx", "kx", "qx", "st_mm", "sm",
            "kv_mm", "kvm", "before", "y_mm", "yt", "state", "ow_mm", "x1", "cs")}
        G = {n: sem(f"g_{n}") for n in ("xa", "w1_mm", "silu", "w2_mm", "att", "fin", "fin_mm", "xs", "osb", "out")}

        x_steps = a["L0_attn_x"].rearrange("b (t p) d -> t p b d", p=P)
        out_steps = out.rearrange("b (t p) d -> t p b d", p=P)
        block = ctx.enter_context(nc.Block())

        def need_apart(eng, sem, value):
            if isinstance(value, int):
                return need(eng, sem, value)
            register = eng.to_reg(value)
            eng.wait_ge(cst_ld, 32)
            eng.wait_ge(sem, register)

        @block.sync
        def _(sp):
            for b in range(NB):
                sp.dma_start(x[:, b, :, :], a["L0_attn_x"][b].rearrange("(t p) d -> p t d", p=P)).then_inc(x_ld[b], 16)
            sp.dma_start(tab[:, :, :, :], a["k_tab"]).then_inc(tab_ld, 16)
            for l in range(DEPTH):
                sp.dma_start(wqkv[:, l, :], a["L0_ffn_wqkv"][l]).then_inc(w_ld, 16)
                sp.dma_start(wo[:, l, :, :], a["L0_ffn_wo"][l].rearrange("(c p) d -> p c d", p=P)).then_inc(w_ld, 16)
                sp.dma_start(w1[:, l, :], a["L0_ffn_w1"][l]).then_inc(w_ld, 16)
                sp.dma_start(w2[:, l, 0:2, :], a["L0_ffn_w2"][l, 0:2 * P, :].rearrange("(c p) d -> p c d", p=P)).then_inc(w_ld, 16)
                sp.dma_start(w2[0:CHUNKS[2][1], l, 2, :], a["L0_ffn_w2"][l, 2 * P:HID, :]).then_inc(w_ld, 16)
            sp.dma_start(xs[:, :, :], x_steps[0]).then_inc(G["xs"], 16)
            sp.wait_ge(G["osb"], 1)
            sp.dma_start(out_steps[0], osb[:, :, :]).then_inc(G["out"], 16)
            with sp.Fori(1, NT) as t:
                sp.dma_start(xs[:, :, :], x_steps[t]).then_inc(G["xs"], 16)
                sp.wait_ge(G["osb"], t + 1)
                sp.dma_start(out_steps[t], osb[:, :, :]).then_inc(G["out"], 16)
            sp.wait_ge(G["out"], 16 * NT)

        def pool_layer_step(eng, l, t):
            S, ct = LS, NT * l + t
            src = xnT if l == 0 else x2T
            first = isinstance(t, int)
            need_apart(eng, S["v_mm"], 4 * ct)
            eng.tensor_copy(hT[0:64, :, :], src[0:64, :, bass.ds(t * P + 1, P)]).then_inc(S["h_ready"], 1)
            for k in range(NB + 1):
                if k < NB:
                    n = 4 * ct + k
                    if not first:
                        need_apart(eng, S["o_mm"], n - 3)
                        eng.tensor_copy(kT[k][:, :, P:P + WIN], kT[k][:, :, WIN:P]).then_inc(S["carried"], 1)
                    need_apart(eng, S["ss_done"], n + 1)
                    eng.tensor_scalar(rn[:, k % 2, :], ss[:, k % 2, :], 1e-24, None, ALU.max).then_inc(S["max_ss"], 1)
                    eng.wait_ge(S["max_ss"], n + 1)
                    eng.tensor_tensor(rn[:, k % 2, :], rn[:, k % 2, :], half_neg[:, 0:2 * H], ALU.pow).then_inc(S["rn_done"], 1)
                    eng.wait_ge(S["mul_done"], 2 * n + 2)
                    eng.tensor_tensor(m1[:, k % 2, :], m1[:, k % 2, :], m2[:, k % 2, :], ALU.add).then_inc(S["add_done"], 1)
                    eng.wait_ge(S["add_done"], n + 1)
                    eng.wait_ge(S["rn_done"], n + 1)
                    need(eng, S["t_mm"], n - 1)
                    eng.tensor_tensor(qkn[:, k % 2, :].rearrange("p (h d) -> p h d", d=DH),
                                      m1[:, k % 2, :].rearrange("p (h d) -> p h d", d=DH),
                                      rn[:, k % 2, :].unsqueeze(2).broadcast_to([P, 2 * H, DH]),
                                      ALU.mult).then_inc(S["qkn_done"], 1)
                    need_apart(eng, S["v_ev"], n + 1)
                    eng.tensor_copy(vmix[k][0:64, :, 0:DH], vown[k][0:64, :, 0:DH]).then_inc(S["vmix_done"], 1)
            if not first:
                need_apart(eng, S["x2_done"], ct)
                eng.tensor_copy(xr[:, :, 0:1], xr[:, :, P:P + 1]).then_inc(S["xr_carried"], 1)
            need_apart(eng, S["ln_st"], NB * ct + NB)
            eng.tensor_scalar(lvar[:, :], lmv[:, :, 1], EPS, None, ALU.add).then_inc(S["ln_eps"], 1)
            eng.wait_ge(S["ln_eps"], ct + 1)
            eng.tensor_tensor(lrs[:, :], lvar[:, :], half_neg[:, 0:NB], ALU.pow).then_inc(S["ln_rs"], 1)

        def pool_retention_step(eng, t):
            for b in range(NB):
                n = 4 * t + b
                need_apart(eng, A["sqq"], 2 * n + 2)
                eng.tensor_scalar(ars[:, b % 2, :], ass[:, b % 2, :], 1e-24, None, ALU.max).then_inc(A["floor"], 1)
                eng.wait_ge(A["floor"], n + 1)
                eng.tensor_tensor(ars[:, b % 2, :], ars[:, b % 2, :], half_neg[:, 0:2], ALU.pow).then_inc(A["rs"], 1)
                if b > 0:
                    pool_mask_qk(eng, t, b - 1)
            pool_mask_qk(eng, t, NB - 1)

        def pool_mask_qk(eng, t, b):
            n = 4 * t + b
            shape = [P, NBL, NG, BL]
            eng.wait_ge(A["t_ev"], n + 1)
            need(eng, A["st_mm"], n - 1)
            eng.tensor_tensor(kx[:, b % 2, :, :, :],
                              aqkT[:, b, 1, :].rearrange("p (c n) -> p c n", c=NBL).unsqueeze(2).broadcast_to(shape),
                              place_mask.unsqueeze(1).unsqueeze(3).broadcast_to(shape), ALU.mult).then_inc(A["kx"], 1)
            need(eng, A["y_mm"], n - 1)
            eng.tensor_tensor(qx[:, b % 2, :, :, :],
                              aqkT[:, b, 0, :].rearrange("p (c n) -> p c n", c=NBL).unsqueeze(2).broadcast_to(shape),
                              group_mask.unsqueeze(1).unsqueeze(3).broadcast_to(shape), ALU.mult).then_inc(A["qx"], 1)

        def pool_group_norm(eng, k):
            g = gn[k]
            eng.wait_ge(g["var"], 1)
            eng.tensor_tensor(grs[:, :], gtmp[:, 0, :], half_neg[:, 0:NB], ALU.pow).then_inc(g["rs"], 1)

        @block.gpsimd
        def _(eng):
            eng.memset(half_neg[:, :], -0.5).then_inc(memset_done, 1)
            eng.memset(state[:, :, :], 0.0).then_inc(memset_done, 1)
            eng.memset(xnT[:, :, 0:1], 0.0).then_inc(memset_done, 1)
            eng.memset(x2T[:, :, 0:1], 0.0).then_inc(memset_done, 1)
            for b in range(NB):
                eng.memset(kT[b][:, :, P:P + WIN], 0.0).then_inc(memset_done, 1)
                eng.memset(vmix[b][:, :, 0:DH], 0.0).then_inc(memset_done, 1)
                eng.memset(vown[b][:, :, DH:DH + 1], 1.0).then_inc(memset_done, 1)
                eng.memset(vmix[b][:, :, DH:DH + 1], 1.0).then_inc(memset_done, 1)
            eng.memset(xr[:, :, 0:1], 0.0).then_inc(memset_done, 1)
            eng.wait_ge(memset_done, 5 + 4 * NB)
            eng.wait_ge(st_done, NT)
            eng.tensor_scalar(vpe[:, :, :], mv[:, :, :, 1], EPS, None, ALU.add).then_inc(var_done, 1)
            eng.wait_ge(var_done, 1)
            eng.tensor_tensor(rstd[:, :, :], vpe[:, :, :],
                              half_neg[:, :].rearrange("p (t b) -> p t b", b=NB), ALU.pow).then_inc(rstd_done, 1)
            eng.wait_ge(tab_ld, 16)
            eng.wait_ge(gain_ld, 16 * 4)
            for l in range(DEPTH):
                for g in range(2):
                    eng.tensor_tensor(rope[l][:, :, g, :], tab[:, :, g, :],
                                      gain[:, l, g, :].unsqueeze(1).broadcast_to([P, NT, DH]),
                                      ALU.mult).then_inc(rope_done, 1)
                    for s in range(2):
                        eng.tensor_tensor(rope[l][:, :, 2 + g, 32 * s:32 * s + 32], tab[:, :, 2 + g, 32 * s:32 * s + 32],
                                          gain[:, l, g, 32 - 32 * s:64 - 32 * s].unsqueeze(1).broadcast_to([P, NT, 32]),
                                          ALU.mult).then_inc(rope_done, 1)
            pool_group_norm(eng, 0)
            pool_layer_step(eng, 0, 0)
            pool_retention_step(eng, 0)
            with eng.Fori(1, NT) as t:
                pool_layer_step(eng, 0, t)
                pool_retention_step(eng, t)
            eng.wait_ge(LS["x2_done"], NT)
            for b in range(NB):
                eng.memset(kT[b][:, :, P:P + WIN], 0.0).then_inc(one_done, 1)
                eng.memset(vmix[b][:, :, 0:DH], 0.0).then_inc(one_done, 1)
            eng.memset(xr[:, :, 0:1], 0.0).then_inc(one_done, 1)
            eng.wait_ge(one_done, 2 * NB + 1)
            pool_group_norm(eng, 1)
            pool_layer_step(eng, 1, 0)
            with eng.Fori(1, NT) as t:
                pool_layer_step(eng, 1, t)

        def act_layer_attn(eng, l, t):
            S, ct = LS, NT * l + t
            first = isinstance(t, int)
            src = xnT if l == 0 else x2T
            need(eng, S["v_mm"], 4 * ct)
            eng.activation(hT[64:P, :, :], src[64:P, :, bass.ds(t * P, P)], ACT.Copy).then_inc(S["h_ready"], 1)
            for k in range(NB + 4):
                if k < NB and not first:
                    need(eng, S["o_mm"], 4 * ct + k - 3)
                    eng.activation(vmix[k][64:P, :, 0:DH], vown[k][64:P, :, 0:DH], ACT.Copy).then_inc(S["v_kept"], 1)
                if 0 <= k - 4 < NB:
                    b = k - 4
                    eng.wait_ge(S["ot_mm"], 4 * ct + b + 1)
                    eng.activation(oT[:, :, b, :], pM[:, :].rearrange("p (c n) -> p c n", c=4), ACT.Copy).then_inc(S["ot_ev"], 1)
                if 0 <= k - 2 < NB:
                    b = k - 2
                    n = 4 * ct + b
                    eng.wait_ge(S["t_mm"], n + 1)
                    eng.activation(qT[:, :, :], pT[:, 0:512].rearrange("p (c n) -> p c n", c=4), ACT.Copy).then_inc(S["t_ev"], 1)
                    if not first:
                        need(eng, S["carried"], n - 3 - 4 * l)
                    eng.activation(kT[b][:, :, 0:P], pT[:, 512:1024].rearrange("p (c n) -> p c n", c=4), ACT.Copy).then_inc(S["t_ev"], 1)
                if k < NB:
                    n = 4 * ct + k
                    eng.wait_ge(S["qk_mm"], n + 1)
                    need(eng, S["ss_done"], n)
                    eng.activation(sq[:, :], pQK[:, :], ACT.Square).then_inc(S["sq_done"], 1)
                if 0 <= k - 3 < NB:
                    b = k - 3
                    eng.wait_ge(S["pt_mm"], 4 * ct + b + 1)
                    eng.activation(prT[:, :, :], pT[:, :].rearrange("p (h n) -> p h n", h=H), ACT.Copy).then_inc(S["pt_ev"], 1)
                if k < NB:
                    n = 4 * ct + k
                    eng.wait_ge(S["v_mm"], n + 1)
                    if not first:
                        need(eng, S["vmix_done"], n - 3)
                        need(eng, S["v_kept"], n - 3 - 4 * l)
                    eng.activation(vown[k][:, :, 0:DH], pV[:, :].rearrange("p (h d) -> p h d", h=H), ACT.Copy).then_inc(S["v_ev"], 1)
                if 0 <= k - 2 < NB:
                    b = k - 2
                    n = 4 * ct + b
                    eng.wait_ge(S["sub_done"], n + 1)
                    eng.activation(pr[:, b % 2, :, :], pr[:, b % 2, :, :], ACT.Exp).then_inc(S["exp_done"], 1)

        def act_ln_ev(eng, l, t):
            S, ct = LS, NT * l + t
            eng.wait_ge(S["hnt_mm"], ct + 1)
            eng.activation(hnT[:, :], pS[:, 512:1024], ACT.Copy).then_inc(S["hnt_ev"], 1)

        def act_gelu(eng, l, t):
            S, ct = LS, NT * l + t
            for k, (lo, m) in enumerate(CHUNKS):
                eng.wait_ge(S["ag_mm"], NC * ct + k + 1)
                need(eng, S["hf_done"], NC * ct + k - 1)
                pag = pQK if k % 2 == 0 else pT
                eng.activation(gg[0:m, k % 2, :], pag[0:m, 512:1024], ACT.Gelu,
                               bias=b1e[0:m, l, 1, k:k + 1]).then_inc(S["gelu_done"], 1)

        def act_retention(eng, t):
            for k in range(NB + 2):
                if 0 <= k - 1 < NB:
                    b = k - 1
                    eng.wait_ge(A["t_mm"], 4 * t + b + 1)
                    eng.activation(aqkT[:, b, :, :], pM[:, 0:256].rearrange("p (g n) -> p g n", g=2), ACT.Copy).then_inc(A["t_ev"], 1)
                if k < NB:
                    n = 4 * t + k
                    eng.wait_ge(A["xa"], n + 1)
                    need(eng, A["vx_mm"], n - 1)
                    eng.activation(xa4[:, k % 2, :, :, :],
                                   xa[:, k, :].rearrange("p (c n) -> p c n", c=NBL).unsqueeze(2).broadcast_to(
                                       [P, NBL, NG, BL]), ACT.Copy).then_inc(A["xa4"], 1)
                    eng.wait_ge(A["qkv_mm"], n + 1)
                    need(eng, A["rs"], n - 1)
                    for g in range(2):
                        need(eng, A["sqq"], 2 * n + g)
                        eng.activation(asq[:, :], pV[:, g * P:(g + 1) * P], ACT.Square,
                                       accum_out=ass[:, k % 2, g:g + 1]).then_inc(A["sqq"], 1)
                    eng.activation(av[:, k, :], pV[:, 2 * P:3 * P], ACT.Copy).then_inc(A["v"], 1)
                if k == 2:
                    act_ln_ev(eng, 0, t)
                if 0 <= k - 2 < NB:
                    b = k - 2
                    eng.wait_ge(A["y_mm"], 4 * t + b + 1)
                    for g in range(NG):
                        r = slice(BL * g, BL * g + BL)
                        eng.activation(ayT[r, b * P:(b + 1) * P].rearrange("p (c n) -> p c n", c=NBL),
                                       pT[r, 512:1024].rearrange("p (c g n) -> p c g n", c=NBL, g=NG)[:, :, g, :],
                                       ACT.Copy).then_inc(A["yt"], 1)

        def act_block_ffn(eng, t):
            for j in range(2):
                eng.wait_ge(G["w1_mm"], 2 * t + j + 1)
                eng.activation(afh[:, j, :], pQK[:, j * 512:(j + 1) * 512], ACT.Silu, bias=c("b1a", j)).then_inc(G["silu"], 1)

        @block.scalar
        def _(eng):
            eng.dma_start(cst[:, :], a["k_cst"]).then_inc(cst_ld, 16)
            eng.dma_start(mask32[:, :, :], a["k_mask"]).then_inc(cst_ld, 16)
            for k, n in enumerate(("qw", "kw", "vw", "ow")):
                eng.dma_start(araw[:, k, :], a["L0_attn_" + n]).then_inc(aw_ld, 16)
            eng.dma_start(araw[:, 4:6, :], a["L0_attn_w1"].rearrange("(c p) d -> p c d", p=P)).then_inc(aw_ld, 16)
            eng.dma_start(araw[:, 6:8, :], a["L0_attn_w2"].rearrange("p (c d) -> p c d", c=2)).then_inc(aw_ld, 16)

            def column(name, ap, k=1):
                with nc.allow_non_contiguous_dma(reason="one value per partition"):
                    eng.dma_start(col[:, COLS[name]:COLS[name] + k], ap).then_inc(col_ld, 16)
            for name, arg in (("ng", "norm_g"), ("nb", "norm_b"), ("ob", "ob"), ("fg", "ffn_norm_g"),
                              ("fb", "ffn_norm_b"), ("b2a", "b2")):
                column(name, a["L0_attn_" + arg].rearrange("(p o) -> p o", o=1))
            column("b1a", a["L0_attn_b1"].rearrange("(c p) -> p c", p=P), 2)
            for name, arg in (("lg", "ln_g"), ("lb", "ln_b"), ("b2", "b2")):
                column(name, a["L0_ffn_" + arg].rearrange("l p -> p l"), 2)
            for g, n in enumerate(("q_scale", "k_scale")):
                for l in range(DEPTH):
                    eng.dma_start(gain[:, l, g, :], a["L0_ffn_" + n][l:l + 1, :].broadcast_to([P, DH])).then_inc(gain_ld, 16)
            with nc.allow_non_contiguous_dma(reason="one value per partition"):
                for l in range(DEPTH):
                    for s in range(2):
                        row = a["L0_ffn_b1"][l, s * HID:(s + 1) * HID]
                        eng.dma_start(b1c[:, l, s, 0:2], row[0:256].rearrange("(c p) -> p c", p=P)).then_inc(col_ld, 16)
                        eng.dma_start(b1c[0:HID - 256, l, s, 2:3], row[256:HID].rearrange("(p o) -> p o", o=1)).then_inc(col_ld, 16)
            for g in range(2):
                eng.wait_ge(awt_mm, g + 1)
                eng.activation(aT[:, 4 * g:4 * g + 4, :], pT[:, 512 * g:512 * g + 512].rearrange("p (k n) -> p k n", k=4),
                               ACT.Copy).then_inc(awt_ev, 1)
            eng.wait_ge(memset_done, 3)
            with eng.Fori(0, NT) as t:
                eng.wait_ge(xnt_mm, t + 1)
                eng.activation(xnT[:, :, bass.ds(t * P + 1, P)], pM[:, :].rearrange("p (b n) -> p b n", b=NB),
                               ACT.Copy).then_inc(xnt_ev, 1)
            eng.wait_ge(memset_done, 5 + 4 * NB)
            eng.wait_ge(be_done, 2)
            eng.wait_ge(col_ld, 16 * 18)
            act_layer_attn(eng, 0, 0)
            act_retention(eng, 0)
            act_gelu(eng, 0, 0)
            with eng.Fori(1, NT) as t:
                act_layer_attn(eng, 0, t)
                act_retention(eng, t)
                act_gelu(eng, 0, t)
            eng.wait_ge(one_done, 2 * NB + 1)
            act_layer_attn(eng, 1, 0)
            act_block_ffn(eng, 0)
            act_ln_ev(eng, 1, 0)
            act_gelu(eng, 1, 0)
            with eng.Fori(1, NT) as t:
                act_layer_attn(eng, 1, t)
                act_block_ffn(eng, t)
                act_ln_ev(eng, 1, t)
                act_gelu(eng, 1, t)

        def dve_layer_attn(eng, l, t):
            S, ct = LS, NT * l + t
            for k in range(NB + 3):
                if k < NB:
                    n = 4 * ct + k
                    qk = pQK[:, :].rearrange("p (g h d) -> p g h d", g=2, h=H)
                    rot = pQK[:, :].rearrange("p (g h s d) -> p g h s d", g=2, h=H, s=2)[:, :, :, ::-1, :]
                    cos = rope[l][:, t, 0:2, :].unsqueeze(2).broadcast_to([P, 2, H, DH])
                    sin = rope[l][:, t, 2:4, :].rearrange("p g (s d) -> p g s d", s=2).unsqueeze(2).broadcast_to([P, 2, H, 2, 32])
                    eng.wait_ge(S["sq_done"], n + 1)
                    need(eng, S["add_done"], n - 1)
                    need(eng, S["max_ss"], n - 1)
                    need(eng, S["qkn_done"], n - 1)
                    eng.tensor_tensor(m1[:, k % 2, :].rearrange("p (g h d) -> p g h d", g=2, h=H), qk, cos,
                                      ALU.mult).then_inc(S["mul_done"], 1)
                    eng.tensor_tensor(m2[:, k % 2, :].rearrange("p (g h s d) -> p g h s d", g=2, h=H, s=2), rot, sin,
                                      ALU.mult).then_inc(S["mul_done"], 1)
                    eng.tensor_reduce(ss[:, k % 2, :], sq[:, :].rearrange("p (h d) -> p h d", d=DH), AX.X,
                                      ALU.add).then_inc(S["ss_done"], 1)
                if 0 <= k - 2 < NB:
                    b = k - 2
                    n = 4 * ct + b
                    eng.wait_ge(S["s_mm"], n + 1)
                    sc = pS[:, :].rearrange("p (h n) -> p h n", h=H)
                    eng.tensor_reduce(mx[:, :], sc, AX.X, ALU.max).then_inc(S["mx_done"], 1)
                    eng.wait_ge(S["mx_done"], n + 1)
                    eng.tensor_tensor(pr[:, b % 2, :, :], sc, mx[:, :].unsqueeze(2).broadcast_to([P, H, P]),
                                      ALU.subtract).then_inc(S["sub_done"], 1)
                if 0 <= k - 3 < NB:
                    b = k - 3
                    n = 4 * ct + b
                    po = pS[:, :].rearrange("p (g z) -> p g z", g=2)[:, :, 0:4 * (DH + 1)].rearrange(
                        "p g (h d) -> p g h d", h=4)
                    eng.wait_ge(S["o_mm"], n + 1)
                    eng.reciprocal(rec[:, :, :], po[:, :, :, DH]).then_inc(S["rec_done"], 1)
                    eng.wait_ge(S["rec_done"], n + 1)
                    eng.tensor_tensor(o[:, :].rearrange("p (c g d) -> p g c d", g=2, d=DH), po[:, :, :, 0:DH],
                                      rec[:, :, :].unsqueeze(3).broadcast_to([P, 2, 4, DH]), ALU.mult).then_inc(S["o_done"], 1)

        def dve_ln(eng, l, t):
            S, ct = LS, NT * l + t
            src = xnT if l == 0 else x2T
            eng.wait_ge(S["wo_mm"], ct + 1)
            if not isinstance(t, int):
                eng.wait_ge(S["xr_carried"], ct - l)
            eng.tensor_tensor(xr[:, :, 1:1 + P], pM[:, :].rearrange("p (b n) -> p b n", b=NB),
                              src[:, :, bass.ds(t * P + 1, P)], ALU.add).then_inc(S["xr_done"], 1)
            eng.wait_ge(S["ln_mm"], ct + 1)
            for b in range(NB):
                eng.bn_stats(lbst[:, b, :], ln_in(b)).then_inc(S["ln_bst"], 1)
            need_apart(eng, S["ln_bst"], NB * ct + NB)
            for b in range(NB):
                eng.bn_aggr(lmv[:, b, :], lbst[:, b, :]).then_inc(S["ln_st"], 1)

        def dve_ln_apply(eng, l, t):
            S, ct = LS, NT * l + t
            eng.wait_ge(S["ln_rs"], ct + 1)
            for b in range(NB):
                eng.tensor_scalar(hn[:, b, :].rearrange("p (s d) -> p s d", s=2), ln_in(b), lmv[:, b, 0:1], lrs[:, b:b + 1],
                                  ALU.subtract, ALU.mult).then_inc(S["hn_done"], 1)

        def dve_ffn(eng, l, t):
            S, ct = LS, NT * l + t
            for k, (lo, m) in enumerate(CHUNKS):
                pag = pQK if k % 2 == 0 else pT
                eng.wait_ge(S["gelu_done"], NC * ct + k + 1)
                eng.scalar_tensor_tensor(out=hf[0:m, k, :], in0=pag[0:m, 0:512], scalar=b1e[0:m, l, 0, k:k + 1],
                                         in1=gg[0:m, k % 2, :], op0=ALU.add, op1=ALU.mult).then_inc(S["hf_done"], 1)
            eng.wait_ge(S["w2_mm"], ct + 1)
            dst = x2T[:, :, bass.ds(t * P + 1, P)] if l == 0 else fin[:, :, :]
            eng.scalar_tensor_tensor(out=dst, in0=pM[:, :].rearrange("p (b n) -> p b n", b=NB), scalar=c("b2", l),
                                     in1=xr[:, :, 1:1 + P], op0=ALU.add, op1=ALU.add).then_inc(S["x2_done"], 1)

        def dve_retention(eng, t):
            need(eng, A["qkv_mm"], 4 * t)
            for b in range(NB):
                eng.tensor_scalar(xa[:, b, :], xnT[:, b, bass.ds(t * P + 1, P)], gsc[0][:, b:b + 1], gsh[0][:, b:b + 1],
                                  ALU.mult, ALU.add).then_inc(A["xa"], 1)
            for k in range(NB + 2):
                if k < NB:
                    n = 4 * t + k
                    eng.wait_ge(A["rs"], n + 1)
                    eng.wait_ge(A["v"], n + 1)
                    for g, dec in enumerate((decay_q, decay_k)):
                        eng.scalar_tensor_tensor(out=aqk[:, k, g, :], in0=pV[:, g * P:(g + 1) * P],
                                                 scalar=ars[:, k % 2, g:g + 1], in1=dec, op0=ALU.mult,
                                                 op1=ALU.mult).then_inc(A["qk"], 1)
                    eng.wait_ge(A["vx_mm"], n + 1)
                    eng.tensor_tensor(vx[:, k, :, :], pT[:, 0:512].rearrange("p (c n) -> p c n", c=NBL),
                                      value_mask.unsqueeze(1).broadcast_to([P, NBL, P]), ALU.mult).then_inc(A["vx"], 1)
                if k == 1:
                    dve_ln_apply(eng, 0, t)
                if 0 <= k - 1 < NB:
                    b = k - 1
                    n = 4 * t + b
                    eng.wait_ge(A["kv_mm"], n + 1)
                    need(eng, A["state"], n - 1)
                    eng.tensor_tensor(before[:, b % 2, :, :], pQK[:, 512:1024].rearrange("p (c n) -> p c n", c=NBL),
                                      same_head.unsqueeze(1).broadcast_to([P, NBL, P]), ALU.mult).then_inc(A["kvm"], 1)
                    eng.wait_ge(A["kvm"], n + 1)
                    eng.tensor_tensor(before[:, b % 2, :, :], before[:, b % 2, :, :],
                                      state[:, b, :].unsqueeze(1).broadcast_to([P, NBL, P]), ALU.add).then_inc(A["before"], 1)
                if 0 <= k - 2 < NB:
                    b = k - 2
                    n = 4 * t + b
                    eng.wait_ge(A["y_mm"], n + 1)
                    eng.tensor_scalar(state[:, b, :], before[:, b % 2, NBL - 1, :], state_decay, None,
                                      ALU.mult).then_inc(A["state"], 1)
                if 0 <= k - 1 < NB:
                    b = k - 1
                    n = 4 * t + b
                    eng.wait_ge(A["st_mm"], n + 1)
                    eng.tensor_tensor(sm[:, b % 2, :, :, :],
                                      pQK[:, 0:512].rearrange("p (c g n) -> p c g n", c=NBL, g=NG),
                                      causal.unsqueeze(1).unsqueeze(1).broadcast_to([P, NBL, NG, BL]),
                                      ALU.mult).then_inc(A["sm"], 1)
            eng.wait_ge(A["ow_mm"], t + 1)
            eng.scalar_tensor_tensor(out=x1T[:, :, bass.ds(t * P, P)], in0=pM[:, :].rearrange("p (b n) -> p b n", b=NB),
                                     scalar=c("ob"), in1=xnT[:, :, bass.ds(t * P + 1, P)], op0=ALU.add,
                                     op1=ALU.add).then_inc(A["x1"], 1)
            eng.wait_ge(A["x1"], t + 1)
            for b in range(NB):
                eng.bn_stats(cbst[1][:, b, t, :], x1T[:, b, bass.ds(t * P, P)]).then_inc(A["cs"], 1)

        def dve_block_ffn(eng, t):
            need(eng, G["w1_mm"], 2 * t)
            for b in range(NB):
                eng.tensor_scalar(xa[:, b, :], x1T[:, b, bass.ds(t * P, P)], gsc[1][:, b:b + 1], gsh[1][:, b:b + 1],
                                  ALU.mult, ALU.add).then_inc(G["xa"], 1)
            dve_ln_apply(eng, 1, t)
            eng.wait_ge(G["w2_mm"], t + 1)
            eng.scalar_tensor_tensor(out=att[:, :, :], in0=pM[:, :].rearrange("p (b n) -> p b n", b=NB), scalar=c("b2a"),
                                     in1=x1T[:, :, bass.ds(t * P, P)], op0=ALU.add, op1=ALU.add).then_inc(G["att"], 1)

        def dve_final(eng, t):
            eng.wait_ge(LS["x2_done"], NT + t + 1)
            eng.wait_ge(G["att"], t + 1)
            eng.tensor_tensor(fin[:, :, :], fin[:, :, :], att[:, :, :], ALU.add).then_inc(G["fin"], 1)
            eng.wait_ge(G["fin_mm"], t + 1)
            need(eng, G["out"], 16 * t)
            eng.wait_ge(G["xs"], 16 * t + 16)
            eng.tensor_tensor(osb[:, :, :], pS[:, 0:512].rearrange("p (b d) -> p b d", b=NB), xs[:, :, :],
                              ALU.add).then_inc(G["osb"], 1)

        def dve_group_norm(eng, k, gain_col, bias_col):
            g = gn[k]
            for b in range(NB):
                eng.bn_aggr(cmv[:, b, :], cbst[k][:, b, :, :]).then_inc(g["agg"], 1)
            eng.wait_ge(g["agg"], NB)
            steps = [0]

            def then(ins):
                steps[0] += 1
                ins.then_inc(g["dve"], 1)
                eng.wait_ge(g["dve"], steps[0])
            then(eng.tensor_copy(cst2[:, 0, :], cmv[:, :, 0]))
            then(eng.tensor_tensor(cst2[:, 1, :], cmv[:, :, 0], cmv[:, :, 0], ALU.mult))
            then(eng.tensor_tensor(cst2[:, 1, :], cst2[:, 1, :], cmv[:, :, 1], ALU.add))
            eng.wait_ge(g["mm"], 1)
            then(eng.tensor_copy(gst[:, :, :], pV[:, 0:2 * NB].rearrange("p (s b) -> p s b", s=2)))
            then(eng.tensor_tensor(gtmp[:, 1, :], gst[:, 0, :], gst[:, 0, :], ALU.mult))
            then(eng.tensor_tensor(gtmp[:, 0, :], gst[:, 1, :], gtmp[:, 1, :], ALU.subtract))
            eng.tensor_scalar(gtmp[:, 0, :], gtmp[:, 0, :], EPS, None, ALU.add).then_inc(g["var"], 1)
            eng.wait_ge(g["rs"], 1)
            then(eng.tensor_scalar(gsc[k][:, :], grs[:, :], gain_col, None, ALU.mult))
            then(eng.tensor_tensor(gtmp[:, 1, :], gst[:, 0, :], gsc[k][:, :], ALU.mult))
            eng.tensor_scalar(gsh[k][:, :], gtmp[:, 1, :], -1.0, bias_col, ALU.mult, ALU.add).then_inc(g["done"], 1)
            eng.wait_ge(g["done"], 1)

        @block.vector
        def _(eng):
            for b in range(NB):
                eng.wait_ge(x_ld[b], 16)
            with eng.Fori(0, NT) as t:
                for b in range(NB):
                    eng.bn_stats(bst[:, b, :], x[:, b, t, :]).then_inc(xst_done, 1)
                need_apart(eng, xst_done, NB * t + NB)
                for b in range(NB):
                    eng.bn_aggr(lmv[:, b, :], bst[:, b, :]).then_inc(agg_done, 1)
                eng.wait_ge(agg_done, NB * t + NB)
                eng.tensor_copy(mv[:, t, :, :], lmv[:, :, :]).then_inc(st_done, 1)
            eng.wait_ge(cst_ld, 32)
            eng.tensor_copy(mask16[:, :, :], mask32[:, :, :]).then_inc(mask_done, 1)
            eng.wait_ge(rstd_done, 1)

            def normalize(half):
                for u in range(2):
                    t = 2 * half + u
                    need(eng, xnt_mm, 2 * half)
                    for b in range(NB):
                        eng.tensor_scalar(xn[:, u, b, :], x[:, b, t, :], mv[:, t, b, 0:1], rstd[:, t, b:b + 1],
                                          ALU.subtract, ALU.mult).then_inc(xn_done, 1)
            normalize(0)
            with eng.Fori(1, NT // 2) as half:
                normalize(half)
            with eng.Fori(0, NT) as t:
                eng.wait_ge(xnt_ev, t + 1)
                for b in range(NB):
                    eng.bn_stats(cbst[0][:, b, t, :], xnT[:, b, bass.ds(t * P + 1, P)]).then_inc(cs_done, 1)
            eng.wait_ge(cs_done, NB * NT)
            eng.wait_ge(w_ld, 16 * 5 * DEPTH)
            eng.wait_ge(col_ld, 16 * (10 + 8))
            eng.wait_ge(be_mm, 1)
            for l in range(DEPTH):
                eng.tensor_scalar(w1[:, l, :], w1[:, l, :], c("lg", l), None, ALU.mult).then_inc(w1g_done, 1)
            pb = pV[:, 64:64 + 2 * DEPTH * NC].rearrange("p (l s k) -> p l s k", l=DEPTH, s=2)
            last = HID - 256
            eng.tensor_tensor(b1e[:, :, :, 0:2], pb[:, :, :, 0:2], b1c[:, :, :, 0:2], ALU.add).then_inc(be_done, 1)
            eng.tensor_tensor(b1e[0:last, :, :, 2], pb[0:last, :, :, 2], b1c[0:last, :, :, 2], ALU.add).then_inc(be_done, 1)
            dve_group_norm(eng, 0, c("ng"), c("nb"))
            eng.wait_ge(rope_done, 6 * DEPTH)
            dve_layer_attn(eng, 0, 0)
            dve_ln(eng, 0, 0)
            dve_retention(eng, 0)
            dve_ffn(eng, 0, 0)
            with eng.Fori(1, NT) as t:
                dve_layer_attn(eng, 0, t)
                dve_ln(eng, 0, t)
                dve_retention(eng, t)
                dve_ffn(eng, 0, t)
            eng.wait_ge(A["cs"], NB * NT)
            dve_group_norm(eng, 1, c("fg"), c("fb"))
            dve_layer_attn(eng, 1, 0)
            dve_ln(eng, 1, 0)
            dve_block_ffn(eng, 0)
            dve_ffn(eng, 1, 0)
            dve_final(eng, 0)
            with eng.Fori(1, NT) as t:
                dve_layer_attn(eng, 1, t)
                dve_ln(eng, 1, t)
                dve_block_ffn(eng, t)
                dve_ffn(eng, 1, t)
                dve_final(eng, t)

        def pe_layer_attn(eng, l, t):
            S, ct = LS, NT * l + t
            first = isinstance(t, int)
            eng.wait_ge(S["h_ready"], 2 * ct + 2)
            for k in range(NB + 4):
                if 0 <= k - 4 < NB:
                    b = k - 4
                    n = 4 * ct + b
                    eng.wait_ge(S["o_done"], n + 1)
                    need(eng, S["ot_ev"], n)
                    for j in range(4):
                        mm = eng.transpose(pM[:, j * P:(j + 1) * P], o[:, j * P:(j + 1) * P], ident)
                    mm.then_inc(S["ot_mm"], 1)
                if 0 <= k - 2 < NB:
                    b = k - 2
                    n = 4 * ct + b
                    eng.wait_ge(S["qkn_done"], n + 1)
                    need(eng, S["t_ev"], 2 * n)
                    need(eng, S["pt_ev"], 4 * ct + max(b - 1, 0))
                    for j in range(8):
                        mm = eng.transpose(pT[:, j * P:(j + 1) * P], qkn[:, b % 2, j * P:(j + 1) * P], ident)
                    mm.then_inc(S["t_mm"], 1)
                if k < NB:
                    n = 4 * ct + k
                    need(eng, S["mul_done"], 2 * n)
                    for g in range(2):
                        mm = eng.matmul(pQK[:, g * 512:(g + 1) * 512], hT[:, k, :], wqkv[:, l, g * 512:(g + 1) * 512],
                                        start=True, stop=True)
                    mm.then_inc(S["qk_mm"], 1)
                if 0 <= k - 2 < NB:
                    b = k - 2
                    n = 4 * ct + b
                    eng.wait_ge(S["t_ev"], 2 * n + 2)
                    need(eng, S["sub_done"], n)
                    need(eng, S["o_done"], 4 * ct + max(b - 1, 0))
                    mask = mask16[:, 0 if first else 1, :].unsqueeze(1).broadcast_to([P, 4, P])
                    for g in range(2):
                        eng.matmul(pS[:, g * 512:(g + 1) * 512], mask16[:, 2, :], mask, start=True, stop=False,
                                   skip_group_check=True)
                    kk = kT[b]
                    for j in range(4):
                        for g in range(2):
                            r = slice(64 * g, 64 * g + 64)
                            at = g * 512 + j * P
                            for w in range(2):
                                if w == 0:
                                    for s, lo in enumerate((0, P)):
                                        mm = eng.matmul(pS[0:64, at + 64 * s:at + 64 * s + 64], qT[r, j, 0:64],
                                                        kk[r, j, lo:lo + 64], start=False, stop=True, skip_group_check=True)
                                else:
                                    mm = eng.matmul(pS[64:P, at:at + P], qT[r, j, 64:P], kk[r, j, 0:P],
                                                    start=False, stop=True, skip_group_check=True)
                    mm.then_inc(S["s_mm"], 1)
                if 0 <= k - 3 < NB:
                    b = k - 3
                    n = 4 * ct + b
                    eng.wait_ge(S["exp_done"], n + 1)
                    need(eng, S["pt_ev"], n)
                    eng.wait_ge(S["t_ev"], 2 * (4 * ct + min(b + 2, 4)))
                    for j in range(8):
                        mm = eng.transpose(pT[:, j * P:(j + 1) * P], pr[:, b % 2, j, :], ident)
                    mm.then_inc(S["pt_mm"], 1)
                if k < NB:
                    n = 4 * ct + k
                    need(eng, S["v_ev"], n)
                    eng.matmul(pV[:, :], hT[:, k, :], wqkv[:, l, 1024:1536], start=True, stop=True).then_inc(S["v_mm"], 1)
                if 0 <= k - 3 < NB:
                    b = k - 3
                    n = 4 * ct + b
                    eng.wait_ge(S["pt_ev"], n + 1)
                    eng.wait_ge(S["vmix_done"], n + 1)
                    need(eng, S["sub_done"], 4 * ct + min(b + 2, 4))
                    need(eng, S["o_done"], n)
                    for i in range(H):
                        g, j = i // 4, i % 4
                        for w in range(2):
                            at = g * 512 + j * (DH + 1)
                            mm = eng.matmul(pS[64 * w:64 * w + 64, at:at + DH + 1], prT[:, i, 64 * w:64 * w + 64],
                                            (vown if w else vmix)[b][:, 2 * j + g, :], start=(j == 0), stop=True,
                                            skip_group_check=True)
                    mm.then_inc(S["o_mm"], 1)

        def pe_ln(eng, l, t):
            S, ct = LS, NT * l + t
            eng.wait_ge(S["ot_ev"], 4 * ct + 4)
            for j in range(4):
                mm = eng.matmul(pM[:, :], wo[:, l, j, :], oT[:, j, :, :], start=(j == 0), stop=(j == 3))
            mm.then_inc(S["wo_mm"], 1)
            need_apart(eng, S["xr_done"], ct + 1)
            for b in range(NB):
                eng.transpose(pS[:, b * 64:b * 64 + 64], xr[0:64, b, 1:1 + P], ident[0:64, 0:64])
                mm = eng.transpose(pS[:, 512 + b * 64:512 + b * 64 + 64], xr[64:P, b, 0:P], ident[64:P, 64:P])
            mm.then_inc(S["ln_mm"], 1)

        def pe_ln_back(eng, l, t):
            S, ct = LS, NT * l + t
            eng.wait_ge(S["hn_done"], 4 * ct + 4)
            for b in range(NB):
                mm = eng.transpose(pS[:, 512 + b * P:512 + (b + 1) * P], hn[:, b, :], ident)
            mm.then_inc(S["hnt_mm"], 1)

        def pe_ffn(eng, l, t):
            S, ct = LS, NT * l + t
            eng.wait_ge(S["hnt_ev"], ct + 1)
            if l == 0:
                eng.wait_ge(A["state"], 4 * ct + 4)
            for k, (lo, m) in enumerate(CHUNKS):
                pag = pQK if k % 2 == 0 else pT
                if k == 2:
                    eng.wait_ge(S["hf_done"], NC * ct + 1)
                for s in range(2):
                    mm = eng.matmul(pag[0:m, s * 512:(s + 1) * 512], w1[:, l, s * HID + lo:s * HID + lo + m], hnT[:, :],
                                    start=True, stop=True)
                mm.then_inc(S["ag_mm"], 1)
            if l == 0:
                eng.wait_ge(A["x1"], ct + 1)
            else:
                eng.wait_ge(G["att"], t + 1)
            for k, (lo, m) in enumerate(CHUNKS):
                eng.wait_ge(S["hf_done"], NC * ct + k + 1)
                mm = eng.matmul(pM[:, :], w2[0:m, l, k, :], hf[0:m, k, :], start=(k == 0), stop=(k == NC - 1))
            mm.then_inc(S["w2_mm"], 1)

        def pe_retention(eng, t):
            eng.wait_ge(A["xa"], 4 * t + 4)
            eng.wait_ge(LS["v_ev"], 4 * t + 4)
            for k in range(NB + 2):
                if 0 <= k - 1 < NB:
                    b = k - 1
                    n = 4 * t + b
                    eng.wait_ge(A["qk"], 2 * n + 2)
                    need(eng, A["t_ev"], n)
                    for g in range(2):
                        mm = eng.transpose(pM[:, g * P:(g + 1) * P], aqk[:, b, g, :], ident)
                    mm.then_inc(A["t_mm"], 1)
                if k < NB:
                    n = 4 * t + k
                    need(eng, A["qk"], 2 * n)
                    eng.matmul(pV[:, 0:3 * P], xa[:, k, :], aT[:, 0:3, :], start=True, stop=True).then_inc(A["qkv_mm"], 1)
                    eng.wait_ge(A["xa4"], n + 1)
                    need(eng, A["vx"], n)
                    for c_ in range(NBL):
                        mm = eng.matmul(pT[:, c_ * P:(c_ + 1) * P],
                                        xa4[:, k % 2, c_, :, :],
                                        aT[:, 2, :], start=True, stop=True)
                    mm.then_inc(A["vx_mm"], 1)
                if k == 2:
                    pe_ln_back(eng, 0, t)
                if 0 <= k - 1 < NB:
                    b = k - 1
                    n = 4 * t + b
                    need(eng, A["kvm"], n)
                    for c_ in range(NBL):
                        rows = slice(0, (c_ + 1) * BL)
                        mm = eng.matmul(pQK[:, 512 + c_ * P:512 + (c_ + 1) * P], aqk[rows, b, 1, :], av[rows, b, :],
                                        start=True, stop=True)
                    mm.then_inc(A["kv_mm"], 1)
                    eng.wait_ge(A["kx"], n + 1)
                    eng.wait_ge(A["qx"], n + 1)
                    need(eng, A["sm"], n)
                    for c_ in range(NBL):
                        mm = eng.matmul(pQK[:, c_ * P:(c_ + 1) * P], kx[:, b % 2, c_, :, :], qx[:, b % 2, c_, :, :],
                                        start=True, stop=True)
                    mm.then_inc(A["st_mm"], 1)
                if 0 <= k - 2 < NB:
                    b = k - 2
                    n = 4 * t + b
                    eng.wait_ge(A["sm"], n + 1)
                    eng.wait_ge(A["before"], n + 1)
                    need(eng, A["yt"], NG * n)
                    for c_ in range(NBL):
                        at = slice(512 + c_ * P, 512 + (c_ + 1) * P)
                        eng.matmul(pT[:, at], vx[:, b, c_, :], sm[:, b % 2, c_, :, :], start=True, stop=False)
                        mm = eng.matmul(pT[:, at], before[:, b % 2, c_ - 1, :] if c_ else state[:, b, :],
                                        qx[:, b % 2, c_, :, :], start=False, stop=True)
                    mm.then_inc(A["y_mm"], 1)
            eng.wait_ge(A["yt"], NG * (4 * t + 4))
            eng.matmul(pM[:, :], aT[:, 3, :], ayT[:, :], start=True, stop=True).then_inc(A["ow_mm"], 1)

        def pe_block_ffn(eng, t):
            eng.wait_ge(G["xa"], 4 * t + 4)
            for j in range(2):
                eng.matmul(pQK[:, j * 512:(j + 1) * 512], aT[:, 4 + j, :], xa[:, :, :], start=True, stop=True).then_inc(G["w1_mm"], 1)
            pe_ln_back(eng, 1, t)
            eng.wait_ge(G["silu"], 2 * t + 2)
            for j in range(2):
                mm = eng.matmul(pM[:, :], aT[:, 6 + j, :], afh[:, j, :], start=(j == 0), stop=(j == 1))
            mm.then_inc(G["w2_mm"], 1)

        def pe_final(eng, t):
            eng.wait_ge(G["fin"], t + 1)
            for b in range(NB):
                mm = eng.transpose(pS[:, b * P:(b + 1) * P], fin[:, b, :], ident)
            mm.then_inc(G["fin_mm"], 1)

        def pe_group_norm(eng, k):
            eng.wait_ge(gn[k]["dve"], 3)
            eng.matmul(pV[:, 0:2 * NB], group_avg, cst2[:, :, :], start=True, stop=True).then_inc(gn[k]["mm"], 1)

        @block.tensor
        def _(eng):
            eng.wait_ge(cst_ld, 32)
            eng.wait_ge(aw_ld, 16 * 6)
            for g in range(2):
                for j in range(4):
                    mm = eng.transpose(pT[:, g * 512 + j * P:g * 512 + (j + 1) * P], araw[:, 4 * g + j, :], ident)
                mm.then_inc(awt_mm, 1)

            def transpose_normalized(half):
                for u in range(2):
                    t = 2 * half + u
                    eng.wait_ge(xn_done, 4 * t + 4)
                    need(eng, xnt_ev, t)
                    for b in range(NB):
                        mm = eng.transpose(pM[:, b * P:(b + 1) * P], xn[:, u, b, :], ident)
                    mm.then_inc(xnt_mm, 1)
            transpose_normalized(0)
            with eng.Fori(1, NT // 2) as half:
                transpose_normalized(half)
            eng.wait_ge(w_ld, 16 * 5 * DEPTH)
            eng.wait_ge(col_ld, 16 * (10 + 8))
            for l in range(DEPTH):
                for s in range(2):
                    for k, (lo, m) in enumerate(CHUNKS):
                        at = 64 + (l * 2 + s) * NC + k
                        mm = eng.matmul(pV[0:m, at:at + 1], w1[:, l, s * HID + lo:s * HID + lo + m], c("lb", l),
                                        start=True, stop=True)
            mm.then_inc(be_mm, 1)
            eng.wait_ge(be_done, 2)
            pe_group_norm(eng, 0)
            eng.wait_ge(gn[0]["done"], 1)
            eng.wait_ge(w1g_done, DEPTH)
            eng.wait_ge(awt_ev, 2)
            eng.wait_ge(xnt_ev, NT)
            eng.wait_ge(mask_done, 1)
            eng.wait_ge(memset_done, 5 + 4 * NB)
            pe_layer_attn(eng, 0, 0)
            pe_ln(eng, 0, 0)
            pe_retention(eng, 0)
            pe_ffn(eng, 0, 0)
            with eng.Fori(1, NT) as t:
                eng.wait_ge(LS["x2_done"], t)
                pe_layer_attn(eng, 0, t)
                pe_ln(eng, 0, t)
                pe_retention(eng, t)
                pe_ffn(eng, 0, t)
            eng.wait_ge(LS["x2_done"], NT)
            pe_group_norm(eng, 1)
            eng.wait_ge(gn[1]["done"], 1)
            pe_layer_attn(eng, 1, 0)
            pe_ln(eng, 1, 0)
            pe_block_ffn(eng, 0)
            pe_ffn(eng, 1, 0)
            pe_final(eng, 0)
            with eng.Fori(1, NT) as t:
                eng.wait_ge(G["osb"], t)
                pe_layer_attn(eng, 1, t)
                pe_ln(eng, 1, t)
                pe_block_ffn(eng, t)
                pe_ffn(eng, 1, t)
                pe_final(eng, t)


_INS = ["L0_attn_x", "L0_attn_norm_g", "L0_attn_norm_b", "L0_attn_qw", "L0_attn_kw", "L0_attn_vw", "L0_attn_ow",
        "L0_attn_ob", "L0_attn_ffn_norm_g", "L0_attn_ffn_norm_b", "L0_attn_w1", "L0_attn_b1", "L0_attn_w2",
        "L0_attn_b2", "L0_ffn_wqkv", "L0_ffn_q_scale", "L0_ffn_k_scale", "L0_ffn_wo", "L0_ffn_ln_g", "L0_ffn_ln_b",
        "L0_ffn_w1", "L0_ffn_b1", "L0_ffn_w2", "L0_ffn_b2"]


def kernel(**inputs):
    import concourse.bacc as _bacc
    from concourse.bass_utils import run_bass_kernel_spmd as _run

    nc = _bacc.Bacc("TRN2", target_bir_lowering=False, num_devices=1)
    cst, tab, mask = constants()
    arrays = {"k_cst": cst, "k_tab": tab, "k_mask": mask}
    arrays.update({n: np.ascontiguousarray(inputs[n]) for n in _INS})
    aps = {n: nc.dram_tensor("in_" + n, v.shape, mybir.dt.from_np(v.dtype), kind="ExternalInput").ap()
           for n, v in arrays.items()}
    out = nc.dram_tensor("out_0", (NB, T, D), F32, kind="ExternalOutput").ap()
    program(nc, aps, out)
    r = _run(nc, [{"in_" + n: v for n, v in arrays.items()}], core_ids=[0])
    return r.results[0]["out_0"]
```

```python
from contextlib import ExitStack

import concourse.bass as bass
import numpy as np
from concourse import mybir

F32 = mybir.dt.float32
BF16 = mybir.dt.bfloat16
ALU = mybir.AluOpType
ACT = mybir.ActivationFunctionType
AX = mybir.AxisListType

P = 128
NB = 4
T = 1024
NT = T // P
D = 128
RH, RD = 16, 8
BL = 32
NBL = P // BL
NG = 4
DEPTH = 2
H, DH = 8, 64
INNER = H * DH
WIN = 64
HID = int(D * 4 * 2 / 3)
CHUNKS = [(0, 128), (128, 128), (256, HID - 256)]
NC = len(CHUNKS)
EPS = 1e-5
MASKED = -1e30

C_ID, C_GRP, C_GQ, C_GK, C_BD, C_VM, C_CAUSAL = 0, 128, 256, 384, 512, 640, 768
C_HM = C_CAUSAL + BL
C_GM, C_SD = C_HM + NG, C_HM + 2 * NG
C_END = C_SD + 1


def constants():
    f = np.float32
    cst = np.zeros((P, C_END), f)
    i = np.arange(P)
    cst[:, C_ID:C_ID + P] = np.eye(P)
    cst[:, C_GRP:C_GRP + P] = (i[:, None] // RD == i[None, :] // RD) / RD
    cst[:, C_CAUSAL:C_CAUSAL + BL] = i[:, None] % BL <= i[None, :BL]
    lin = np.linspace(np.log(1.0 / 32.0), np.log(1.0 / 512.0), RH).astype(f)
    gam = (f(1.0) - np.exp(lin)).astype(np.float64)
    head = i // RD
    cst[:, C_GQ:C_GQ + P] = gam[head][None, :] ** i[:, None] / np.sqrt(RD)
    cst[:, C_GK:C_GK + P] = gam[head][None, :] ** (-i[:, None].astype(np.float64))
    cst[:, C_BD:C_BD + P] = head[:, None] == head[None, :]
    cst[:, C_VM:C_VM + P] = i[:, None] // BL == head[None, :] % NG
    cst[:, C_HM:C_HM + NG] = head[:, None] % NG == np.arange(NG)[None, :]
    cst[:, C_GM:C_GM + NG] = head[:, None] // NG == np.arange(NG)[None, :]
    cst[:, C_SD] = gam[head] ** P
    half = np.arange(0, DH, 2, dtype=f)
    inv = (f(1.0) / np.power(f(10000.0), half / f(DH))).astype(f)
    t = np.arange(T, dtype=f)
    fr = t[:, None] * inv[None, :]
    fr = np.concatenate([fr, fr], -1)
    base = ((half + f(0.4 * DH)) / f(1.4 * DH)).astype(f)
    power = (t - f(T // 2)) / f(WIN // 2)
    sc = np.power(base[None, :], power[:, None]).astype(f)
    sc = np.concatenate([sc, sc], -1)
    sign = np.where(np.arange(DH) < DH // 2, -1.0, 1.0).astype(f)
    cos, sin = np.cos(fr), np.sin(fr) * sign
    tab = np.stack([cos * sc * f(8), cos / sc, sin * sc * f(8), sin / sc], 1).astype(f)
    tab = tab.reshape(NT, P, 4, DH).transpose(1, 0, 2, 3)
    own = (i[:WIN, None] >= i[None, :WIN])
    before = (i[:WIN, None] <= i[None, :WIN])
    even = np.concatenate([own, before], 1)
    odd = np.concatenate([before, own], 1)
    m = np.concatenate([even, odd], 0)
    first = m.copy()
    first[:WIN, WIN:] = False
    mask = np.where(np.stack([first, m], 1), 0.0, MASKED).astype(f)
    mask = np.concatenate([mask, np.eye(P, dtype=f)[:, None, :]], 1)
    return cst, np.ascontiguousarray(tab), np.ascontiguousarray(mask)


def need(eng, sem, value):
    if isinstance(value, int) and value <= 0:
        return
    eng.wait_ge(sem, value)


def program(nc, a, out):
    with ExitStack() as ctx:
        def sb(name, shape, dt=F32):
            return ctx.enter_context(nc.sbuf_tensor(name, shape, dt))

        def sem(name):
            return ctx.enter_context(nc.semaphore(name))

        cst = sb("cst", [P, C_END])
        ident = cst[:, C_ID:C_ID + P]
        group_avg = cst[:, C_GRP:C_GRP + P]
        causal = cst[:, C_CAUSAL:C_CAUSAL + BL]
        decay_q = cst[:, C_GQ:C_GQ + P]
        decay_k = cst[:, C_GK:C_GK + P]
        same_head = cst[:, C_BD:C_BD + P]
        value_mask = cst[:, C_VM:C_VM + P]
        place_mask = cst[:, C_HM:C_HM + NG]
        group_mask = cst[:, C_GM:C_GM + NG]
        state_decay = cst[:, C_SD:C_SD + 1]
        hidden = sb("hidden", [P, NC * NB * P])
        mask32 = hidden[:, 0:3 * P].rearrange("p (s n) -> p s n", s=3)
        mask16 = sb("mask16", [P, 3, P], BF16)
        tab = sb("tab", [P, NT, 4, DH])
        gain = hidden[:, 3 * P:3 * P + DEPTH * 2 * DH].rearrange("p (l g d) -> p l g d", l=DEPTH, g=2)
        rope = [sb("rope0", [P, NT, 4, DH]), tab]
        half_neg = sb("half_neg", [P, NB * NT])
        wqkv = sb("wqkv", [P, DEPTH, 3 * INNER])
        wo = sb("wo", [P, DEPTH, 4, D])
        w1 = sb("w1", [P, DEPTH, 2 * HID])
        w2 = sb("w2", [P, DEPTH, NC, D])
        b1c = sb("b1c", [P, DEPTH, 2, NC])
        b1e = sb("b1e", [P, DEPTH, 2, NC])
        col = sb("col", [P, 16])
        COLS = {"ng": 0, "nb": 1, "ob": 2, "fg": 3, "fb": 4, "b1a": 5, "b2a": 7,
                "lg": 8, "lb": 10, "b2": 12}

        def c(name, k=0):
            return col[:, COLS[name] + k:COLS[name] + k + 1]

        aT = sb("aT", [P, 8, P])

        x = sb("x", [P, NB, NT, D])
        x1T = x[:, :, :, :].rearrange("p b t d -> p b (t d)")
        xnT = sb("xnT", [P, NB, 1 + T])
        x2T = sb("x2T", [P, NB, 1 + T])

        bst = sb("bst", [P, NB, 6])
        mv = sb("mv", [P, NT, NB, 2])
        vpe = sb("vpe", [P, NT, NB])
        rstd = sb("rstd", [P, NT, NB])
        cbst = [sb(f"cbst{k}", [P, NB, NT, 6]) for k in range(2)]
        cmv = sb("cmv", [P, NB, 2])
        cst2 = sb("cst2", [P, 2, NB])
        gst = sb("gst", [P, 2, NB])
        gtmp = sb("gtmp", [P, 2, NB])
        grs = sb("grs", [P, NB])
        gsc = [sb(f"gsc{k}", [P, NB]) for k in range(2)]
        gsh = [sb(f"gsh{k}", [P, NB]) for k in range(2)]

        hT = sb("hT", [P, NB, P])
        sq = sb("sq", [P, 2 * INNER])
        ss = sb("ss", [P, 2, 2 * H])
        rn = sb("rn", [P, 2, 2 * H])
        m1 = sb("m1", [P, 2, 2 * INNER])
        m2 = sb("m2", [P, 2, 2 * INNER])
        qkn = sb("qkn", [P, 2, 2 * INNER])
        xn = m1[:, :, 0:NB * D].rearrange("p u (b d) -> p u b d", b=NB)
        qT = sb("qT", [P, 4, P])
        kT = [sb(f"kT{b}", [P, 4, P + WIN]) for b in range(NB)]
        vown = [sb(f"vown{b}", [P, H, DH + 1]) for b in range(NB)]
        vmix = [sb(f"vmix{b}", [P, H, DH + 1]) for b in range(NB)]
        mx = sb("mx", [P, H])
        pr = sb("pr", [P, 2, H, P])
        prT = sb("prT", [P, H, P])
        rec = sb("rec", [P, 2, 4])
        o = sb("o", [P, INNER])
        oT = sb("oT", [P, 4, P])
        xr = sb("xr", [P, NB, 1 + P])
        lmv = sb("lmv", [P, NB, 2])
        lbst = sb("lbst", [P, NB, 6])
        lvar = sb("lvar", [P, NB])
        lrs = sb("lrs", [P, NB])
        hn = sb("hn", [P, NB, D])
        hs = hn
        hnT = sb("hnT", [P, NB * P])
        gg = sb("gg", [P, 2, NB * P])
        hf = hidden[:, :].rearrange("p (k n) -> p k n", k=NC)
        xa = sb("xa", [P, NB, P])
        xa4 = sb("xa4", [P, 2, NBL, NG, BL])
        asq = sb("asq", [P, P])
        ass = sb("ass", [P, 2, 2])
        ars = sb("ars", [P, 2, 2])
        aqk = sb("aqk", [P, 2, 2, P])
        av = sb("av", [P, 2, P])
        aqkT = sb("aqkT", [P, 2, 2, P])
        araw = pr[:, :, :, :].rearrange("p u h n -> p (u h) n")[:, 0:8, :]
        state = sb("state", [P, NB, P])
        vx = m2[:, 0, :].rearrange("p (u c n) -> p u c n", u=2, c=NBL)
        kx = sq[:, :].rearrange("p (u c j n) -> p u c j n", u=2, c=NBL, j=NG)
        qx = prT[:, :, :].rearrange("p h n -> p (h n)").rearrange("p (u c g n) -> p u c g n", u=2, c=NBL, g=NG)
        sm = m1[:, 0, :].rearrange("p (u c g n) -> p u c g n", u=2, c=NBL, g=NG)
        before = hidden[:, 0:2 * NBL * P].rearrange("p (u c n) -> p u c n", u=2, c=NBL)
        ayT = gg[:, 0, :]
        afh = xa4[:, :, :, :, :].rearrange("p s c g n -> p s (c g n)")
        att = state
        fin = aqk[:, :, :, :].rearrange("p u g n -> p (u g) n")
        xs = sb("xs", [P, NB, D])
        osb = aqkT[:, :, :, :].rearrange("p u g n -> p (u g) n")

        pQK = ctx.enter_context(nc.psum_tensor("pQK", [P, 1024], F32))
        pV = ctx.enter_context(nc.psum_tensor("pV", [P, 512], F32))
        pT = ctx.enter_context(nc.psum_tensor("pT", [P, 1024], F32))
        pS = ctx.enter_context(nc.psum_tensor("pS", [P, 1024], F32))
        pM = ctx.enter_context(nc.psum_tensor("pM", [P, 512], F32))

        ffn_banks = (pT, pS, pT)
        y_banks = (pT, pS)

        x_ld = [sem(f"x_ld{b}") for b in range(NB)]
        cst_ld, tab_ld, aw_ld, w_ld, gain_ld, col_ld = (
            sem(n) for n in ("cst_ld", "tab_ld", "aw_ld", "w_ld", "gain_ld", "col_ld"))
        memset_done, mask_done = sem("memset_done"), sem("mask_done")
        xst_done, agg_done, st_done, var_done, rstd_done, xn_done, xnt_mm, xnt_ev, cs_done = (
            sem(n) for n in ("xst_done", "agg_done", "st_done", "var_done", "rstd_done", "xn_done", "xnt_mm", "xnt_ev", "cs_done"))
        awt_mm, awt_ev, be_mm, be_done, w1g_done, rope_done = (
            sem(n) for n in ("awt_mm", "awt_ev", "be_mm", "be_done", "w1g_done", "rope_done"))
        gn = [{n: sem(f"gn{k}_{n}") for n in ("agg", "dve", "mm", "var", "rs", "done")} for k in range(2)]
        LS = {n: sem(n) for n in (
            "carried", "v_kept", "h_ready", "qk_mm", "v_mm", "sq_done", "ss_done", "mul_done", "max_ss", "rn_done", "add_done",
            "qkn_done", "t_mm", "t_ev", "v_ev", "s_mm", "mx_done", "sub_done", "exp_done",
            "pt_mm", "pt_ev", "o_mm", "rec_done", "o_done", "ot_mm", "ot_ev", "wo_mm", "xr_carried", "xr_done", "hs",
            "ln_mm", "ln_bst", "ln_st", "ln_eps", "ln_rs", "hn_done", "hnt_mm", "hnt_ev", "ag_mm", "gelu_done",
            "hf_done", "w2_mm", "x2_done")}
        A = {n: sem(f"a_{n}") for n in (
            "xa", "xa4", "qkv_mm", "sqq", "v", "floor", "rs", "qk", "t_mm", "t_ev", "vx_mm", "vx", "kx", "qx", "st_mm", "sm",
            "kv_mm", "kvm", "before", "y_mm", "yt", "state", "ow_mm", "x1", "cs")}
        G = {n: sem(f"g_{n}") for n in ("xa", "w1_mm", "silu", "w2_mm", "att", "fin", "fin_mm", "xs", "osb", "out")}

        x_steps = a["L0_attn_x"].rearrange("b (t p) d -> t p b d", p=P)
        out_steps = out.rearrange("b (t p) d -> t p b d", p=P)
        block = ctx.enter_context(nc.Block())

        def need_apart(eng, sem, value):
            if isinstance(value, int):
                return need(eng, sem, value)
            register = eng.to_reg(value)
            eng.wait_ge(cst_ld, 32)
            eng.wait_ge(sem, register)

        def step_count(step):
            return NT * step[0] + step[1]

        def count(step, b):
            return NB * step_count(step) + b

        def is_first(step):
            return isinstance(step[1], int) and step[1] == 0

        def is_start(step):
            return step[0] == 0 and is_first(step)

        def at(new, old, k):
            step = new if k >= 0 else old
            return (step, k % NB, count(step, k % NB)) if step else None

        def run_bodies(eng, body, between):
            body((0, 0), None, None)
            body((0, 1), (0, 0), None)
            with eng.Fori(2, NT) as t:
                body((0, t), (0, t - 1), (0, t - 2))
            body((1, 0), (0, NT - 1), (0, NT - 2))
            between()
            body((1, 1), (1, 0), (0, NT - 1))
            with eng.Fori(2, NT) as t:
                body((1, t), (1, t - 1), (1, t - 2))
            body(None, (1, NT - 1), (1, NT - 2))
            body(None, None, (1, NT - 1))

        @block.sync
        def _(sp):
            for b in range(NB):
                sp.dma_start(x[:, b, :, :], a["L0_attn_x"][b].rearrange("(t p) d -> p t d", p=P)).then_inc(x_ld[b], 16)
            sp.dma_start(tab[:, :, :, :], a["k_tab"]).then_inc(tab_ld, 16)
            for l in range(DEPTH):
                sp.dma_start(wqkv[:, l, :], a["L0_ffn_wqkv"][l]).then_inc(w_ld, 16)
                sp.dma_start(wo[:, l, :, :], a["L0_ffn_wo"][l].rearrange("(c p) d -> p c d", p=P)).then_inc(w_ld, 16)
                sp.dma_start(w1[:, l, :], a["L0_ffn_w1"][l]).then_inc(w_ld, 16)
                sp.dma_start(w2[:, l, 0:2, :], a["L0_ffn_w2"][l, 0:2 * P, :].rearrange("(c p) d -> p c d", p=P)).then_inc(w_ld, 16)
                sp.dma_start(w2[0:CHUNKS[2][1], l, 2, :], a["L0_ffn_w2"][l, 2 * P:HID, :]).then_inc(w_ld, 16)
            sp.dma_start(xs[:, :, :], x_steps[0]).then_inc(G["xs"], 16)
            sp.wait_ge(G["osb"], 1)
            sp.dma_start(out_steps[0], osb[:, :, :]).then_inc(G["out"], 16)
            with sp.Fori(1, NT) as t:
                sp.wait_ge(G["out"], 16 * t)
                sp.dma_start(xs[:, :, :], x_steps[t]).then_inc(G["xs"], 16)
                sp.wait_ge(G["osb"], t + 1)
                sp.dma_start(out_steps[t], osb[:, :, :]).then_inc(G["out"], 16)
            sp.wait_ge(G["out"], 16 * NT)

        def pool_slot(eng, new, old, k):
            S = LS
            if old and k == 0 and not is_start(old):
                need_apart(eng, S["hs"], 2 * step_count(old))
                if is_first(old):
                    eng.memset(xr[:, :, 0:1], 0.0).then_inc(S["xr_carried"], 1)
                else:
                    eng.tensor_copy(xr[:, :, 0:1], xr[:, :, P:P + 1]).then_inc(S["xr_carried"], 1)
            if new:
                n = count(new, k)
                if k == NB - 1 and new[0] == 0:
                    pool_retention_norm(eng, new[1], 0)
                need_apart(eng, S["ss_done"], n + 1)
                eng.tensor_scalar(rn[:, k % 2, :], ss[:, k % 2, :], 1e-24, None, ALU.max).then_inc(S["max_ss"], 1)
                eng.wait_ge(S["max_ss"], n + 1)
                eng.tensor_tensor(rn[:, k % 2, :], rn[:, k % 2, :], half_neg[:, 0:2 * H], ALU.pow).then_inc(S["rn_done"], 1)
            if old and k == NB - 1:
                ct = step_count(old)
                need_apart(eng, S["ln_st"], NB * ct + NB)
                eng.tensor_scalar(lvar[:, :], lmv[:, :, 1], EPS, None, ALU.add).then_inc(S["ln_eps"], 1)
                eng.wait_ge(S["ln_eps"], ct + 1)
                eng.tensor_tensor(lrs[:, :], lvar[:, :], half_neg[:, 0:NB], ALU.pow).then_inc(S["ln_rs"], 1)
            if new:
                if not (k == NB - 1 and new[0] == 0):
                    pool_add(eng, n, k)
                    pool_scale(eng, n, k)

        def pool_add(eng, n, k):
            S = LS
            eng.wait_ge(S["mul_done"], 2 * n + 2)
            eng.tensor_tensor(m1[:, k % 2, :], m1[:, k % 2, :], m2[:, k % 2, :], ALU.add).then_inc(S["add_done"], 1)

        def pool_scale(eng, n, k):
            S = LS
            eng.wait_ge(S["add_done"], n + 1)
            eng.wait_ge(S["rn_done"], n + 1)
            need(eng, S["t_mm"], 2 * (n - 1))
            eng.tensor_tensor(qkn[:, k % 2, :].rearrange("p (h d) -> p h d", d=DH),
                              m1[:, k % 2, :].rearrange("p (h d) -> p h d", d=DH),
                              rn[:, k % 2, :].unsqueeze(2).broadcast_to([P, 2 * H, DH]),
                              ALU.mult).then_inc(S["qkn_done"], 1)

        def pool_retention_norm(eng, t, b):
            n = 4 * t + b
            need_apart(eng, A["sqq"], 2 * n + 2)
            eng.tensor_scalar(ars[:, b % 2, :], ass[:, b % 2, :], 1e-24, None, ALU.max).then_inc(A["floor"], 1)
            eng.wait_ge(A["floor"], n + 1)
            eng.tensor_tensor(ars[:, b % 2, :], ars[:, b % 2, :], half_neg[:, 0:2], ALU.pow).then_inc(A["rs"], 1)

        def pool_retention(eng, t):
            for b in range(NB):
                pool_mask_qk(eng, t, b)
                if b < NB - 1:
                    pool_retention_norm(eng, t, b + 1)
                if b == 0:
                    pool_add(eng, count((0, t), NB - 1), NB - 1)
                if b == 1:
                    pool_scale(eng, count((0, t), NB - 1), NB - 1)

        def pool_mask_qk(eng, t, b):
            n = 4 * t + b
            shape = [P, NBL, NG, BL]
            eng.wait_ge(A["t_ev"], n + 1)
            need(eng, A["st_mm"], n - 1)
            eng.tensor_tensor(kx[:, b % 2, :, :, :],
                              aqkT[:, b % 2, 1, :].rearrange("p (c n) -> p c n", c=NBL).unsqueeze(2).broadcast_to(shape),
                              place_mask.unsqueeze(1).unsqueeze(3).broadcast_to(shape), ALU.mult).then_inc(A["kx"], 1)
            need(eng, A["y_mm"], n - 1)
            eng.tensor_tensor(qx[:, b % 2, :, :, :],
                              aqkT[:, b % 2, 0, :].rearrange("p (c n) -> p c n", c=NBL).unsqueeze(2).broadcast_to(shape),
                              group_mask.unsqueeze(1).unsqueeze(3).broadcast_to(shape), ALU.mult).then_inc(A["qx"], 1)

        def pool_group_norm(eng, k):
            g = gn[k]
            eng.wait_ge(g["var"], 1)
            eng.tensor_tensor(grs[:, :], gtmp[:, 0, :], half_neg[:, 0:NB], ALU.pow).then_inc(g["rs"], 1)

        @block.gpsimd
        def _(eng):
            eng.memset(half_neg[:, :], -0.5).then_inc(memset_done, 1)
            eng.memset(state[:, :, :], 0.0).then_inc(memset_done, 1)
            eng.memset(xnT[:, :, 0:1], 0.0).then_inc(memset_done, 1)
            eng.memset(x2T[:, :, 0:1], 0.0).then_inc(memset_done, 1)
            for b in range(NB):
                eng.memset(kT[b][:, :, P:P + WIN], 0.0).then_inc(memset_done, 1)
                eng.memset(vmix[b][:, :, 0:DH], 0.0).then_inc(memset_done, 1)
                eng.memset(vown[b][:, :, DH:DH + 1], 1.0).then_inc(memset_done, 1)
                eng.memset(vmix[b][:, :, DH:DH + 1], 1.0).then_inc(memset_done, 1)
            eng.memset(xr[:, :, 0:1], 0.0).then_inc(memset_done, 1)
            eng.wait_ge(memset_done, 5 + 4 * NB)
            eng.wait_ge(st_done, NT)
            eng.tensor_scalar(vpe[:, :, :], mv[:, :, :, 1], EPS, None, ALU.add).then_inc(var_done, 1)
            eng.wait_ge(var_done, 1)
            eng.tensor_tensor(rstd[:, :, :], vpe[:, :, :],
                              half_neg[:, :].rearrange("p (t b) -> p t b", b=NB), ALU.pow).then_inc(rstd_done, 1)
            eng.wait_ge(tab_ld, 16)
            eng.wait_ge(gain_ld, 16 * 4)
            for l in range(DEPTH):
                for g in range(2):
                    eng.tensor_tensor(rope[l][:, :, g, :], tab[:, :, g, :],
                                      gain[:, l, g, :].unsqueeze(1).broadcast_to([P, NT, DH]),
                                      ALU.mult).then_inc(rope_done, 1)
                    for s in range(2):
                        eng.tensor_tensor(rope[l][:, :, 2 + g, 32 * s:32 * s + 32], tab[:, :, 2 + g, 32 * s:32 * s + 32],
                                          gain[:, l, g, 32 - 32 * s:64 - 32 * s].unsqueeze(1).broadcast_to([P, NT, 32]),
                                          ALU.mult).then_inc(rope_done, 1)
            pool_group_norm(eng, 0)
            def body(new, old, ff):
                for k in range(NB):
                    pool_slot(eng, new, old, k)
                if new and new[0] == 0:
                    pool_retention(eng, new[1])

            run_bodies(eng, body, lambda: pool_group_norm(eng, 1))

        def act_shift(eng, step, b):
            src = xnT if step[0] == 0 else x2T
            need(eng, LS["qk_mm"], count(step, b) - 3)
            for rows, back in ((slice(0, 64), 0), (slice(64, P), 1)):
                eng.activation(hT[rows, b, :], src[rows, b, bass.ds(step[1] * P + 1 - back, P)],
                               ACT.Copy).then_inc(LS["h_ready"], 1)

        def act_slot(eng, new, old, ff, k):
            S = LS
            if new:
                n = count(new, k)
                if k == 0:
                    if new[0] == 1:
                        eng.wait_ge(S["x2_done"], new[1] + 1)
                    act_shift(eng, new, 0)
                if k < NB - 1:
                    act_shift(eng, new, k + 1)
                if not is_start(new):
                    need(eng, S["o_mm"], n - 3)
                    eng.activation(vmix[k][64:P, :, 0:DH], vown[k][64:P, :, 0:DH], ACT.Copy).then_inc(S["v_kept"], 1)
                    eng.activation(kT[k][:, :, P:P + WIN], kT[k][:, :, WIN:P], ACT.Copy).then_inc(S["carried"], 1)
            turned = at(new, old, k - 2)
            if turned:
                step, b, m = turned
                eng.wait_ge(S["t_mm"], 2 * m + 1)
                if not is_start(step):
                    eng.wait_ge(S["carried"], m - 3)
                eng.activation(kT[b][:, :, 0:P], pT[:, 512:1024].rearrange("p (c n) -> p c n", c=4), ACT.Copy).then_inc(S["t_ev"], 1)
                eng.wait_ge(S["t_mm"], 2 * m + 2)
                eng.activation(qT[:, :, :], pT[:, 0:512].rearrange("p (c n) -> p c n", c=4), ACT.Copy).then_inc(S["t_ev"], 1)
            if new:
                eng.wait_ge(S["v_mm"], n + 1)
                if not is_start(new):
                    eng.wait_ge(S["v_kept"], n - 3)
                values = pV[:, :].rearrange("p (h d) -> p h d", h=H)
                eng.activation(vown[k][:, :, 0:DH], values, ACT.Copy).then_inc(S["v_ev"], 1)
                eng.activation(vmix[k][0:64, :, 0:DH], values[0:64], ACT.Copy).then_inc(S["v_ev"], 1)
            if ff and ff[0] == 1 and k == 1:
                act_block_ffn(eng, ff[1])
            weighted = at(new, old, k - 3)
            if weighted:
                eng.wait_ge(S["pt_mm"], weighted[2] + 1)
                eng.activation(prT[:, :, :], pT[:, :].rearrange("p (h n) -> p h n", h=H), ACT.Copy).then_inc(S["pt_ev"], 1)
            if k > 0:
                act_output(eng, old, k)
            if ff and k == 0:
                eng.wait_ge(S["hnt_mm"], step_count(ff) + 1)
                eng.activation(hnT[:, :], pM[:, :], ACT.Copy).then_inc(S["hnt_ev"], 1)
            if k == 0 and turned:
                act_exp(eng, b, m)
            if new:
                eng.wait_ge(S["qk_mm"], n + 1)
                need(eng, S["ss_done"], n)
                eng.activation(sq[:, :], pQK[:, :], ACT.Square).then_inc(S["sq_done"], 1)
            if k == 0:
                if ff:
                    act_gelu(eng, ff)
                act_output(eng, old, 0)
            if k == NB - 1 and new and new[0] == 0:
                act_retention_project(eng, new[1], 0)
            if old and k == NB - 1:
                eng.wait_ge(S["xr_done"], count(old, NB - 1) + 1)
                need(eng, S["hnt_mm"], step_count(old))
                eng.activation(hs[0:64, :, :], xr[0:64, :, 1:1 + P], ACT.Copy).then_inc(S["hs"], 1)
                eng.activation(hs[64:P, :, :], xr[64:P, :, 0:P], ACT.Copy).then_inc(S["hs"], 1)
            if k > 0 and turned:
                act_exp(eng, b, m)

        def act_exp(eng, b, n):
            eng.wait_ge(LS["sub_done"], n + 1)
            eng.activation(pr[:, b % 2, :, :], pr[:, b % 2, :, :], ACT.Exp).then_inc(LS["exp_done"], 1)

        def act_output(eng, step, b):
            if step:
                eng.wait_ge(LS["ot_mm"], count(step, b) + 1)
                eng.activation(oT[:, :, :], pM[:, :].rearrange("p (c n) -> p c n", c=4), ACT.Copy).then_inc(LS["ot_ev"], 1)

        def act_gelu(eng, step):
            S, l, ct = LS, step[0], step_count(step)
            for k, (lo, m) in enumerate(CHUNKS):
                eng.wait_ge(S["ag_mm"], NC * ct + k + 1)
                if k >= 2:
                    eng.wait_ge(S["hf_done"], NC * ct + k - 1)
                pag = ffn_banks[k]
                eng.activation(gg[0:m, k % 2, :], pag[0:m, 512:1024], ACT.Gelu,
                               bias=b1e[0:m, l, 1, k:k + 1]).then_inc(S["gelu_done"], 1)

        def act_retention_project(eng, t, b):
            n = 4 * t + b
            if b == 0:
                eng.wait_ge(A["xa"], 4 * t + 4)
            need(eng, A["vx_mm"], n - 1)
            eng.activation(xa4[:, b % 2, :, :, :],
                           xa[:, b, :].rearrange("p (c n) -> p c n", c=NBL).unsqueeze(2).broadcast_to(
                               [P, NBL, NG, BL]), ACT.Copy).then_inc(A["xa4"], 1)
            eng.wait_ge(A["qkv_mm"], n + 1)
            need(eng, A["rs"], n - 1)
            for g in range(2):
                need(eng, A["sqq"], 2 * n + g)
                eng.activation(asq[:, :], pV[:, g * P:(g + 1) * P], ACT.Square,
                               accum_out=ass[:, b % 2, g:g + 1]).then_inc(A["sqq"], 1)
            need(eng, A["kv_mm"], n - 1)
            eng.activation(av[:, b % 2, :], pV[:, 2 * P:3 * P], ACT.Copy).then_inc(A["v"], 1)

        def act_retention(eng, t):
            for k in range(NB + 1):
                if k < NB:
                    n = 4 * t + k
                    eng.wait_ge(A["t_mm"], n + 1)
                    need(eng, A["qx"], n - 1)
                    eng.activation(aqkT[:, k % 2, :, :], pS[:, 0:256].rearrange("p (g n) -> p g n", g=2),
                                   ACT.Copy).then_inc(A["t_ev"], 1)
                if k + 1 < NB:
                    act_retention_project(eng, t, k + 1)
                if k > 0:
                    b = k - 1
                    eng.wait_ge(A["y_mm"], 4 * t + b + 1)
                    for g in range(NG):
                        r = slice(BL * g, BL * g + BL)
                        eng.activation(ayT[r, b * P:(b + 1) * P].rearrange("p (c n) -> p c n", c=NBL),
                                       y_banks[b % 2][r, 512:1024].rearrange("p (c g n) -> p c g n", c=NBL, g=NG)[:, :, g, :],
                                       ACT.Copy).then_inc(A["yt"], 1)

        def act_block_ffn(eng, t):
            for j in range(2):
                eng.wait_ge(G["w1_mm"], 2 * t + j + 1)
                eng.activation(afh[:, j, :], pQK[:, j * 512:(j + 1) * 512], ACT.Silu, bias=c("b1a", j)).then_inc(G["silu"], 1)

        @block.scalar
        def _(eng):
            eng.dma_start(cst[:, :], a["k_cst"]).then_inc(cst_ld, 16)
            eng.dma_start(mask32[:, :, :], a["k_mask"]).then_inc(cst_ld, 16)
            for k, n in enumerate(("qw", "kw", "vw", "ow")):
                eng.dma_start(araw[:, k, :], a["L0_attn_" + n]).then_inc(aw_ld, 16)
            eng.dma_start(araw[:, 4:6, :], a["L0_attn_w1"].rearrange("(c p) d -> p c d", p=P)).then_inc(aw_ld, 16)
            eng.dma_start(araw[:, 6:8, :], a["L0_attn_w2"].rearrange("p (c d) -> p c d", c=2)).then_inc(aw_ld, 16)

            def column(name, ap, k=1):
                with nc.allow_non_contiguous_dma(reason="one value per partition"):
                    eng.dma_start(col[:, COLS[name]:COLS[name] + k], ap).then_inc(col_ld, 16)
            for name, arg in (("ng", "norm_g"), ("nb", "norm_b"), ("ob", "ob"), ("fg", "ffn_norm_g"),
                              ("fb", "ffn_norm_b"), ("b2a", "b2")):
                column(name, a["L0_attn_" + arg].rearrange("(p o) -> p o", o=1))
            column("b1a", a["L0_attn_b1"].rearrange("(c p) -> p c", p=P), 2)
            for name, arg in (("lg", "ln_g"), ("lb", "ln_b"), ("b2", "b2")):
                column(name, a["L0_ffn_" + arg].rearrange("l p -> p l"), 2)
            for g, n in enumerate(("q_scale", "k_scale")):
                for l in range(DEPTH):
                    eng.dma_start(gain[:, l, g, :], a["L0_ffn_" + n][l:l + 1, :].broadcast_to([P, DH])).then_inc(gain_ld, 16)
            with nc.allow_non_contiguous_dma(reason="one value per partition"):
                for l in range(DEPTH):
                    for s in range(2):
                        row = a["L0_ffn_b1"][l, s * HID:(s + 1) * HID]
                        eng.dma_start(b1c[:, l, s, 0:2], row[0:256].rearrange("(c p) -> p c", p=P)).then_inc(col_ld, 16)
                        eng.dma_start(b1c[0:HID - 256, l, s, 2:3], row[256:HID].rearrange("(p o) -> p o", o=1)).then_inc(col_ld, 16)
            for g in range(2):
                eng.wait_ge(awt_mm, g + 1)
                eng.activation(aT[:, 4 * g:4 * g + 4, :], pT[:, 512 * g:512 * g + 512].rearrange("p (k n) -> p k n", k=4),
                               ACT.Copy).then_inc(awt_ev, 1)
            eng.wait_ge(memset_done, 3)
            with eng.Fori(0, NT) as t:
                eng.wait_ge(xnt_mm, t + 1)
                eng.activation(xnT[:, :, bass.ds(t * P + 1, P)], pM[:, :].rearrange("p (b n) -> p b n", b=NB),
                               ACT.Copy).then_inc(xnt_ev, 1)
            eng.wait_ge(memset_done, 5 + 4 * NB)
            eng.wait_ge(be_done, 2)
            eng.wait_ge(col_ld, 16 * 18)

            def body(new, old, ff):
                for k in range(NB):
                    act_slot(eng, new, old, ff, k)
                if new and new[0] == 0:
                    act_retention(eng, new[1])

            run_bodies(eng, body, lambda: None)

        def dve_rotate(eng, step, k, weighted, ff=None):
            S, (l, t), n = LS, step, count(step, k)
            qk = pQK[:, :].rearrange("p (g h d) -> p g h d", g=2, h=H)
            rot = pQK[:, :].rearrange("p (g h s d) -> p g h s d", g=2, h=H, s=2)[:, :, :, ::-1, :]
            cos = rope[l][:, t, 0:2, :].unsqueeze(2).broadcast_to([P, 2, H, DH])
            sin = rope[l][:, t, 2:4, :].rearrange("p g (s d) -> p g s d", s=2).unsqueeze(2).broadcast_to([P, 2, H, 2, 32])
            eng.wait_ge(S["sq_done"], n + 1)
            need(eng, S["max_ss"], n - 1)
            eng.tensor_reduce(ss[:, k % 2, :], sq[:, :].rearrange("p (h d) -> p h d", d=DH), AX.X,
                              ALU.add).then_inc(S["ss_done"], 1)
            if weighted:
                dve_output(eng, weighted[2])
            need(eng, S["add_done"], n - 1)
            need(eng, S["qkn_done"], n - 1)
            for i, (m, src, by, sizes) in enumerate(((m1, qk, cos, {"d": DH}), (m2, rot, sin, {"s": 2, "d": 32}))):
                shape = "p (g h d) -> p g h d" if i == 0 else "p (g h s d) -> p g h s d"
                eng.tensor_tensor(m[:, k % 2, :].rearrange(shape, g=2, h=H, **sizes), src, by,
                                  ALU.mult).then_inc(S["mul_done"], 1)
                if i == 0 and ff:
                    dve_hidden(eng, ff, 0)

        def dve_scores(eng, b, n):
            S = LS
            eng.wait_ge(S["s_mm"], n + 1)
            sc = pS[:, :].rearrange("p (h n) -> p h n", h=H)
            eng.tensor_reduce(mx[:, :], sc, AX.X, ALU.max).then_inc(S["mx_done"], 1)
            eng.wait_ge(S["mx_done"], n + 1)
            eng.tensor_tensor(pr[:, b % 2, :, :], sc, mx[:, :].unsqueeze(2).broadcast_to([P, H, P]),
                              ALU.subtract).then_inc(S["sub_done"], 1)

        def dve_output(eng, n):
            S = LS
            po = pS[:, :].rearrange("p (g z) -> p g z", g=2)[:, :, 0:4 * (DH + 1)].rearrange("p g (h d) -> p g h d", h=4)
            eng.wait_ge(S["o_mm"], n + 1)
            eng.reciprocal(rec[:, :, :], po[:, :, :, DH]).then_inc(S["rec_done"], 1)
            eng.wait_ge(S["rec_done"], n + 1)
            eng.tensor_tensor(o[:, :].rearrange("p (c g d) -> p g c d", g=2, d=DH), po[:, :, :, 0:DH],
                              rec[:, :, :].unsqueeze(3).broadcast_to([P, 2, 4, DH]), ALU.mult).then_inc(S["o_done"], 1)

        def dve_residual(eng, step, b):
            S, (l, t), n = LS, step, count(step, b)
            src = xnT if l == 0 else x2T
            eng.wait_ge(S["wo_mm"], n + 1)
            if not is_start(step):
                eng.wait_ge(S["xr_carried"], step_count(step))
            eng.tensor_tensor(xr[:, b, 1:1 + P], pM[:, 0:P], src[:, b, bass.ds(t * P + 1, P)],
                              ALU.add).then_inc(S["xr_done"], 1)

        def dve_slot(eng, new, old, ff, k):
            retain = k == NB - 1 and new and new[0] == 0
            if retain:
                dve_retention_in(eng, new[1])
            if ff and k == 0:
                dve_ln_apply(eng, ff)
            if old and k == 0 and old[0] == 0:
                dve_retention_out(eng, old[1])
            turned = at(new, old, k - 2)
            if turned:
                dve_scores(eng, turned[1], turned[2])
            if k > 0 and old:
                dve_residual(eng, old, k)
            weighted = at(new, old, k - 3)
            if k == 0 and ff:
                if ff[0] == 1:
                    dve_block_in(eng, ff[1])
                if new:
                    dve_rotate(eng, new, 0, None, ff)
                else:
                    dve_hidden(eng, ff, 0)
                dve_hidden(eng, ff, 1)
                dve_hidden(eng, ff, 2)
                dve_ffn_out(eng, ff)
                if weighted:
                    dve_output(eng, weighted[2])
            elif new:
                dve_rotate(eng, new, k, weighted)
            elif weighted:
                dve_output(eng, weighted[2])
            if k == 0 and old:
                dve_residual(eng, old, 0)
            if ff and ff[0] == 1 and k == 1:
                dve_block_out(eng, ff[1])
            if ff and ff[0] == 1 and k == 2:
                dve_final(eng, ff[1])
            if retain:
                dve_retention_qk(eng, new[1], 0)
            if old and k == NB - 1:
                dve_ln(eng, old)

        def dve_ln(eng, step):
            S, ct = LS, step_count(step)
            eng.wait_ge(S["ln_mm"], ct + 1)
            for b in range(NB):
                eng.bn_stats(lbst[:, b, :], pM[:, b * D:(b + 1) * D]).then_inc(S["ln_bst"], 1)
            need_apart(eng, S["ln_bst"], NB * ct + NB)
            for b in range(NB):
                eng.bn_aggr(lmv[:, b, :], lbst[:, b, :]).then_inc(S["ln_st"], 1)

        def dve_ln_apply(eng, step):
            S, ct = LS, step_count(step)
            eng.wait_ge(S["ln_rs"], ct + 1)
            for b in range(NB):
                eng.tensor_scalar(hn[:, b, :], pM[:, b * D:(b + 1) * D], lmv[:, b, 0:1], lrs[:, b:b + 1],
                                  ALU.subtract, ALU.mult).then_inc(S["hn_done"], 1)

        def dve_hidden(eng, step, k):
            S, l, ct = LS, step[0], step_count(step)
            m, pag = CHUNKS[k][1], ffn_banks[k]
            eng.wait_ge(S["gelu_done"], NC * ct + k + 1)
            eng.scalar_tensor_tensor(out=hf[0:m, k, :], in0=pag[0:m, 0:512], scalar=b1e[0:m, l, 0, k:k + 1],
                                     in1=gg[0:m, k % 2, :], op0=ALU.add, op1=ALU.mult).then_inc(S["hf_done"], 1)

        def dve_ffn_out(eng, step):
            S, (l, t), ct = LS, step, step_count(step)
            eng.wait_ge(S["w2_mm"], ct + 1)
            dst = x2T[:, :, bass.ds(t * P + 1, P)] if l == 0 else fin[:, :, :]
            eng.scalar_tensor_tensor(out=dst, in0=pM[:, :].rearrange("p (b n) -> p b n", b=NB), scalar=c("b2", l),
                                     in1=xr[:, :, 1:1 + P], op0=ALU.add, op1=ALU.add).then_inc(S["x2_done"], 1)

        def dve_retention_in(eng, t):
            need(eng, A["qkv_mm"], 4 * t)
            for b in range(NB):
                eng.tensor_scalar(xa[:, b, :], xnT[:, b, bass.ds(t * P + 1, P)], gsc[0][:, b:b + 1], gsh[0][:, b:b + 1],
                                  ALU.mult, ALU.add).then_inc(A["xa"], 1)

        def dve_retention_qk(eng, t, b):
            n = 4 * t + b
            eng.wait_ge(A["rs"], n + 1)
            eng.wait_ge(A["v"], n + 1)
            need(eng, A["kv_mm"], n - 1)
            for g, dec in enumerate((decay_q, decay_k)):
                eng.scalar_tensor_tensor(out=aqk[:, b % 2, g, :], in0=pV[:, g * P:(g + 1) * P],
                                         scalar=ars[:, b % 2, g:g + 1], in1=dec, op0=ALU.mult,
                                         op1=ALU.mult).then_inc(A["qk"], 1)

        def dve_retention(eng, t):
            eng.wait_ge(LS["qkn_done"], 4 * t + 3)
            for k in range(NB + 1):
                if k < NB:
                    n = 4 * t + k
                    eng.wait_ge(A["vx_mm"], n + 1)
                    need(eng, A["y_mm"], n - 1)
                    eng.tensor_tensor(vx[:, k % 2, :, :], pT[:, 0:512].rearrange("p (c n) -> p c n", c=NBL),
                                      value_mask.unsqueeze(1).broadcast_to([P, NBL, P]), ALU.mult).then_inc(A["vx"], 1)
                    eng.wait_ge(A["kv_mm"], n + 1)
                    need(eng, A["state"], n - 1)
                    eng.tensor_tensor(before[:, k % 2, :, :], pQK[:, 512:1024].rearrange("p (c n) -> p c n", c=NBL),
                                      same_head.unsqueeze(1).broadcast_to([P, NBL, P]), ALU.mult).then_inc(A["kvm"], 1)
                    eng.wait_ge(A["kvm"], n + 1)
                    eng.tensor_tensor(before[:, k % 2, :, :], before[:, k % 2, :, :],
                                      state[:, k, :].unsqueeze(1).broadcast_to([P, NBL, P]), ALU.add).then_inc(A["before"], 1)
                if k + 1 < NB:
                    dve_retention_qk(eng, t, k + 1)
                if k > 0:
                    b = k - 1
                    n = 4 * t + b
                    eng.wait_ge(A["y_mm"], n + 1)
                    eng.tensor_scalar(state[:, b, :], before[:, b % 2, NBL - 1, :], state_decay, None,
                                      ALU.mult).then_inc(A["state"], 1)
                if k < NB:
                    n = 4 * t + k
                    eng.wait_ge(A["st_mm"], n + 1)
                    eng.tensor_tensor(sm[:, k % 2, :, :, :],
                                      pQK[:, 0:512].rearrange("p (c g n) -> p c g n", c=NBL, g=NG),
                                      causal.unsqueeze(1).unsqueeze(1).broadcast_to([P, NBL, NG, BL]),
                                      ALU.mult).then_inc(A["sm"], 1)
        def dve_retention_out(eng, t):
            eng.wait_ge(A["ow_mm"], t + 1)
            eng.scalar_tensor_tensor(out=x1T[:, :, bass.ds(t * P, P)], in0=pS[:, 0:512].rearrange("p (b n) -> p b n", b=NB),
                                     scalar=c("ob"), in1=xnT[:, :, bass.ds(t * P + 1, P)], op0=ALU.add,
                                     op1=ALU.add).then_inc(A["x1"], 1)
            eng.wait_ge(A["x1"], t + 1)
            for b in range(NB):
                eng.bn_stats(cbst[1][:, b, t, :], x1T[:, b, bass.ds(t * P, P)]).then_inc(A["cs"], 1)

        def dve_block_in(eng, t):
            for b in range(NB):
                eng.tensor_scalar(xa[:, b, :], x1T[:, b, bass.ds(t * P, P)], gsc[1][:, b:b + 1], gsh[1][:, b:b + 1],
                                  ALU.mult, ALU.add).then_inc(G["xa"], 1)

        def dve_block_out(eng, t):
            eng.wait_ge(G["w2_mm"], t + 1)
            eng.scalar_tensor_tensor(out=att[:, :, :], in0=pM[:, :].rearrange("p (b n) -> p b n", b=NB), scalar=c("b2a"),
                                     in1=x1T[:, :, bass.ds(t * P, P)], op0=ALU.add, op1=ALU.add).then_inc(G["att"], 1)
            eng.wait_ge(LS["x2_done"], NT + t + 1)
            eng.wait_ge(G["att"], t + 1)
            eng.tensor_tensor(fin[:, :, :], fin[:, :, :], att[:, :, :], ALU.add).then_inc(G["fin"], 1)

        def dve_final(eng, t):
            eng.wait_ge(G["fin_mm"], t + 1)
            eng.wait_ge(G["xs"], 16 * t + 16)
            eng.tensor_tensor(osb[:, :, :], pM[:, :].rearrange("p (b d) -> p b d", b=NB), xs[:, :, :],
                              ALU.add).then_inc(G["osb"], 1)

        def dve_group_norm(eng, k, gain_col, bias_col):
            g = gn[k]
            for b in range(NB):
                eng.bn_aggr(cmv[:, b, :], cbst[k][:, b, :, :]).then_inc(g["agg"], 1)
            eng.wait_ge(g["agg"], NB)
            steps = [0]

            def then(ins):
                steps[0] += 1
                ins.then_inc(g["dve"], 1)
                eng.wait_ge(g["dve"], steps[0])
            then(eng.tensor_copy(cst2[:, 0, :], cmv[:, :, 0]))
            then(eng.tensor_tensor(cst2[:, 1, :], cmv[:, :, 0], cmv[:, :, 0], ALU.mult))
            then(eng.tensor_tensor(cst2[:, 1, :], cst2[:, 1, :], cmv[:, :, 1], ALU.add))
            eng.wait_ge(g["mm"], 1)
            then(eng.tensor_copy(gst[:, :, :], pV[:, 0:2 * NB].rearrange("p (s b) -> p s b", s=2)))
            then(eng.tensor_tensor(gtmp[:, 1, :], gst[:, 0, :], gst[:, 0, :], ALU.mult))
            then(eng.tensor_tensor(gtmp[:, 0, :], gst[:, 1, :], gtmp[:, 1, :], ALU.subtract))
            eng.tensor_scalar(gtmp[:, 0, :], gtmp[:, 0, :], EPS, None, ALU.add).then_inc(g["var"], 1)
            eng.wait_ge(g["rs"], 1)
            then(eng.tensor_scalar(gsc[k][:, :], grs[:, :], gain_col, None, ALU.mult))
            then(eng.tensor_tensor(gtmp[:, 1, :], gst[:, 0, :], gsc[k][:, :], ALU.mult))
            eng.tensor_scalar(gsh[k][:, :], gtmp[:, 1, :], -1.0, bias_col, ALU.mult, ALU.add).then_inc(g["done"], 1)
            eng.wait_ge(g["done"], 1)

        @block.vector
        def _(eng):
            for b in range(NB):
                eng.wait_ge(x_ld[b], 16)
            with eng.Fori(0, NT) as t:
                for b in range(NB):
                    eng.bn_stats(bst[:, b, :], x[:, b, t, :]).then_inc(xst_done, 1)
                need_apart(eng, xst_done, NB * t + NB)
                for b in range(NB):
                    eng.bn_aggr(lmv[:, b, :], bst[:, b, :]).then_inc(agg_done, 1)
                eng.wait_ge(agg_done, NB * t + NB)
                eng.tensor_copy(mv[:, t, :, :], lmv[:, :, :]).then_inc(st_done, 1)
            eng.wait_ge(cst_ld, 32)
            eng.tensor_copy(mask16[:, :, :], mask32[:, :, :]).then_inc(mask_done, 1)
            eng.wait_ge(rstd_done, 1)

            def normalize(half):
                for u in range(2):
                    t = 2 * half + u
                    need(eng, xnt_mm, 2 * half)
                    for b in range(NB):
                        eng.tensor_scalar(xn[:, u, b, :], x[:, b, t, :], mv[:, t, b, 0:1], rstd[:, t, b:b + 1],
                                          ALU.subtract, ALU.mult).then_inc(xn_done, 1)
            normalize(0)
            with eng.Fori(1, NT // 2) as half:
                normalize(half)
            with eng.Fori(0, NT) as t:
                eng.wait_ge(xnt_ev, t + 1)
                for b in range(NB):
                    eng.bn_stats(cbst[0][:, b, t, :], xnT[:, b, bass.ds(t * P + 1, P)]).then_inc(cs_done, 1)
            eng.wait_ge(cs_done, NB * NT)
            eng.wait_ge(w_ld, 16 * 5 * DEPTH)
            eng.wait_ge(col_ld, 16 * (10 + 8))
            eng.wait_ge(be_mm, 1)
            for l in range(DEPTH):
                eng.tensor_scalar(w1[:, l, :], w1[:, l, :], c("lg", l), None, ALU.mult).then_inc(w1g_done, 1)
            pb = pV[:, 64:64 + 2 * DEPTH * NC].rearrange("p (l s k) -> p l s k", l=DEPTH, s=2)
            last = HID - 256
            eng.tensor_tensor(b1e[:, :, :, 0:2], pb[:, :, :, 0:2], b1c[:, :, :, 0:2], ALU.add).then_inc(be_done, 1)
            eng.tensor_tensor(b1e[0:last, :, :, 2], pb[0:last, :, :, 2], b1c[0:last, :, :, 2], ALU.add).then_inc(be_done, 1)
            dve_group_norm(eng, 0, c("ng"), c("nb"))
            eng.wait_ge(rope_done, 6 * DEPTH)

            def body(new, old, ff):
                for k in range(NB):
                    dve_slot(eng, new, old, ff, k)
                if new and new[0] == 0:
                    dve_retention(eng, new[1])

            def between():
                eng.wait_ge(A["cs"], NB * NT)
                dve_group_norm(eng, 1, c("fg"), c("fb"))

            run_bodies(eng, body, between)

        def pe_turn(eng, b, n):
            S = LS
            eng.wait_ge(S["qkn_done"], n + 1)
            need(eng, S["t_ev"], 2 * n)
            need(eng, S["pt_ev"], n - 1)
            for half in (1, 0):
                for j in range(4 * half, 4 * half + 4):
                    mm = eng.transpose(pT[:, j * P:(j + 1) * P], qkn[:, b % 2, j * P:(j + 1) * P], ident)
                mm.then_inc(S["t_mm"], 1)

        def pe_scores(eng, step, b, n):
            S = LS
            eng.wait_ge(S["t_ev"], 2 * n + 2)
            need(eng, S["sub_done"], n)
            need(eng, S["o_done"], n - 1)
            if b == 2:
                eng.wait_ge(A["x1"], step[1] + 1 if step[0] == 0 else NT)
            mask = mask16[:, 0 if is_first(step) else 1, :].unsqueeze(1).broadcast_to([P, 4, P])
            for g in range(2):
                eng.matmul(pS[:, g * 512:(g + 1) * 512], mask16[:, 2, :], mask, start=True, stop=False,
                           skip_group_check=True)
            kk = kT[b]
            for j in range(4):
                for g in range(2):
                    r = slice(64 * g, 64 * g + 64)
                    col0 = g * 512 + j * P
                    for w in range(2):
                        if w == 0:
                            for s, lo in enumerate((0, P)):
                                mm = eng.matmul(pS[0:64, col0 + 64 * s:col0 + 64 * s + 64], qT[r, j, 0:64],
                                                kk[r, j, lo:lo + 64], start=False, stop=True, skip_group_check=True)
                        else:
                            mm = eng.matmul(pS[64:P, col0:col0 + P], qT[r, j, 64:P], kk[r, j, 0:P],
                                            start=False, stop=True, skip_group_check=True)
            mm.then_inc(S["s_mm"], 1)

        def pe_turn_weights(eng, b, n, turned):
            S = LS
            eng.wait_ge(S["exp_done"], n + 1)
            need(eng, S["pt_ev"], n)
            if turned:
                eng.wait_ge(S["t_ev"], 2 * (n + 2))
            for j in range(8):
                mm = eng.transpose(pT[:, j * P:(j + 1) * P], pr[:, b % 2, j, :], ident)
            mm.then_inc(S["pt_mm"], 1)

        def pe_values(eng, b, n, turned):
            S = LS
            eng.wait_ge(S["pt_ev"], n + 1)
            eng.wait_ge(S["v_ev"], 2 * n + 2)
            if turned:
                eng.wait_ge(S["sub_done"], n + 2)
            need(eng, S["o_done"], n)
            for i in range(H):
                g, j = i // 4, i % 4
                for w in range(2):
                    col0 = g * 512 + j * (DH + 1)
                    mm = eng.matmul(pS[64 * w:64 * w + 64, col0:col0 + DH + 1], prT[:, i, 64 * w:64 * w + 64],
                                    (vown if w else vmix)[b][:, 2 * j + g, :], start=(j == 0), stop=True,
                                    skip_group_check=True)
            mm.then_inc(S["o_mm"], 1)

        def pe_turn_output(eng, n):
            S = LS
            eng.wait_ge(S["o_done"], n + 1)
            need(eng, S["xr_done"], n)
            for j in range(4):
                mm = eng.transpose(pM[:, j * P:(j + 1) * P], o[:, j * P:(j + 1) * P], ident)
            mm.then_inc(S["ot_mm"], 1)

        def pe_wo(eng, l, n):
            eng.wait_ge(LS["ot_ev"], n + 1)
            for j in range(4):
                mm = eng.matmul(pM[:, 0:P], wo[:, l, j, :], oT[:, j, :], start=(j == 0), stop=(j == 3))
            mm.then_inc(LS["wo_mm"], 1)

        def pe_slot(eng, new, old, ff, k):
            S = LS
            block_ffn = ff and ff[0] == 1
            turned = at(new, old, k - 2)
            weighted = at(new, old, k - 3)
            if k == 0 and old and old[0] == 0:
                eng.wait_ge(A["yt"], NG * (4 * old[1] + 3))
            if turned:
                pe_turn(eng, turned[1], turned[2])
            if k == 0 and old and old[0] == 0:
                pe_retention_out(eng, old[1])
            if new:
                l, n = new[0], count(new, k)
                eng.wait_ge(S["h_ready"], 2 * n + 2)
                need(eng, S["v_ev"], 2 * n)
                eng.matmul(pV[:, :], hT[:, k, :], wqkv[:, l, 1024:1536], start=True, stop=True).then_inc(S["v_mm"], 1)
            if k == 1 and block_ffn:
                need(eng, S["mul_done"], 2 * n if new else 0)
                eng.wait_ge(G["xa"], 4 * ff[1] + 4)
                for j in range(2):
                    eng.matmul(pQK[:, j * 512:(j + 1) * 512], aT[:, 4 + j, :], xa[:, :, :], start=True,
                               stop=True).then_inc(G["w1_mm"], 1)
            if turned:
                pe_scores(eng, *turned)
            if weighted:
                pe_turn_weights(eng, weighted[1], weighted[2], turned)
            if k == 0 and ff:
                ct = step_count(ff)
                eng.wait_ge(S["hn_done"], NB * ct + NB)
                for b in range(NB):
                    mm = eng.transpose(pM[:, b * P:(b + 1) * P], hn[:, b, :], ident)
                mm.then_inc(S["hnt_mm"], 1)
            if k > 0 and old:
                if k == 2 and block_ffn:
                    eng.wait_ge(G["att"], ff[1] + 1)
                if k == 3 and block_ffn:
                    eng.wait_ge(G["osb"], ff[1] + 1)
                pe_turn_output(eng, count(old, k))
            if new:
                need(eng, S["mul_done"], 2 * n)
                if k == 1 and block_ffn:
                    eng.wait_ge(G["silu"], 2 * ff[1] + 2)
                for g in range(2):
                    mm = eng.matmul(pQK[:, g * 512:(g + 1) * 512], hT[:, k, :], wqkv[:, l, g * 512:(g + 1) * 512],
                                    start=True, stop=True)
                mm.then_inc(S["qk_mm"], 1)
            if k == 0 and ff:
                pe_ffn(eng, ff, turned, weighted)
            if k == 0 and old:
                if ff:
                    eng.wait_ge(S["x2_done"], step_count(ff) + 1)
                pe_turn_output(eng, count(old, 0))
            if k > 0 and old:
                pe_wo(eng, old[0], count(old, k))
            if k == NB - 1 and new and new[0] == 0:
                pe_retention_project(eng, new[1], 0)
            if weighted:
                pe_values(eng, weighted[1], weighted[2], turned)
            if k == 0 and old:
                pe_wo(eng, old[0], count(old, 0))
            if k == 1 and block_ffn:
                eng.wait_ge(G["silu"], 2 * ff[1] + 2)
                eng.wait_ge(S["x2_done"], NT + ff[1] + 1)
                if old:
                    eng.wait_ge(S["xr_done"], count(old, 1) + 1)
                for j in range(2):
                    mm = eng.matmul(pM[:, :], aT[:, 6 + j, :], afh[:, j, :], start=(j == 0), stop=(j == 1))
                mm.then_inc(G["w2_mm"], 1)
            if k == 2 and block_ffn:
                eng.wait_ge(G["fin"], ff[1] + 1)
                if old:
                    eng.wait_ge(S["xr_done"], count(old, 2) + 1)
                for b in range(NB):
                    mm = eng.transpose(pM[:, b * P:(b + 1) * P], fin[:, b, :], ident)
                mm.then_inc(G["fin_mm"], 1)
            if k == NB - 1 and old:
                eng.wait_ge(S["hs"], 2 * step_count(old) + 2)
                for b in range(NB):
                    mm = eng.transpose(pM[:, b * P:(b + 1) * P], hs[:, b, :], ident)
                mm.then_inc(S["ln_mm"], 1)

        def pe_ffn(eng, step, turned, weighted):
            S, l, ct = LS, step[0], step_count(step)
            eng.wait_ge(S["hnt_ev"], ct + 1)
            if weighted:
                eng.wait_ge(S["pt_ev"], weighted[2] + 1)
            for k, (lo, m) in enumerate(CHUNKS):
                if k == 1 and turned:
                    eng.wait_ge(S["sub_done"], turned[2] + 1)
                if k == 2:
                    eng.wait_ge(S["hf_done"], NC * ct + 1)
                for s in range(2):
                    mm = eng.matmul(ffn_banks[k][0:m, s * 512:(s + 1) * 512], w1[:, l, s * HID + lo:s * HID + lo + m],
                                    hnT[:, :], start=True, stop=True)
                mm.then_inc(S["ag_mm"], 1)
            for k, (lo, m) in enumerate(CHUNKS):
                eng.wait_ge(S["hf_done"], NC * ct + k + 1)
                mm = eng.matmul(pM[:, :], w2[0:m, l, k, :], hf[0:m, k, :], start=(k == 0), stop=(k == NC - 1))
            mm.then_inc(S["w2_mm"], 1)

        def pe_retention_project(eng, t, b):
            n = 4 * t + b
            if b == 0:
                eng.wait_ge(A["xa"], 4 * t + 4)
                eng.wait_ge(LS["v_ev"], 2 * (4 * t + 4))
            need(eng, A["qk"], 2 * n)
            eng.matmul(pV[:, 0:3 * P], xa[:, b, :], aT[:, 0:3, :], start=True, stop=True).then_inc(A["qkv_mm"], 1)

        def pe_retention(eng, t):
            eng.wait_ge(LS["pt_ev"], 4 * t + 1)
            eng.wait_ge(LS["o_done"], 4 * t + 1)
            for k in range(NB + 1):
                if k < NB:
                    n = 4 * t + k
                    eng.wait_ge(A["qk"], 2 * n + 2)
                    need(eng, A["t_ev"], n)
                    for g in range(2):
                        mm = eng.transpose(pS[:, g * P:(g + 1) * P], aqk[:, k % 2, g, :], ident)
                    mm.then_inc(A["t_mm"], 1)
                if k + 1 < NB:
                    pe_retention_project(eng, t, k + 1)
                if k < NB:
                    eng.wait_ge(A["xa4"], n + 1)
                    need(eng, A["vx"], n)
                    for c_ in range(NBL):
                        mm = eng.matmul(pT[:, c_ * P:(c_ + 1) * P], xa4[:, k % 2, c_, :, :], aT[:, 2, :],
                                        start=True, stop=True)
                    mm.then_inc(A["vx_mm"], 1)
                    if k == 0:
                        eng.wait_ge(LS["mul_done"], 8 * t + 8)
                    need(eng, A["kvm"], n)
                    for c_ in range(NBL):
                        rows = slice(0, (c_ + 1) * BL)
                        mm = eng.matmul(pQK[:, 512 + c_ * P:512 + (c_ + 1) * P], aqk[rows, k % 2, 1, :], av[rows, k % 2, :],
                                        start=True, stop=True)
                    mm.then_inc(A["kv_mm"], 1)
                if k > 0:
                    b = k - 1
                    n = 4 * t + b
                    eng.wait_ge(A["sm"], n + 1)
                    eng.wait_ge(A["before"], n + 1)
                    need(eng, A["yt"], NG * (n - 1))
                    for c_ in range(NBL):
                        cols = slice(512 + c_ * P, 512 + (c_ + 1) * P)
                        eng.matmul(y_banks[b % 2][:, cols], vx[:, b % 2, c_, :], sm[:, b % 2, c_, :, :], start=True, stop=False)
                        mm = eng.matmul(y_banks[b % 2][:, cols], before[:, b % 2, c_ - 1, :] if c_ else state[:, b, :],
                                        qx[:, b % 2, c_, :, :], start=False, stop=True)
                    mm.then_inc(A["y_mm"], 1)
                if k < NB:
                    n = 4 * t + k
                    eng.wait_ge(A["kx"], n + 1)
                    eng.wait_ge(A["qx"], n + 1)
                    need(eng, A["sm"], n)
                    for c_ in range(NBL):
                        mm = eng.matmul(pQK[:, c_ * P:(c_ + 1) * P], kx[:, k % 2, c_, :, :], qx[:, k % 2, c_, :, :],
                                        start=True, stop=True)
                    mm.then_inc(A["st_mm"], 1)

        def pe_retention_out(eng, t):
            eng.wait_ge(A["yt"], NG * (4 * t + 4))
            eng.matmul(pS[:, 0:512], aT[:, 3, :], ayT[:, :], start=True, stop=True).then_inc(A["ow_mm"], 1)

        def pe_group_norm(eng, k):
            eng.wait_ge(gn[k]["dve"], 3)
            eng.matmul(pV[:, 0:2 * NB], group_avg, cst2[:, :, :], start=True, stop=True).then_inc(gn[k]["mm"], 1)

        @block.tensor
        def _(eng):
            eng.wait_ge(cst_ld, 32)
            eng.wait_ge(aw_ld, 16 * 6)
            for g in range(2):
                for j in range(4):
                    mm = eng.transpose(pT[:, g * 512 + j * P:g * 512 + (j + 1) * P], araw[:, 4 * g + j, :], ident)
                mm.then_inc(awt_mm, 1)

            def transpose_normalized(half):
                for u in range(2):
                    t = 2 * half + u
                    eng.wait_ge(xn_done, 4 * t + 4)
                    need(eng, xnt_ev, t)
                    for b in range(NB):
                        mm = eng.transpose(pM[:, b * P:(b + 1) * P], xn[:, u, b, :], ident)
                    mm.then_inc(xnt_mm, 1)
            transpose_normalized(0)
            with eng.Fori(1, NT // 2) as half:
                transpose_normalized(half)
            eng.wait_ge(w_ld, 16 * 5 * DEPTH)
            eng.wait_ge(col_ld, 16 * (10 + 8))
            for l in range(DEPTH):
                for s in range(2):
                    for k, (lo, m) in enumerate(CHUNKS):
                        at = 64 + (l * 2 + s) * NC + k
                        mm = eng.matmul(pV[0:m, at:at + 1], w1[:, l, s * HID + lo:s * HID + lo + m], c("lb", l),
                                        start=True, stop=True)
            mm.then_inc(be_mm, 1)
            eng.wait_ge(be_done, 2)
            pe_group_norm(eng, 0)
            eng.wait_ge(gn[0]["done"], 1)
            eng.wait_ge(w1g_done, DEPTH)
            eng.wait_ge(awt_ev, 2)
            eng.wait_ge(xnt_ev, NT)
            eng.wait_ge(mask_done, 1)
            eng.wait_ge(memset_done, 5 + 4 * NB)

            def body(new, old, ff):
                for k in range(NB):
                    pe_slot(eng, new, old, ff, k)
                if new and new[0] == 0:
                    pe_retention(eng, new[1])

            def between():
                eng.wait_ge(LS["v_ev"], 2 * (4 * NT + 4))
                pe_group_norm(eng, 1)
                eng.wait_ge(gn[1]["dve"], 4)

            run_bodies(eng, body, between)


_INS = ["L0_attn_x", "L0_attn_norm_g", "L0_attn_norm_b", "L0_attn_qw", "L0_attn_kw", "L0_attn_vw", "L0_attn_ow",
        "L0_attn_ob", "L0_attn_ffn_norm_g", "L0_attn_ffn_norm_b", "L0_attn_w1", "L0_attn_b1", "L0_attn_w2",
        "L0_attn_b2", "L0_ffn_wqkv", "L0_ffn_q_scale", "L0_ffn_k_scale", "L0_ffn_wo", "L0_ffn_ln_g", "L0_ffn_ln_b",
        "L0_ffn_w1", "L0_ffn_b1", "L0_ffn_w2", "L0_ffn_b2"]


def kernel(**inputs):
    import concourse.bacc as _bacc
    from concourse.bass_utils import run_bass_kernel_spmd as _run

    nc = _bacc.Bacc("TRN2", target_bir_lowering=False, num_devices=1)
    cst, tab, mask = constants()
    arrays = {"k_cst": cst, "k_tab": tab, "k_mask": mask}
    arrays.update({n: np.ascontiguousarray(inputs[n]) for n in _INS})
    aps = {n: nc.dram_tensor("in_" + n, v.shape, mybir.dt.from_np(v.dtype), kind="ExternalInput").ap()
           for n, v in arrays.items()}
    out = nc.dram_tensor("out_0", (NB, T, D), F32, kind="ExternalOutput").ap()
    program(nc, aps, out)
    r = _run(nc, [{"in_" + n: v for n, v in arrays.items()}], core_ids=[0])
    return r.results[0]["out_0"]
```

```python
from contextlib import ExitStack

import concourse.bass as bass
import numpy as np
from concourse import mybir

F32 = mybir.dt.float32
BF16 = mybir.dt.bfloat16
ALU = mybir.AluOpType
ACT = mybir.ActivationFunctionType
AX = mybir.AxisListType

P = 128
NB = 4
T = 1024
NT = T // P
D = 128
RH, RD = 16, 8
BL = 32
NBL = P // BL
NG = 4
DEPTH = 2
H, DH = 8, 64
INNER = H * DH
WIN = 64
HID = int(D * 4 * 2 / 3)
CHUNKS = [(0, 128), (128, 128), (256, HID - 256)]
NC = len(CHUNKS)
EPS = 1e-5
MASKED = -1e30

C_ID, C_GRP, C_GQ, C_GK, C_BD, C_VM, C_CAUSAL = 0, 128, 256, 384, 512, 640, 768
C_HM = C_CAUSAL + BL
C_GM, C_SD = C_HM + NG, C_HM + 2 * NG
C_END = C_SD + 1


def constants():
    f = np.float32
    cst = np.zeros((P, C_END), f)
    i = np.arange(P)
    cst[:, C_ID:C_ID + P] = np.eye(P)
    cst[:, C_GRP:C_GRP + P] = (i[:, None] // RD == i[None, :] // RD) / RD
    cst[:, C_CAUSAL:C_CAUSAL + BL] = i[:, None] % BL <= i[None, :BL]
    lin = np.linspace(np.log(1.0 / 32.0), np.log(1.0 / 512.0), RH).astype(f)
    gam = (f(1.0) - np.exp(lin)).astype(np.float64)
    head = i // RD
    cst[:, C_GQ:C_GQ + P] = gam[head][None, :] ** i[:, None] / np.sqrt(RD)
    cst[:, C_GK:C_GK + P] = gam[head][None, :] ** (-i[:, None].astype(np.float64))
    cst[:, C_BD:C_BD + P] = head[:, None] == head[None, :]
    cst[:, C_VM:C_VM + P] = i[:, None] // BL == head[None, :] % NG
    cst[:, C_HM:C_HM + NG] = head[:, None] % NG == np.arange(NG)[None, :]
    cst[:, C_GM:C_GM + NG] = head[:, None] // NG == np.arange(NG)[None, :]
    cst[:, C_SD] = gam[head] ** P
    half = np.arange(0, DH, 2, dtype=f)
    inv = (f(1.0) / np.power(f(10000.0), half / f(DH))).astype(f)
    t = np.arange(T, dtype=f)
    fr = t[:, None] * inv[None, :]
    fr = np.concatenate([fr, fr], -1)
    base = ((half + f(0.4 * DH)) / f(1.4 * DH)).astype(f)
    power = (t - f(T // 2)) / f(WIN // 2)
    sc = np.power(base[None, :], power[:, None]).astype(f)
    sc = np.concatenate([sc, sc], -1)
    sign = np.where(np.arange(DH) < DH // 2, -1.0, 1.0).astype(f)
    cos, sin = np.cos(fr), np.sin(fr) * sign
    tab = np.stack([cos * sc * f(8), cos / sc, sin * sc * f(8), sin / sc], 1).astype(f)
    tab = tab.reshape(NT, P, 4, DH).transpose(1, 0, 2, 3)
    own = (i[:WIN, None] >= i[None, :WIN])
    before = (i[:WIN, None] <= i[None, :WIN])
    even = np.concatenate([own, before], 1)
    odd = np.concatenate([before, own], 1)
    m = np.concatenate([even, odd], 0)
    first = m.copy()
    first[:WIN, WIN:] = False
    mask = np.where(np.stack([first, m], 1), 0.0, MASKED).astype(f)
    mask = np.concatenate([mask, np.eye(P, dtype=f)[:, None, :]], 1)
    return cst, np.ascontiguousarray(tab), np.ascontiguousarray(mask)


def need(eng, sem, value):
    if isinstance(value, int) and value <= 0:
        return
    eng.wait_ge(sem, value)


def program(nc, a, out):
    with ExitStack() as ctx:
        def sb(name, shape, dt=F32):
            return ctx.enter_context(nc.sbuf_tensor(name, shape, dt))

        def sem(name):
            return ctx.enter_context(nc.semaphore(name))

        cst = sb("cst", [P, C_END])
        ident = cst[:, C_ID:C_ID + P]
        group_avg = cst[:, C_GRP:C_GRP + P]
        causal = cst[:, C_CAUSAL:C_CAUSAL + BL]
        decay_q = cst[:, C_GQ:C_GQ + P]
        decay_k = cst[:, C_GK:C_GK + P]
        same_head = cst[:, C_BD:C_BD + P]
        value_mask = cst[:, C_VM:C_VM + P]
        place_mask = cst[:, C_HM:C_HM + NG]
        group_mask = cst[:, C_GM:C_GM + NG]
        state_decay = cst[:, C_SD:C_SD + 1]
        hidden = sb("hidden", [P, NC * NB * P])
        mask32 = hidden[:, 0:3 * P].rearrange("p (s n) -> p s n", s=3)
        mask16 = sb("mask16", [P, 3, P], BF16)
        tab = sb("tab", [P, NT, 4, DH])
        gain = hidden[:, 3 * P:3 * P + DEPTH * 2 * DH].rearrange("p (l g d) -> p l g d", l=DEPTH, g=2)
        rope = [sb("rope0", [P, NT, 4, DH]), tab]
        warm = sb("warm", [P, 3])
        half_neg = sb("half_neg", [P, NB * NT])
        wqkv = sb("wqkv", [P, DEPTH, 3 * INNER])
        wo = sb("wo", [P, DEPTH, 4, D])
        w1 = sb("w1", [P, DEPTH, 2 * HID])
        w2 = sb("w2", [P, DEPTH, NC, D])
        b1c = sb("b1c", [P, DEPTH, 2, NC])
        b1e = sb("b1e", [P, DEPTH, 2, NC])
        col = sb("col", [P, 16])
        COLS = {"ng": 0, "nb": 1, "ob": 2, "fg": 3, "fb": 4, "b1a": 5, "b2a": 7,
                "lg": 8, "lb": 10, "b2": 12}

        def c(name, k=0):
            return col[:, COLS[name] + k:COLS[name] + k + 1]

        aT = sb("aT", [P, 8, P])

        x = sb("x", [P, NB, NT, D])
        x1T = x[:, :, :, :].rearrange("p b t d -> p b (t d)")
        xnT = sb("xnT", [P, NB, 1 + T])
        x2T = sb("x2T", [P, NB, 1 + T])

        mv = sb("mv", [P, NT, NB, 2])
        vpe = sb("vpe", [P, NT, NB])
        rstd = sb("rstd", [P, NT, NB])
        cbst = [sb("cbst0", [P, NB, 2, 6]), sb("cbst1", [P, NB, NT, 6])]
        xst = cbst[1]
        cmv = sb("cmv", [P, NB, 2])
        cst2 = sb("cst2", [P, 2, NB])
        gst = sb("gst", [P, 2, NB])
        gtmp = sb("gtmp", [P, 2, NB])
        grs = sb("grs", [P, NB])
        gsc = [sb(f"gsc{k}", [P, NB]) for k in range(2)]
        gsh = [sb(f"gsh{k}", [P, NB]) for k in range(2)]

        hT = sb("hT", [P, NB, P])
        sq = sb("sq", [P, 2 * INNER])
        ss = sb("ss", [P, 2, 2 * H])
        rn = sb("rn", [P, 2, 2 * H])
        m1 = sb("m1", [P, 2, 2 * INNER])
        m2 = sb("m2", [P, 2, 2 * INNER])
        qkn = sb("qkn", [P, 2, 2 * INNER])
        xn = m1[:, :, 0:NB * D].rearrange("p u (b d) -> p u b d", b=NB)
        qT = sb("qT", [P, 4, P])
        kT = [sb(f"kT{b}", [P, 4, P + WIN]) for b in range(NB)]
        vown = [sb(f"vown{b}", [P, H, DH + 1]) for b in range(NB)]
        vmix = [sb(f"vmix{b}", [P, H, DH + 1]) for b in range(NB)]
        mx = sb("mx", [P, H])
        pr = sb("pr", [P, 2, H, P])
        prT = sb("prT", [P, H, P])
        rec = sb("rec", [P, 2, 4])
        o = sb("o", [P, INNER])
        oT = sb("oT", [P, 4, P])
        xr = sb("xr", [P, NB, 1 + P])
        lmv = sb("lmv", [P, NB, 2])
        lbst = sb("lbst", [P, NB, 6])
        lvar = sb("lvar", [P, NB])
        lrs = sb("lrs", [P, NB])
        hn = sb("hn", [P, NB, D])
        hs = hn
        hnT = sb("hnT", [P, NB * P])
        gg = sb("gg", [P, 2, NB * P])
        hf = hidden[:, :].rearrange("p (k n) -> p k n", k=NC)
        xa = sb("xa", [P, NB, P])
        xa4 = sb("xa4", [P, 2, NBL, NG, BL])
        asq = sb("asq", [P, P])
        ass = sb("ass", [P, 2, 2])
        ars = sb("ars", [P, 2, 2])
        aqk = sb("aqk", [P, 2, 2, P])
        av = sb("av", [P, 2, P])
        aqkT = sb("aqkT", [P, 2, 2, P])
        araw = pr[:, :, :, :].rearrange("p u h n -> p (u h) n")[:, 0:8, :]
        state = sb("state", [P, NB, P])
        vx = m2[:, 0, :].rearrange("p (u c n) -> p u c n", u=2, c=NBL)
        kx = sq[:, :].rearrange("p (u c j n) -> p u c j n", u=2, c=NBL, j=NG)
        qx = prT[:, :, :].rearrange("p h n -> p (h n)").rearrange("p (u c g n) -> p u c g n", u=2, c=NBL, g=NG)
        sm = m1[:, 0, :].rearrange("p (u c g n) -> p u c g n", u=2, c=NBL, g=NG)
        before = hidden[:, 0:2 * NBL * P].rearrange("p (u c n) -> p u c n", u=2, c=NBL)
        ayT = gg[:, 0, :]
        afh = xa4[:, :, :, :, :].rearrange("p s c g n -> p s (c g n)")
        att = state
        fin = aqk[:, :, :, :].rearrange("p u g n -> p (u g) n")
        xs = sb("xs", [P, NB, D])
        osb = aqkT[:, :, :, :].rearrange("p u g n -> p (u g) n")

        pQK = ctx.enter_context(nc.psum_tensor("pQK", [P, 1024], F32))
        pV = ctx.enter_context(nc.psum_tensor("pV", [P, 512], F32))
        pT = ctx.enter_context(nc.psum_tensor("pT", [P, 1024], F32))
        pS = ctx.enter_context(nc.psum_tensor("pS", [P, 1024], F32))
        pM = ctx.enter_context(nc.psum_tensor("pM", [P, 512], F32))

        ffn_banks = (pT, pS, pT)
        xn_banks = (pM, pV)
        y_banks = (pT, pS)


        def score_bank(b):
            return pS[:, 512:1024] if b == 0 else pQK[:, 0:512]

        x_ld = [sem(f"x_ld{b}") for b in range(NB)]
        cst_ld, tab_ld, aw_ld, wqkv_ld, w1_ld, w_ld, gain_ld, col_ld = (
            sem(n) for n in ("cst_ld", "tab_ld", "aw_ld", "wqkv_ld", "w1_ld", "w_ld", "gain_ld", "col_ld"))
        memset_done, mask_done = sem("memset_done"), sem("mask_done")
        xst_done, st_done, var_done, rstd_done, xn_done, xnt_mm, xnt_ev, cs_done = (
            sem(n) for n in ("xst_done", "st_done", "var_done", "rstd_done", "xn_done", "xnt_mm", "xnt_ev", "cs_done"))
        awt_mm, awt_ev, be_mm, be_done, w1g_done, rope_done = (
            sem(n) for n in ("awt_mm", "awt_ev", "be_mm", "be_done", "w1g_done", "rope_done"))
        gn = [{n: sem(f"gn{k}_{n}") for n in ("agg", "dve", "mm", "var", "rs", "done")} for k in range(2)]
        LS = {n: sem(n) for n in (
            "carried", "v_kept", "h_ready", "qk_mm", "v_mm", "sq_done", "ss_done", "mul_done", "max_ss", "rn_done", "add_done",
            "qkn_done", "t_mm", "t_ev", "v_ev", "s_mm", "mx_done", "sub_done", "exp_done",
            "pt_mm", "pt_ev", "o_mm", "rec_done", "o_done", "ot_mm", "ot_ev", "wo_mm", "xr_carried", "xr_done", "hs",
            "ln_mm", "ln_bst", "ln_st", "ln_eps", "ln_rs", "hn_done", "hnt_mm", "hnt_ev", "ag_mm", "gelu_done",
            "hf_done", "w2_mm", "x2_done")}
        A = {n: sem(f"a_{n}") for n in (
            "xa", "xa4", "qkv_mm", "sqq", "v", "floor", "rs", "qk", "t_mm", "t_ev", "vx_mm", "vx", "kx", "qx", "st_mm", "sm",
            "kv_mm", "kvm", "before", "y_mm", "yt", "state", "ow_mm", "x1", "cs")}
        G = {n: sem(f"g_{n}") for n in ("xa", "w1_mm", "silu", "w2_mm", "att", "fin", "fin_mm", "xs", "osb", "out")}

        x_steps = a["L0_attn_x"].rearrange("b (t p) d -> t p b d", p=P)
        out_steps = out.rearrange("b (t p) d -> t p b d", p=P)
        block = ctx.enter_context(nc.Block())

        def need_apart(eng, sem, value):
            if isinstance(value, int):
                return need(eng, sem, value)
            register = eng.to_reg(value)
            eng.wait_ge(cst_ld, 32)
            eng.wait_ge(sem, register)

        def is_second_norm(new, k):
            return new and new[0] == 1 and isinstance(new[1], int) and (new[1], k) == (0, 3)

        def step_count(step):
            return NT * step[0] + step[1]

        def count(step, b):
            return NB * step_count(step) + b

        def is_first(step):
            return isinstance(step[1], int) and step[1] == 0

        def is_start(step):
            return step[0] == 0 and is_first(step)

        def at(new, old, k):
            step = new if k >= 0 else old
            return (step, k % NB, count(step, k % NB)) if step else None

        def run_bodies(eng, body):
            body((0, 0), None, None)
            body((0, 1), (0, 0), None)
            with eng.Fori(2, NT) as t:
                body((0, t), (0, t - 1), (0, t - 2))
            body((1, 0), (0, NT - 1), (0, NT - 2))
            body((1, 1), (1, 0), (0, NT - 1))
            with eng.Fori(2, NT) as t:
                body((1, t), (1, t - 1), (1, t - 2))
            body(None, (1, NT - 1), (1, NT - 2))
            body(None, None, (1, NT - 1))

        @block.sync
        def _(sp):
            for b in range(NB):
                sp.dma_start(x[:, b, :, :], a["L0_attn_x"][b].rearrange("(t p) d -> p t d", p=P)).then_inc(x_ld[b], 16)
            sp.dma_start(tab[:, :, :, :], a["k_tab"]).then_inc(tab_ld, 16)
            sp.dma_start(wqkv[:, 0, :], a["L0_ffn_wqkv"][0]).then_inc(wqkv_ld, 16)
            for l in range(DEPTH):
                sp.dma_start(w1[:, l, :], a["L0_ffn_w1"][l]).then_inc(w1_ld, 16)
            sp.dma_start(wqkv[:, 1, :], a["L0_ffn_wqkv"][1]).then_inc(w_ld, 16)
            for l in range(DEPTH):
                sp.dma_start(wo[:, l, :, :], a["L0_ffn_wo"][l].rearrange("(c p) d -> p c d", p=P)).then_inc(w_ld, 16)
                sp.dma_start(w2[:, l, 0:2, :], a["L0_ffn_w2"][l, 0:2 * P, :].rearrange("(c p) d -> p c d", p=P)).then_inc(w_ld, 16)
                sp.dma_start(w2[0:CHUNKS[2][1], l, 2, :], a["L0_ffn_w2"][l, 2 * P:HID, :]).then_inc(w_ld, 16)
            sp.dma_start(xs[:, :, :], x_steps[0]).then_inc(G["xs"], 16)
            sp.wait_ge(G["osb"], 1)
            sp.dma_start(out_steps[0], osb[:, :, :]).then_inc(G["out"], 16)
            with sp.Fori(1, NT) as t:
                sp.wait_ge(G["out"], 16 * t)
                sp.dma_start(xs[:, :, :], x_steps[t]).then_inc(G["xs"], 16)
                sp.wait_ge(G["osb"], t + 1)
                sp.dma_start(out_steps[t], osb[:, :, :]).then_inc(G["out"], 16)
            sp.wait_ge(G["out"], 16 * NT)

        def pool_slot(eng, new, old, k):
            S = LS
            if old and k == 0 and not is_start(old):
                need_apart(eng, S["hs"], 2 * step_count(old))
                if is_first(old):
                    eng.memset(xr[:, :, 0:1], 0.0).then_inc(S["xr_carried"], 1)
                else:
                    eng.tensor_copy(xr[:, :, 0:1], xr[:, :, P:P + 1]).then_inc(S["xr_carried"], 1)
            retain = k == NB - 1 and new and new[0] == 0
            if retain:
                pool_retention_norm(eng, new[1], 0)
                return
            if old and k == NB - 1:
                pool_ln(eng, old)
            if new:
                n = count(new, k)
                pool_norm(eng, n, k)
                pool_add(eng, n, k)
                pool_scale(eng, n, k)

        def pool_norm(eng, n, k):
            S = LS
            need_apart(eng, S["ss_done"], n + 1)
            eng.tensor_scalar(rn[:, k % 2, :], ss[:, k % 2, :], 1e-24, None, ALU.max).then_inc(S["max_ss"], 1)
            eng.wait_ge(S["max_ss"], n + 1)
            eng.tensor_tensor(rn[:, k % 2, :], rn[:, k % 2, :], half_neg[:, 0:2 * H], ALU.pow).then_inc(S["rn_done"], 1)

        def pool_ln(eng, step):
            S, ct = LS, step_count(step)
            need_apart(eng, S["ln_st"], NB * ct + NB)
            eng.tensor_scalar(lvar[:, :], lmv[:, :, 1], EPS, None, ALU.add).then_inc(S["ln_eps"], 1)
            eng.wait_ge(S["ln_eps"], ct + 1)
            eng.tensor_tensor(lrs[:, :], lvar[:, :], half_neg[:, 0:NB], ALU.pow).then_inc(S["ln_rs"], 1)

        def pool_add(eng, n, k):
            S = LS
            eng.wait_ge(S["mul_done"], 2 * n + 2)
            eng.tensor_tensor(m1[:, k % 2, :], m1[:, k % 2, :], m2[:, k % 2, :], ALU.add).then_inc(S["add_done"], 1)

        def pool_scale(eng, n, k):
            S = LS
            eng.wait_ge(S["add_done"], n + 1)
            eng.wait_ge(S["rn_done"], n + 1)
            need(eng, S["t_mm"], 2 * (n - 1))
            eng.tensor_tensor(qkn[:, k % 2, :].rearrange("p (h d) -> p h d", d=DH),
                              m1[:, k % 2, :].rearrange("p (h d) -> p h d", d=DH),
                              rn[:, k % 2, :].unsqueeze(2).broadcast_to([P, 2 * H, DH]),
                              ALU.mult).then_inc(S["qkn_done"], 1)

        def pool_retention_norm(eng, t, b):
            n = 4 * t + b
            need_apart(eng, A["sqq"], 2 * n + 2)
            eng.tensor_scalar(ars[:, b % 2, :], ass[:, b % 2, :], 1e-24, None, ALU.max).then_inc(A["floor"], 1)
            eng.wait_ge(A["floor"], n + 1)
            eng.tensor_tensor(ars[:, b % 2, :], ars[:, b % 2, :], half_neg[:, 0:2], ALU.pow).then_inc(A["rs"], 1)

        def pool_retention(eng, t, old):
            last = NB - 1
            n = count((0, t), last)
            eng.wait_ge(LS["ss_done"], n + 1)
            for b in range(NB):
                pool_mask_qk(eng, t, b)
                if b < last:
                    pool_retention_norm(eng, t, b + 1)
            if old:
                pool_ln(eng, old)
            pool_norm(eng, n, last)
            pool_add(eng, n, last)
            pool_scale(eng, n, last)

        def pool_mask_qk(eng, t, b):
            n = 4 * t + b
            shape = [P, NBL, NG, BL]
            eng.wait_ge(A["t_ev"], n + 1)
            need(eng, A["st_mm"], n - 1)
            eng.tensor_tensor(kx[:, b % 2, :, :, :],
                              aqkT[:, b % 2, 1, :].rearrange("p (c n) -> p c n", c=NBL).unsqueeze(2).broadcast_to(shape),
                              place_mask.unsqueeze(1).unsqueeze(3).broadcast_to(shape), ALU.mult).then_inc(A["kx"], 1)
            need(eng, A["y_mm"], n - 1)
            eng.tensor_tensor(qx[:, b % 2, :, :, :],
                              aqkT[:, b % 2, 0, :].rearrange("p (c n) -> p c n", c=NBL).unsqueeze(2).broadcast_to(shape),
                              group_mask.unsqueeze(1).unsqueeze(3).broadcast_to(shape), ALU.mult).then_inc(A["qx"], 1)

        def pool_group_norm(eng, k):
            g = gn[k]
            eng.wait_ge(g["var"], 1)
            eng.tensor_tensor(grs[:, :], gtmp[:, 0, :], half_neg[:, 0:NB], ALU.pow).then_inc(g["rs"], 1)

        @block.gpsimd
        def _(eng):
            eng.memset(half_neg[:, :], -0.5).then_inc(memset_done, 1)
            eng.memset(state[:, :, :], 0.0).then_inc(memset_done, 1)
            eng.memset(xnT[:, :, 0:1], 0.0).then_inc(memset_done, 1)
            eng.memset(x2T[:, :, 0:1], 0.0).then_inc(memset_done, 1)
            for b in range(NB):
                eng.memset(kT[b][:, :, P:P + WIN], 0.0).then_inc(memset_done, 1)
                eng.memset(vmix[b][:, :, 0:DH], 0.0).then_inc(memset_done, 1)
                eng.memset(vown[b][:, :, DH:DH + 1], 1.0).then_inc(memset_done, 1)
                eng.memset(vmix[b][:, :, DH:DH + 1], 1.0).then_inc(memset_done, 1)
            eng.memset(xr[:, :, 0:1], 0.0).then_inc(memset_done, 1)
            eng.wait_ge(memset_done, 5 + 4 * NB)
            for half in range(2):
                steps = slice(half * NT // 2, (half + 1) * NT // 2)
                eng.wait_ge(st_done, NB * steps.stop)
                eng.tensor_scalar(vpe[:, steps, :], mv[:, steps, :, 1], EPS, None, ALU.add).then_inc(var_done, 1)
                eng.wait_ge(var_done, half + 1)
                eng.tensor_tensor(rstd[:, steps, :], vpe[:, steps, :],
                                  half_neg[:, :].rearrange("p (t b) -> p t b", b=NB)[:, steps, :],
                                  ALU.pow).then_inc(rstd_done, 1)
            eng.wait_ge(tab_ld, 16)
            eng.wait_ge(gain_ld, 16 * 4)
            for l in range(DEPTH):
                for g in range(2):
                    eng.tensor_tensor(rope[l][:, :, g, :], tab[:, :, g, :],
                                      gain[:, l, g, :].unsqueeze(1).broadcast_to([P, NT, DH]),
                                      ALU.mult).then_inc(rope_done, 1)
                    for s in range(2):
                        eng.tensor_tensor(rope[l][:, :, 2 + g, 32 * s:32 * s + 32], tab[:, :, 2 + g, 32 * s:32 * s + 32],
                                          gain[:, l, g, 32 - 32 * s:64 - 32 * s].unsqueeze(1).broadcast_to([P, NT, 32]),
                                          ALU.mult).then_inc(rope_done, 1)

            def body(new, old, ff):
                for k in range(NB):
                    if k == 1 and new and is_start(new):
                        pool_group_norm(eng, 0)
                    if is_second_norm(new, k):
                        pool_group_norm(eng, 1)
                    pool_slot(eng, new, old, k)
                if new and new[0] == 0:
                    pool_retention(eng, new[1], old)

            run_bodies(eng, body)

        def act_load_table(eng, function):
            place = (ACT.Gelu, ACT.Silu, ACT.Exp).index(function)
            eng.activation(warm[:, place:place + 1], half_neg[:, 0:1], function)

        def act_shift(eng, step, b):
            src = xnT if step[0] == 0 else x2T
            need(eng, LS["qk_mm"], count(step, b) - 3)
            for rows, back in ((slice(0, 64), 0), (slice(64, P), 1)):
                eng.activation(hT[rows, b, :], src[rows, b, bass.ds(step[1] * P + 1 - back, P)],
                               ACT.Copy).then_inc(LS["h_ready"], 1)

        def act_slot(eng, new, old, ff, k):
            S = LS
            if new:
                n = count(new, k)
                if k == 0:
                    if new[0] == 1:
                        eng.wait_ge(S["x2_done"], new[1] + 1)
                    act_shift(eng, new, 0)
            turned = at(new, old, k - 2)
            if turned:
                step, b, m = turned
                eng.wait_ge(S["t_mm"], 2 * m + 1)
                if not is_start(step):
                    eng.wait_ge(S["carried"], m - 3)
                eng.activation(kT[b][:, :, 0:P], pT[:, 512:1024].rearrange("p (c n) -> p c n", c=4), ACT.Copy).then_inc(S["t_ev"], 1)
                eng.wait_ge(S["t_mm"], 2 * m + 2)
                eng.activation(qT[:, :, :], pT[:, 0:512].rearrange("p (c n) -> p c n", c=4), ACT.Copy).then_inc(S["t_ev"], 1)
            if new:
                if not is_start(new):
                    need(eng, S["o_mm"], n - 3)
                    eng.activation(vmix[k][64:P, :, 0:DH], vown[k][64:P, :, 0:DH], ACT.Copy).then_inc(S["v_kept"], 1)
                    eng.activation(kT[k][:, :, P:P + WIN], kT[k][:, :, WIN:P], ACT.Copy).then_inc(S["carried"], 1)
                if k < NB - 1:
                    act_shift(eng, new, k + 1)
                eng.wait_ge(S["v_mm"], n + 1)
                if not is_start(new):
                    eng.wait_ge(S["v_kept"], n - 3)
                values = pV[:, :].rearrange("p (h d) -> p h d", h=H)
                eng.activation(vown[k][:, :, 0:DH], values, ACT.Copy).then_inc(S["v_ev"], 1)
                eng.activation(vmix[k][0:64, :, 0:DH], values[0:64], ACT.Copy).then_inc(S["v_ev"], 1)
            if ff and ff[0] == 1 and k == 1:
                act_block_ffn(eng, ff[1])
                act_load_table(eng, ACT.Exp)
            weighted = at(new, old, k - 3)
            if weighted:
                eng.wait_ge(S["pt_mm"], weighted[2] + 1)
                eng.activation(prT[:, :, :], pT[:, :].rearrange("p (h n) -> p h n", h=H), ACT.Copy).then_inc(S["pt_ev"], 1)
            if k > 0:
                act_output(eng, old, k)
            if ff and k == 0:
                eng.wait_ge(S["hnt_mm"], step_count(ff) + 1)
                eng.activation(hnT[:, :], pM[:, :], ACT.Copy).then_inc(S["hnt_ev"], 1)
            if k == NB - 1 and new and new[0] == 0:
                act_retention_project(eng, new[1], 0)
            if k == 0 and turned:
                act_exp(eng, b, m)
            if k == 0 and ff:
                act_load_table(eng, ACT.Gelu)
                act_gelu(eng, ff, 0)
            if new:
                eng.wait_ge(S["qk_mm"], n + 1)
                need(eng, S["ss_done"], n)
                eng.activation(sq[:, :], pQK[:, :], ACT.Square).then_inc(S["sq_done"], 1)
            if k == 0:
                if ff:
                    act_gelu(eng, ff, 1)
                act_output(eng, old, 0)
                if ff:
                    act_gelu(eng, ff, 2)
                    act_load_table(eng, ACT.Silu if ff[0] == 1 else ACT.Exp)
            if not (k == NB - 1 and new and new[0] == 0):
                if old and k == NB - 1:
                    act_shift_residual(eng, old)
                if k > 0 and turned:
                    act_exp(eng, b, m)

        def act_shift_residual(eng, step):
            S = LS
            eng.wait_ge(S["xr_done"], count(step, NB - 1) + 1)
            need(eng, S["hnt_mm"], step_count(step))
            eng.activation(hs[0:64, :, :], xr[0:64, :, 1:1 + P], ACT.Copy).then_inc(S["hs"], 1)
            eng.activation(hs[64:P, :, :], xr[64:P, :, 0:P], ACT.Copy).then_inc(S["hs"], 1)

        def act_exp(eng, b, n):
            eng.wait_ge(LS["sub_done"], n + 1)
            eng.activation(pr[:, b % 2, :, :], pr[:, b % 2, :, :], ACT.Exp).then_inc(LS["exp_done"], 1)

        def act_output(eng, step, b):
            if step:
                eng.wait_ge(LS["ot_mm"], count(step, b) + 1)
                bank = pV if b == 0 else pM
                eng.activation(oT[:, :, :], bank[:, :].rearrange("p (c n) -> p c n", c=4), ACT.Copy).then_inc(LS["ot_ev"], 1)

        def act_gelu(eng, step, k):
            S, l, ct, m = LS, step[0], step_count(step), CHUNKS[k][1]
            eng.wait_ge(S["ag_mm"], NC * ct + k + 1)
            if k >= 2:
                eng.wait_ge(S["hf_done"], NC * ct + k - 1)
            eng.activation(gg[0:m, k % 2, :], ffn_banks[k][0:m, 512:1024], ACT.Gelu,
                           bias=b1e[0:m, l, 1, k:k + 1]).then_inc(S["gelu_done"], 1)

        def act_retention_project(eng, t, b):
            n = 4 * t + b
            if b == 0:
                eng.wait_ge(A["xa"], 4 * t + 4)
            need(eng, A["vx_mm"], n - 1)
            eng.activation(xa4[:, b % 2, :, :, :],
                           xa[:, b, :].rearrange("p (c n) -> p c n", c=NBL).unsqueeze(2).broadcast_to(
                               [P, NBL, NG, BL]), ACT.Copy).then_inc(A["xa4"], 1)
            eng.wait_ge(A["qkv_mm"], n + 1)
            need(eng, A["rs"], n - 1)
            for g in range(2):
                need(eng, A["sqq"], 2 * n + g)
                eng.activation(asq[:, :], pV[:, g * P:(g + 1) * P], ACT.Square,
                               accum_out=ass[:, b % 2, g:g + 1]).then_inc(A["sqq"], 1)
            need(eng, A["kv_mm"], n - 1)
            eng.activation(av[:, b % 2, :], pV[:, 2 * P:3 * P], ACT.Copy).then_inc(A["v"], 1)

        def act_retention(eng, t, old):
            for k in range(NB + 1):
                if k < NB:
                    n = 4 * t + k
                    eng.wait_ge(A["t_mm"], n + 1)
                    need(eng, A["qx"], n - 1)
                    eng.activation(aqkT[:, k % 2, :, :], pM[:, 0:256].rearrange("p (g n) -> p g n", g=2),
                                   ACT.Copy).then_inc(A["t_ev"], 1)
                if k + 1 < NB:
                    act_retention_project(eng, t, k + 1)
                if k == 0:
                    act_exp(eng, 1, count((0, t), 1))
                    if old:
                        act_shift_residual(eng, old)
                if k > 0:
                    b = k - 1
                    eng.wait_ge(A["y_mm"], 4 * t + b + 1)
                    for g in range(NG):
                        r = slice(BL * g, BL * g + BL)
                        eng.activation(ayT[r, b * P:(b + 1) * P].rearrange("p (c n) -> p c n", c=NBL),
                                       y_banks[b % 2][r, 512:1024].rearrange("p (c g n) -> p c g n", c=NBL, g=NG)[:, :, g, :],
                                       ACT.Copy).then_inc(A["yt"], 1)

        def act_block_ffn(eng, t):
            for j in range(2):
                eng.wait_ge(G["w1_mm"], 2 * t + j + 1)
                eng.activation(afh[:, j, :], pQK[:, j * 512:(j + 1) * 512], ACT.Silu, bias=c("b1a", j)).then_inc(G["silu"], 1)

        @block.scalar
        def _(eng):
            eng.dma_start(cst[:, :], a["k_cst"]).then_inc(cst_ld, 16)
            eng.dma_start(mask32[:, :, :], a["k_mask"]).then_inc(cst_ld, 16)
            for k, n in enumerate(("qw", "kw", "vw", "ow")):
                eng.dma_start(araw[:, k, :], a["L0_attn_" + n]).then_inc(aw_ld, 16)
            eng.dma_start(araw[:, 4:6, :], a["L0_attn_w1"].rearrange("(c p) d -> p c d", p=P)).then_inc(aw_ld, 16)
            eng.dma_start(araw[:, 6:8, :], a["L0_attn_w2"].rearrange("p (c d) -> p c d", c=2)).then_inc(aw_ld, 16)

            def column(name, ap, k=1):
                with nc.allow_non_contiguous_dma(reason="one value per partition"):
                    eng.dma_start(col[:, COLS[name]:COLS[name] + k], ap).then_inc(col_ld, 16)
            for name, arg in (("ng", "norm_g"), ("nb", "norm_b"), ("ob", "ob"), ("fg", "ffn_norm_g"),
                              ("fb", "ffn_norm_b"), ("b2a", "b2")):
                column(name, a["L0_attn_" + arg].rearrange("(p o) -> p o", o=1))
            column("b1a", a["L0_attn_b1"].rearrange("(c p) -> p c", p=P), 2)
            for name, arg in (("lg", "ln_g"), ("lb", "ln_b"), ("b2", "b2")):
                column(name, a["L0_ffn_" + arg].rearrange("l p -> p l"), 2)
            for g, n in enumerate(("q_scale", "k_scale")):
                for l in range(DEPTH):
                    eng.dma_start(gain[:, l, g, :], a["L0_ffn_" + n][l:l + 1, :].broadcast_to([P, DH])).then_inc(gain_ld, 16)
            with nc.allow_non_contiguous_dma(reason="one value per partition"):
                for l in range(DEPTH):
                    for s in range(2):
                        row = a["L0_ffn_b1"][l, s * HID:(s + 1) * HID]
                        eng.dma_start(b1c[:, l, s, 0:2], row[0:256].rearrange("(c p) -> p c", p=P)).then_inc(col_ld, 16)
                        eng.dma_start(b1c[0:HID - 256, l, s, 2:3], row[256:HID].rearrange("(p o) -> p o", o=1)).then_inc(col_ld, 16)
            for g in range(2):
                eng.wait_ge(awt_mm, g + 1)
                eng.activation(aT[:, 4 * g:4 * g + 4, :], pT[:, 512 * g:512 * g + 512].rearrange("p (k n) -> p k n", k=4),
                               ACT.Copy).then_inc(awt_ev, 1)
            eng.wait_ge(memset_done, 3)
            with eng.Fori(0, NT // 2) as half:
                for u in range(2):
                    t = 2 * half + u
                    eng.wait_ge(xnt_mm, t + 1)
                    eng.activation(xnT[:, :, bass.ds(t * P + 1, P)], xn_banks[u][:, :].rearrange("p (b n) -> p b n", b=NB),
                                   ACT.Copy).then_inc(xnt_ev, 1)
            eng.wait_ge(memset_done, 5 + 4 * NB)

            def body(new, old, ff):
                for k in range(NB):
                    if k == NB - 1 and new and is_start(new):
                        eng.wait_ge(be_done, 2)
                        eng.wait_ge(col_ld, 16 * 18)
                    act_slot(eng, new, old, ff, k)
                if new and new[0] == 0:
                    act_retention(eng, new[1], old)

            run_bodies(eng, body)

        def dve_rotate(eng, step, k, weighted, ff=None, normed=None):
            S, (l, t), n = LS, step, count(step, k)
            qk = pQK[:, :].rearrange("p (g h d) -> p g h d", g=2, h=H)
            rot = pQK[:, :].rearrange("p (g h s d) -> p g h s d", g=2, h=H, s=2)[:, :, :, ::-1, :]
            cos = rope[l][:, t, 0:2, :].unsqueeze(2).broadcast_to([P, 2, H, DH])
            sin = rope[l][:, t, 2:4, :].rearrange("p g (s d) -> p g s d", s=2).unsqueeze(2).broadcast_to([P, 2, H, 2, 32])
            if ff:
                dve_hidden(eng, ff, 0)
            eng.wait_ge(S["sq_done"], n + 1)
            need(eng, S["max_ss"], n - 1)
            eng.tensor_reduce(ss[:, k % 2, :], sq[:, :].rearrange("p (h d) -> p h d", d=DH), AX.X,
                              ALU.add).then_inc(S["ss_done"], 1)
            if weighted:
                dve_output(eng, weighted[2])
            if k == NB - 1 and l == 1 and normed:
                dve_ln(eng, normed)
            need(eng, S["add_done"], n - 1)
            need(eng, S["qkn_done"], n - 1)
            for i, (m, src, by, sizes) in enumerate(((m1, qk, cos, {"d": DH}), (m2, rot, sin, {"s": 2, "d": 32}))):
                shape = "p (g h d) -> p g h d" if i == 0 else "p (g h s d) -> p g h s d"
                eng.tensor_tensor(m[:, k % 2, :].rearrange(shape, g=2, h=H, **sizes), src, by,
                                  ALU.mult).then_inc(S["mul_done"], 1)
                if i == 0 and ff:
                    dve_hidden(eng, ff, 1)

        def dve_scores(eng, b, n):
            S = LS
            eng.wait_ge(S["s_mm"], n + 1)
            sc = pS[:, :].rearrange("p (h n) -> p h n", h=H)
            eng.tensor_reduce(mx[:, :], sc, AX.X, ALU.max).then_inc(S["mx_done"], 1)
            eng.wait_ge(S["mx_done"], n + 1)
            eng.tensor_tensor(pr[:, b % 2, :, :], sc, mx[:, :].unsqueeze(2).broadcast_to([P, H, P]),
                              ALU.subtract).then_inc(S["sub_done"], 1)

        def dve_output(eng, n):
            S = LS
            po = pS[:, :].rearrange("p (g z) -> p g z", g=2)[:, :, 0:4 * (DH + 1)].rearrange("p g (h d) -> p g h d", h=4)
            eng.wait_ge(S["o_mm"], n + 1)
            eng.reciprocal(rec[:, :, :], po[:, :, :, DH]).then_inc(S["rec_done"], 1)
            eng.wait_ge(S["rec_done"], n + 1)
            eng.tensor_tensor(o[:, :].rearrange("p (c g d) -> p g c d", g=2, d=DH), po[:, :, :, 0:DH],
                              rec[:, :, :].unsqueeze(3).broadcast_to([P, 2, 4, DH]), ALU.mult).then_inc(S["o_done"], 1)

        def dve_residual(eng, step, b):
            S, (l, t), n = LS, step, count(step, b)
            src = xnT if l == 0 else x2T
            eng.wait_ge(S["wo_mm"], n + 1)
            if not is_start(step):
                eng.wait_ge(S["xr_carried"], step_count(step))
            eng.tensor_tensor(xr[:, b, 1:1 + P], (pV if b == 0 else pM)[:, 0:P], src[:, b, bass.ds(t * P + 1, P)],
                              ALU.add).then_inc(S["xr_done"], 1)

        def dve_slot(eng, new, old, ff, k):
            retain = k == NB - 1 and new and new[0] == 0
            if retain:
                dve_retention_in(eng, new[1])
            if ff and k == 0:
                dve_ln_apply(eng, ff)
            if old and k == 0 and old[0] == 0:
                dve_retention_out(eng, old[1])
            turned = at(new, old, k - 2)
            if turned:
                dve_scores(eng, turned[1], turned[2])
            if retain:
                dve_retention_qk(eng, new[1], 0)
            if k > 0 and old:
                dve_residual(eng, old, k)
            weighted = at(new, old, k - 3)
            if k == 0 and ff:
                if ff[0] == 1:
                    dve_block_in(eng, ff[1])
                if new:
                    dve_rotate(eng, new, 0, None, ff)
                else:
                    dve_hidden(eng, ff, 0)
                    dve_hidden(eng, ff, 1)
                dve_hidden(eng, ff, 2)
                if weighted:
                    dve_output(eng, weighted[2])
                dve_ffn_out(eng, ff)
            elif new:
                dve_rotate(eng, new, k, weighted, normed=old)
            elif weighted:
                dve_output(eng, weighted[2])
            if k == 0 and old:
                if ff:
                    eng.wait_ge(LS["x2_done"], step_count(ff) + 1)
                dve_residual(eng, old, 0)
            if ff and ff[0] == 1 and k == 1:
                dve_block_out(eng, ff[1])
            if ff and ff[0] == 1 and k == 2:
                dve_final(eng, ff[1])
            if old and not new and k == NB - 1:
                dve_ln(eng, old)

        def dve_ln(eng, step):
            S, ct = LS, step_count(step)
            eng.wait_ge(S["ln_mm"], ct + 1)
            for b in range(NB):
                eng.bn_stats(lbst[:, b, :], pM[:, b * D:(b + 1) * D]).then_inc(S["ln_bst"], 1)
            need_apart(eng, S["ln_bst"], NB * ct + NB)
            for b in range(NB):
                eng.bn_aggr(lmv[:, b, :], lbst[:, b, :]).then_inc(S["ln_st"], 1)

        def dve_ln_apply(eng, step):
            S, ct = LS, step_count(step)
            eng.wait_ge(S["ln_rs"], ct + 1)
            for b in range(NB):
                eng.tensor_scalar(hn[:, b, :], pM[:, b * D:(b + 1) * D], lmv[:, b, 0:1], lrs[:, b:b + 1],
                                  ALU.subtract, ALU.mult).then_inc(S["hn_done"], 1)

        def dve_hidden(eng, step, k):
            S, l, ct = LS, step[0], step_count(step)
            m, pag = CHUNKS[k][1], ffn_banks[k]
            eng.wait_ge(S["gelu_done"], NC * ct + k + 1)
            eng.scalar_tensor_tensor(out=hf[0:m, k, :], in0=pag[0:m, 0:512], scalar=b1e[0:m, l, 0, k:k + 1],
                                     in1=gg[0:m, k % 2, :], op0=ALU.add, op1=ALU.mult).then_inc(S["hf_done"], 1)

        def dve_ffn_out(eng, step):
            S, (l, t), ct = LS, step, step_count(step)
            eng.wait_ge(S["w2_mm"], ct + 1)
            dst = x2T[:, :, bass.ds(t * P + 1, P)] if l == 0 else fin[:, :, :]
            eng.scalar_tensor_tensor(out=dst, in0=pM[:, :].rearrange("p (b n) -> p b n", b=NB), scalar=c("b2", l),
                                     in1=xr[:, :, 1:1 + P], op0=ALU.add, op1=ALU.add).then_inc(S["x2_done"], 1)

        def dve_retention_in(eng, t):
            need(eng, A["qkv_mm"], 4 * t)
            for b in range(NB):
                eng.tensor_scalar(xa[:, b, :], xnT[:, b, bass.ds(t * P + 1, P)], gsc[0][:, b:b + 1], gsh[0][:, b:b + 1],
                                  ALU.mult, ALU.add).then_inc(A["xa"], 1)

        def dve_retention_qk(eng, t, b):
            n = 4 * t + b
            eng.wait_ge(A["rs"], n + 1)
            eng.wait_ge(A["v"], n + 1)
            need(eng, A["kv_mm"], n - 1)
            for g, dec in enumerate((decay_q, decay_k)):
                eng.scalar_tensor_tensor(out=aqk[:, b % 2, g, :], in0=pV[:, g * P:(g + 1) * P],
                                         scalar=ars[:, b % 2, g:g + 1], in1=dec, op0=ALU.mult,
                                         op1=ALU.mult).then_inc(A["qk"], 1)

        def dve_retention(eng, t, old):
            eng.wait_ge(LS["qkn_done"], 4 * t + 3)
            for k in range(NB + 1):
                if k < NB:
                    n = 4 * t + k
                    if k < NB - 1:
                        dve_retention_qk(eng, t, k + 1)
                    eng.wait_ge(A["vx_mm"], n + 1)
                    need(eng, A["y_mm"], n - 1)
                    eng.tensor_tensor(vx[:, k % 2, :, :], pT[:, 0:512].rearrange("p (c n) -> p c n", c=NBL),
                                      value_mask.unsqueeze(1).broadcast_to([P, NBL, P]), ALU.mult).then_inc(A["vx"], 1)
                    eng.wait_ge(A["kv_mm"], n + 1)
                    need(eng, A["state"], n - 1)
                    eng.tensor_tensor(before[:, k % 2, :, :], pS[:, 0:512].rearrange("p (c n) -> p c n", c=NBL),
                                      same_head.unsqueeze(1).broadcast_to([P, NBL, P]), ALU.mult).then_inc(A["kvm"], 1)
                    eng.wait_ge(A["kvm"], n + 1)
                    eng.tensor_tensor(before[:, k % 2, :, :], before[:, k % 2, :, :],
                                      state[:, k, :].unsqueeze(1).broadcast_to([P, NBL, P]), ALU.add).then_inc(A["before"], 1)
                if k == NB - 1:
                    dve_block_scores(eng, t, k)
                    if old:
                        dve_ln(eng, old)
                if k > 0:
                    b = k - 1
                    n = 4 * t + b
                    eng.wait_ge(A["y_mm"], n + 1)
                    eng.tensor_scalar(state[:, b, :], before[:, b % 2, NBL - 1, :], state_decay, None,
                                      ALU.mult).then_inc(A["state"], 1)
                if k < NB - 1:
                    dve_block_scores(eng, t, k)

        def dve_block_scores(eng, t, b):
            n = 4 * t + b
            eng.wait_ge(A["st_mm"], n + 1)
            eng.tensor_tensor(sm[:, b % 2, :, :, :],
                              score_bank(b).rearrange("p (c g n) -> p c g n", c=NBL, g=NG),
                              causal.unsqueeze(1).unsqueeze(1).broadcast_to([P, NBL, NG, BL]),
                              ALU.mult).then_inc(A["sm"], 1)

        def dve_retention_out(eng, t):
            eng.wait_ge(A["ow_mm"], t + 1)
            eng.scalar_tensor_tensor(out=x1T[:, :, bass.ds(t * P, P)], in0=pS[:, 0:512].rearrange("p (b n) -> p b n", b=NB),
                                     scalar=c("ob"), in1=xnT[:, :, bass.ds(t * P + 1, P)], op0=ALU.add,
                                     op1=ALU.add).then_inc(A["x1"], 1)
            eng.wait_ge(A["x1"], t + 1)
            for b in range(NB):
                eng.bn_stats(cbst[1][:, b, t, :], x1T[:, b, bass.ds(t * P, P)]).then_inc(A["cs"], 1)

        def dve_block_in(eng, t):
            for b in range(NB):
                eng.tensor_scalar(xa[:, b, :], x1T[:, b, bass.ds(t * P, P)], gsc[1][:, b:b + 1], gsh[1][:, b:b + 1],
                                  ALU.mult, ALU.add).then_inc(G["xa"], 1)

        def dve_block_out(eng, t):
            eng.wait_ge(G["w2_mm"], t + 1)
            eng.scalar_tensor_tensor(out=att[:, :, :], in0=pM[:, :].rearrange("p (b n) -> p b n", b=NB), scalar=c("b2a"),
                                     in1=x1T[:, :, bass.ds(t * P, P)], op0=ALU.add, op1=ALU.add).then_inc(G["att"], 1)
            eng.wait_ge(LS["x2_done"], NT + t + 1)
            eng.wait_ge(G["att"], t + 1)
            eng.tensor_tensor(fin[:, :, :], fin[:, :, :], att[:, :, :], ALU.add).then_inc(G["fin"], 1)

        def dve_final(eng, t):
            eng.wait_ge(G["fin_mm"], t + 1)
            eng.wait_ge(G["xs"], 16 * t + 16)
            eng.tensor_tensor(osb[:, :, :], pM[:, :].rearrange("p (b d) -> p b d", b=NB), xs[:, :, :],
                              ALU.add).then_inc(G["osb"], 1)

        def dve_group_norm(eng, k, gain_col, bias_col):
            g = gn[k]
            for b in range(NB):
                eng.bn_aggr(cmv[:, b, :], cbst[k][:, b, :, :]).then_inc(g["agg"], 1)
            eng.wait_ge(g["agg"], NB)
            steps = [0]

            def then(ins):
                steps[0] += 1
                ins.then_inc(g["dve"], 1)
                eng.wait_ge(g["dve"], steps[0])
            then(eng.tensor_copy(cst2[:, 0, :], cmv[:, :, 0]))
            then(eng.tensor_tensor(cst2[:, 1, :], cmv[:, :, 0], cmv[:, :, 0], ALU.mult))
            then(eng.tensor_tensor(cst2[:, 1, :], cst2[:, 1, :], cmv[:, :, 1], ALU.add))
            eng.wait_ge(g["mm"], 1)
            then(eng.tensor_copy(gst[:, :, :], (pM, pV)[k][:, 0:2 * NB].rearrange("p (s b) -> p s b", s=2)))
            then(eng.tensor_tensor(gtmp[:, 1, :], gst[:, 0, :], gst[:, 0, :], ALU.mult))
            then(eng.tensor_tensor(gtmp[:, 0, :], gst[:, 1, :], gtmp[:, 1, :], ALU.subtract))
            eng.tensor_scalar(gtmp[:, 0, :], gtmp[:, 0, :], EPS, None, ALU.add).then_inc(g["var"], 1)
            eng.wait_ge(g["rs"], 1)
            then(eng.tensor_scalar(gsc[k][:, :], grs[:, :], gain_col, None, ALU.mult))
            then(eng.tensor_tensor(gtmp[:, 1, :], gst[:, 0, :], gsc[k][:, :], ALU.mult))
            eng.tensor_scalar(gsh[k][:, :], gtmp[:, 1, :], -1.0, bias_col, ALU.mult, ALU.add).then_inc(g["done"], 1)
            eng.wait_ge(g["done"], 1)

        @block.vector
        def _(eng):
            for b in range(NB):
                eng.wait_ge(x_ld[b], 16)
                with eng.Fori(0, NT // 4) as quad:
                    for u in range(4):
                        t = 4 * quad + u
                        eng.bn_stats(xst[:, b, t, :], x[:, b, t, :]).then_inc(xst_done, 1)
            eng.wait_ge(xst_done, NB * NT)
            for t in range(NT):
                for b in range(NB):
                    eng.bn_aggr(mv[:, t, b, :], xst[:, b, t, :]).then_inc(st_done, 1)
            eng.wait_ge(cst_ld, 32)
            eng.tensor_copy(mask16[:, :, :], mask32[:, :, :]).then_inc(mask_done, 1)
            eng.wait_ge(rstd_done, 1)

            def normalize(half):
                for u in range(2):
                    t = 2 * half + u
                    need(eng, xnt_mm, t - 1)
                    for b in range(NB):
                        eng.tensor_scalar(xn[:, u, b, :], x[:, b, t, :], mv[:, t, b, 0:1], rstd[:, t, b:b + 1],
                                          ALU.subtract, ALU.mult).then_inc(xn_done, 1)
            for half in range(NT // 4):
                normalize(half)
            eng.wait_ge(rstd_done, 2)
            with eng.Fori(NT // 4, NT // 2) as half:
                normalize(half)
            eng.wait_ge(rope_done, 6 * DEPTH)

            def input_stats():
                eng.wait_ge(xnt_ev, NT)
                for b in range(NB):
                    for h in range(2):
                        eng.bn_stats(cbst[0][:, b, h, :], xnT[:, b, 1 + h * T // 2:1 + (h + 1) * T // 2]).then_inc(cs_done, 1)
                eng.wait_ge(cs_done, NB * 2)

            def bias_into_ffn():
                eng.wait_ge(w1_ld, 16 * DEPTH)
                eng.wait_ge(col_ld, 16 * (10 + 8))
                eng.wait_ge(be_mm, 1)
                pb = pM[:, 0:2 * DEPTH * NC].rearrange("p (l s k) -> p l s k", l=DEPTH, s=2)
                last = HID - 256
                eng.tensor_tensor(b1e[:, :, :, 0:2], pb[:, :, :, 0:2], b1c[:, :, :, 0:2], ALU.add).then_inc(be_done, 1)
                eng.tensor_tensor(b1e[0:last, :, :, 2], pb[0:last, :, :, 2], b1c[0:last, :, :, 2], ALU.add).then_inc(be_done, 1)

            def gain_into_ffn():
                for l in range(DEPTH):
                    eng.tensor_scalar(w1[:, l, :], w1[:, l, :], c("lg", l), None, ALU.mult).then_inc(w1g_done, 1)

            def body(new, old, ff):
                for k in range(NB):
                    if new and is_start(new):
                        if k == 0:
                            input_stats()
                        if k == 1:
                            bias_into_ffn()
                            dve_group_norm(eng, 0, c("ng"), c("nb"))
                    if is_second_norm(new, k):
                        eng.wait_ge(A["cs"], NB * NT)
                        dve_group_norm(eng, 1, c("fg"), c("fb"))
                    dve_slot(eng, new, old, ff, k)
                    if k == 2 and new and is_start(new):
                        gain_into_ffn()
                if new and new[0] == 0:
                    dve_retention(eng, new[1], old)

            run_bodies(eng, body)

        def pe_turn(eng, b, n):
            S = LS
            eng.wait_ge(S["qkn_done"], n + 1)
            need(eng, S["t_ev"], 2 * n)
            need(eng, S["pt_ev"], n - 1)
            for half in (1, 0):
                for j in range(4 * half, 4 * half + 4):
                    mm = eng.transpose(pT[:, j * P:(j + 1) * P], qkn[:, b % 2, j * P:(j + 1) * P], ident)
                mm.then_inc(S["t_mm"], 1)

        def pe_scores(eng, step, b, n):
            S = LS
            eng.wait_ge(S["t_ev"], 2 * n + 2)
            need(eng, S["sub_done"], n)
            need(eng, S["o_done"], n - 1)
            if b == 2:
                eng.wait_ge(A["x1"], step[1] + 1 if step[0] == 0 else NT)
            mask = mask16[:, 0 if is_first(step) else 1, :].unsqueeze(1).broadcast_to([P, 4, P])
            for g in range(2):
                eng.matmul(pS[:, g * 512:(g + 1) * 512], mask16[:, 2, :], mask, start=True, stop=False,
                           skip_group_check=True)
            kk = kT[b]
            for j in range(4):
                for g in range(2):
                    r = slice(64 * g, 64 * g + 64)
                    col0 = g * 512 + j * P
                    for w in range(2):
                        if w == 0:
                            keys = kk[r, j, :].rearrange("p (s n) -> p s n", n=WIN)[:, 0:3:2, :]
                        else:
                            keys = kk[r, j, 0:P]
                        mm = eng.matmul(pS[64 * w:64 * w + 64, col0:col0 + P], qT[r, j, 64 * w:64 * w + 64], keys,
                                        start=False, stop=True, skip_group_check=True)
            mm.then_inc(S["s_mm"], 1)

        def pe_turn_weights(eng, b, n, turned):
            S = LS
            eng.wait_ge(S["exp_done"], n + 1)
            need(eng, S["pt_ev"], n)
            if turned:
                eng.wait_ge(S["t_ev"], 2 * (n + 2))
            for j in range(8):
                mm = eng.transpose(pT[:, j * P:(j + 1) * P], pr[:, b % 2, j, :], ident)
            mm.then_inc(S["pt_mm"], 1)

        def pe_values(eng, b, n, turned):
            S = LS
            eng.wait_ge(S["pt_ev"], n + 1)
            eng.wait_ge(S["v_ev"], 2 * n + 2)
            if turned:
                eng.wait_ge(S["sub_done"], n + 2)
            need(eng, S["o_done"], n)
            for i in range(H):
                g, j = i // 4, i % 4
                for w in range(2):
                    col0 = g * 512 + j * (DH + 1)
                    mm = eng.matmul(pS[64 * w:64 * w + 64, col0:col0 + DH + 1], prT[:, i, 64 * w:64 * w + 64],
                                    (vown if w else vmix)[b][:, 2 * j + g, :], start=(j == 0), stop=True,
                                    skip_group_check=True)
            mm.then_inc(S["o_mm"], 1)

        def pe_turn_output(eng, n, bank=pM):
            S = LS
            eng.wait_ge(S["o_done"], n + 1)
            need(eng, S["xr_done"], n)
            for j in range(4):
                mm = eng.transpose(bank[:, j * P:(j + 1) * P], o[:, j * P:(j + 1) * P], ident)
            mm.then_inc(S["ot_mm"], 1)

        def pe_wo(eng, l, n, bank=pM):
            eng.wait_ge(LS["ot_ev"], n + 1)
            for j in range(4):
                mm = eng.matmul(bank[:, 0:P], wo[:, l, j, :], oT[:, j, :], start=(j == 0), stop=(j == 3))
            mm.then_inc(LS["wo_mm"], 1)

        def pe_slot(eng, new, old, ff, k):
            S = LS
            block_ffn = ff and ff[0] == 1
            turned = at(new, old, k - 2)
            weighted = at(new, old, k - 3)
            if k == 0 and old and old[0] == 0:
                eng.wait_ge(A["yt"], NG * (4 * old[1] + 3))
            if turned:
                pe_turn(eng, turned[1], turned[2])
            if k == 0 and old and old[0] == 0:
                pe_retention_out(eng, old[1])
            if new:
                l, n = new[0], count(new, k)
                eng.wait_ge(S["h_ready"], 2 * n + 2)
                need(eng, S["v_ev"], 2 * n)
                if k == 1 and old:
                    eng.wait_ge(S["xr_done"], count(old, 0) + 1)
                eng.matmul(pV[:, :], hT[:, k, :], wqkv[:, l, 1024:1536], start=True, stop=True).then_inc(S["v_mm"], 1)
            if k == 1 and block_ffn:
                need(eng, S["mul_done"], 2 * n if new else 0)
                eng.wait_ge(G["xa"], 4 * ff[1] + 4)
                for j in range(2):
                    eng.matmul(pQK[:, j * 512:(j + 1) * 512], aT[:, 4 + j, :], xa[:, :, :], start=True,
                               stop=True).then_inc(G["w1_mm"], 1)
            if turned:
                pe_scores(eng, *turned)
            if weighted:
                pe_turn_weights(eng, weighted[1], weighted[2], turned)
            if k == 0 and ff:
                ct = step_count(ff)
                eng.wait_ge(S["hn_done"], NB * ct + NB)
                for b in range(NB):
                    mm = eng.transpose(pM[:, b * P:(b + 1) * P], hn[:, b, :], ident)
                mm.then_inc(S["hnt_mm"], 1)
            if k > 0 and old:
                if k == 1 and ff:
                    eng.wait_ge(S["x2_done"], step_count(ff) + 1)
                if k == 2 and block_ffn:
                    eng.wait_ge(G["att"], ff[1] + 1)
                if k == 3 and block_ffn:
                    eng.wait_ge(G["osb"], ff[1] + 1)
                pe_turn_output(eng, count(old, k))
            if k == NB - 1 and new and new[0] == 0:
                pe_retention_project(eng, new[1], 0)
            if new:
                need(eng, S["mul_done"], 2 * n)
                if k == 1 and block_ffn:
                    eng.wait_ge(G["silu"], 2 * ff[1] + 2)
                for g in range(2):
                    mm = eng.matmul(pQK[:, g * 512:(g + 1) * 512], hT[:, k, :], wqkv[:, l, g * 512:(g + 1) * 512],
                                    start=True, stop=True)
                mm.then_inc(S["qk_mm"], 1)
            if k == 0:
                if ff:
                    pe_hidden(eng, ff, (0, 1), turned, weighted)
                if old:
                    if new:
                        eng.wait_ge(S["v_ev"], 2 * n + 2)
                    pe_turn_output(eng, count(old, 0), pV)
                if ff:
                    pe_hidden(eng, ff, (2,), turned, weighted)
                    pe_ffn_out(eng, ff, lambda: weighted and pe_values(eng, weighted[1], weighted[2], turned))
            if k > 0 and old:
                pe_wo(eng, old[0], count(old, k))
            if weighted and not (k == 0 and ff):
                pe_values(eng, weighted[1], weighted[2], turned)
            if k == 0 and old:
                pe_wo(eng, old[0], count(old, 0), pV)
            if k == 1 and block_ffn:
                eng.wait_ge(G["silu"], 2 * ff[1] + 2)
                eng.wait_ge(S["x2_done"], NT + ff[1] + 1)
                if old:
                    eng.wait_ge(S["xr_done"], count(old, 1) + 1)
                for j in range(2):
                    mm = eng.matmul(pM[:, :], aT[:, 6 + j, :], afh[:, j, :], start=(j == 0), stop=(j == 1))
                mm.then_inc(G["w2_mm"], 1)
            if k == 2 and block_ffn:
                eng.wait_ge(G["fin"], ff[1] + 1)
                if old:
                    eng.wait_ge(S["xr_done"], count(old, 2) + 1)
                for b in range(NB):
                    mm = eng.transpose(pM[:, b * P:(b + 1) * P], fin[:, b, :], ident)
                mm.then_inc(G["fin_mm"], 1)
            if k == NB - 1 and old and not (new and new[0] == 0):
                pe_ln(eng, old)

        def pe_ln(eng, step):
            S = LS
            eng.wait_ge(S["hs"], 2 * step_count(step) + 2)
            for b in range(NB):
                mm = eng.transpose(pM[:, b * P:(b + 1) * P], hs[:, b, :], ident)
            mm.then_inc(S["ln_mm"], 1)

        def pe_hidden(eng, step, chunks, turned, weighted):
            S, l, ct = LS, step[0], step_count(step)
            for k in chunks:
                lo, m = CHUNKS[k]
                if k == 0:
                    eng.wait_ge(S["hnt_ev"], ct + 1)
                    if weighted:
                        eng.wait_ge(S["pt_ev"], weighted[2] + 1)
                if k == 1 and turned:
                    eng.wait_ge(S["sub_done"], turned[2] + 1)
                if k == 2:
                    eng.wait_ge(S["hf_done"], NC * ct + 1)
                for s in range(2):
                    mm = eng.matmul(ffn_banks[k][0:m, s * 512:(s + 1) * 512], w1[:, l, s * HID + lo:s * HID + lo + m],
                                    hnT[:, :], start=True, stop=True)
                mm.then_inc(S["ag_mm"], 1)

        def pe_ffn_out(eng, step, other):
            S, l, ct = LS, step[0], step_count(step)
            for k, (lo, m) in enumerate(CHUNKS):
                if k == NC - 1:
                    other()
                eng.wait_ge(S["hf_done"], NC * ct + k + 1)
                mm = eng.matmul(pM[:, :], w2[0:m, l, k, :], hf[0:m, k, :], start=(k == 0), stop=(k == NC - 1))
            mm.then_inc(S["w2_mm"], 1)

        def pe_retention_project(eng, t, b):
            n = 4 * t + b
            if b == 0:
                eng.wait_ge(A["xa"], 4 * t + 4)
                eng.wait_ge(LS["v_ev"], 2 * (4 * t + 4))
            need(eng, A["qk"], 2 * n)
            eng.matmul(pV[:, 0:3 * P], xa[:, b, :], aT[:, 0:3, :], start=True, stop=True).then_inc(A["qkv_mm"], 1)

        def pe_retention(eng, t, old):
            eng.wait_ge(LS["pt_ev"], 4 * t + 1)
            if old:
                eng.wait_ge(LS["xr_done"], count(old, NB - 1) + 1)
            for k in range(NB + 1):
                if k < NB:
                    n = 4 * t + k
                    eng.wait_ge(A["qk"], 2 * n + 2)
                    need(eng, A["t_ev"], n)
                    for g in range(2):
                        mm = eng.transpose(pM[:, g * P:(g + 1) * P], aqk[:, k % 2, g, :], ident)
                    mm.then_inc(A["t_mm"], 1)
                if k + 1 < NB:
                    pe_retention_project(eng, t, k + 1)
                if k < NB:
                    eng.wait_ge(A["xa4"], n + 1)
                    need(eng, A["vx"], n)
                    for c_ in range(NBL):
                        mm = eng.matmul(pT[:, c_ * P:(c_ + 1) * P], xa4[:, k % 2, c_, :, :], aT[:, 2, :],
                                        start=True, stop=True)
                    mm.then_inc(A["vx_mm"], 1)
                    if k == 0:
                        eng.wait_ge(LS["o_done"], 4 * t + 1)
                    need(eng, A["kvm"], n)
                    for c_ in range(NBL):
                        rows = slice(0, (c_ + 1) * BL)
                        mm = eng.matmul(pS[:, c_ * P:(c_ + 1) * P], aqk[rows, k % 2, 1, :], av[rows, k % 2, :],
                                        start=True, stop=True)
                    mm.then_inc(A["kv_mm"], 1)
                if k == NB - 1:
                    if old:
                        eng.wait_ge(A["t_ev"], 4 * t + 4)
                        pe_ln(eng, old)
                    pe_block_scores(eng, t, k)
                if k > 0:
                    b = k - 1
                    n = 4 * t + b
                    eng.wait_ge(A["sm"], n + 1)
                    eng.wait_ge(A["before"], n + 1)
                    need(eng, A["yt"], NG * (n - 1))
                    for c_ in range(NBL):
                        cols = slice(512 + c_ * P, 512 + (c_ + 1) * P)
                        eng.matmul(y_banks[b % 2][:, cols], vx[:, b % 2, c_, :], sm[:, b % 2, c_, :, :], start=True, stop=False)
                        mm = eng.matmul(y_banks[b % 2][:, cols], before[:, b % 2, c_ - 1, :] if c_ else state[:, b, :],
                                        qx[:, b % 2, c_, :, :], start=False, stop=True)
                    mm.then_inc(A["y_mm"], 1)
                if k < NB - 1:
                    pe_block_scores(eng, t, k)

        def pe_block_scores(eng, t, b):
            n = 4 * t + b
            if b == 1:
                eng.wait_ge(LS["mul_done"], 8 * t + 8)
            eng.wait_ge(A["kx"], n + 1)
            eng.wait_ge(A["qx"], n + 1)
            if b > 1:
                eng.wait_ge(A["sm"], n)
            for c_ in range(NBL):
                mm = eng.matmul(score_bank(b)[:, c_ * P:(c_ + 1) * P], kx[:, b % 2, c_, :, :], qx[:, b % 2, c_, :, :],
                                start=True, stop=True)
            mm.then_inc(A["st_mm"], 1)

        def pe_retention_out(eng, t):
            eng.wait_ge(A["yt"], NG * (4 * t + 4))
            eng.matmul(pS[:, 0:512], aT[:, 3, :], ayT[:, :], start=True, stop=True).then_inc(A["ow_mm"], 1)

        def pe_group_norm(eng, k):
            eng.wait_ge(gn[k]["dve"], 3)
            eng.matmul((pM, pV)[k][:, 0:2 * NB], group_avg, cst2[:, :, :], start=True, stop=True).then_inc(gn[k]["mm"], 1)

        @block.tensor
        def _(eng):
            eng.wait_ge(cst_ld, 32)
            eng.wait_ge(aw_ld, 16 * 6)
            for g in range(2):
                for j in range(4):
                    mm = eng.transpose(pT[:, g * 512 + j * P:g * 512 + (j + 1) * P], araw[:, 4 * g + j, :], ident)
                mm.then_inc(awt_mm, 1)

            def transpose_normalized(half):
                for u in range(2):
                    t = 2 * half + u
                    eng.wait_ge(xn_done, 4 * t + 4)
                    need(eng, xnt_ev, t - 1)
                    for b in range(NB):
                        mm = eng.transpose(xn_banks[u][:, b * P:(b + 1) * P], xn[:, u, b, :], ident)
                    mm.then_inc(xnt_mm, 1)
            transpose_normalized(0)
            with eng.Fori(1, NT // 2) as half:
                transpose_normalized(half)

            def bias_through_w1():
                eng.wait_ge(w1_ld, 16 * DEPTH)
                eng.wait_ge(col_ld, 16 * (10 + 8))
                for l in range(DEPTH):
                    for s in range(2):
                        for k, (lo, m) in enumerate(CHUNKS):
                            place = (l * 2 + s) * NC + k
                            mm = eng.matmul(pM[0:m, place:place + 1], w1[:, l, s * HID + lo:s * HID + lo + m], c("lb", l),
                                            start=True, stop=True)
                mm.then_inc(be_mm, 1)

            eng.wait_ge(wqkv_ld, 16)
            eng.wait_ge(awt_ev, 2)
            eng.wait_ge(xnt_ev, NT)
            eng.wait_ge(mask_done, 1)
            eng.wait_ge(memset_done, 5 + 4 * NB)

            def body(new, old, ff):
                for k in range(NB):
                    if new and is_start(new) and k == 1:
                        bias_through_w1()
                    if new and is_start(new) and k == 2:
                        eng.wait_ge(be_done, 2)
                        pe_group_norm(eng, 0)
                        eng.wait_ge(w_ld, 16 * (1 + 3 * DEPTH))
                    if is_second_norm(new, k):
                        eng.wait_ge(LS["v_ev"], 2 * count(new, k))
                        pe_group_norm(eng, 1)
                        eng.wait_ge(gn[1]["dve"], 4)
                    pe_slot(eng, new, old, ff, k)
                if new and new[0] == 0:
                    if is_start(new):
                        eng.wait_ge(w1g_done, DEPTH)
                    pe_retention(eng, new[1], old)

            run_bodies(eng, body)


_INS = ["L0_attn_x", "L0_attn_norm_g", "L0_attn_norm_b", "L0_attn_qw", "L0_attn_kw", "L0_attn_vw", "L0_attn_ow",
        "L0_attn_ob", "L0_attn_ffn_norm_g", "L0_attn_ffn_norm_b", "L0_attn_w1", "L0_attn_b1", "L0_attn_w2",
        "L0_attn_b2", "L0_ffn_wqkv", "L0_ffn_q_scale", "L0_ffn_k_scale", "L0_ffn_wo", "L0_ffn_ln_g", "L0_ffn_ln_b",
        "L0_ffn_w1", "L0_ffn_b1", "L0_ffn_w2", "L0_ffn_b2"]


def kernel(**inputs):
    import concourse.bacc as _bacc
    from concourse.bass_utils import run_bass_kernel_spmd as _run

    nc = _bacc.Bacc("TRN2", target_bir_lowering=False, num_devices=1)
    cst, tab, mask = constants()
    arrays = {"k_cst": cst, "k_tab": tab, "k_mask": mask}
    arrays.update({n: np.ascontiguousarray(inputs[n]) for n in _INS})
    aps = {n: nc.dram_tensor("in_" + n, v.shape, mybir.dt.from_np(v.dtype), kind="ExternalInput").ap()
           for n, v in arrays.items()}
    out = nc.dram_tensor("out_0", (NB, T, D), F32, kind="ExternalOutput").ap()
    program(nc, aps, out)
    r = _run(nc, [{"in_" + n: v for n, v in arrays.items()}], core_ids=[0])
    return r.results[0]["out_0"]
```
